# Optimizing a Trainium2 kernel written in Bass

```python
import numpy as np
import jax
import jax.numpy as jnp

def _softmax(x, axis=-1):
    return jax.nn.softmax(x, axis=axis)

def _gelu(x):
    return jax.nn.gelu(x, approximate=True)

def _silu(x):
    return jax.nn.silu(x)

def _sigmoid(x):
    return jax.nn.sigmoid(x)

def _layernorm(x, axis=-1, eps=1e-05):
    m = jnp.mean(x, axis=axis, keepdims=True)
    v = jnp.var(x, axis=axis, keepdims=True)
    return (x - m) / jnp.sqrt(v + eps)

def _scatter_add(tgt, idx, src, axis=0):
    return tgt.at[idx].add(src)

def _segment_sum(src, seg, n):
    return jax.ops.segment_sum(src, seg, n)
kernel_name = 'mk_gnn_ffn_d2_gnn_r32_6003b8'

def setup_inputs(seed: int=0):
    np.random.seed(seed)
    _w = jnp.asarray

    def _rec_inputs():
        import jax
        import jax.numpy as jnp
        _gk = jax.random.key(seed)
        x = -8.776e-05 + 1 * jax.random.normal(jax.random.fold_in(_gk, 1), (3125, 256), jnp.float32)
        _s = jax.random.randint(jax.random.fold_in(_gk, 2), (25000,), 0, 3125, jnp.int32)
        _d = jax.random.randint(jax.random.fold_in(_gk, 3), (25000,), 0, 3125, jnp.int32)
        _loop = jnp.arange(3125, dtype=jnp.int32)
        src = jnp.concatenate([_s, _d, _loop])
        dst = jnp.concatenate([_d, _s, _loop])
        _o = jnp.argsort(dst, stable=True)
        src = src[_o]
        dst = dst[_o]
        edge_type_8 = jax.random.randint(jax.random.fold_in(_gk, 13), (53125,), 0, 8, jnp.int32)
        edge_weight = jax.random.uniform(jax.random.fold_in(_gk, 14), (53125,), jnp.float32, 0.0, 0.999996)
        node_type_4 = jax.random.randint(jax.random.fold_in(_gk, 15), (3125,), 0, 4, jnp.int32)
        return (x, src, dst, edge_type_8, edge_weight, node_type_4)
    x, src, dst, edge_type_8, edge_weight, node_type_4 = _rec_inputs()

    def _L0_gnn_setup():
        import jax, jax.numpy as jnp
        import numpy as np
        N_NODES = 625
        N_EDGES = 10000
        D = 256
        NUM_LAYERS = 5

        def gru_cell(m, h, w_ih, w_hh, b_ih, b_hh):
            gi = m @ w_ih.T + b_ih
            gh = h @ w_hh.T + b_hh
            i_r, i_z, i_n = jnp.split(gi, 3, axis=1)
            h_r, h_z, h_n = jnp.split(gh, 3, axis=1)
            r = jax.nn.sigmoid(i_r + h_r)
            z = jax.nn.sigmoid(i_z + h_z)
            n = jnp.tanh(i_n + r * h_n)
            return (1.0 - z) * n + z * h
        key = jax.random.key(seed)
        ks = jax.random.split(key, 8)
        x = jax.random.normal(ks[0], (N_NODES, D), dtype=jnp.float32)
        src = jax.random.randint(ks[1], (N_EDGES,), 0, N_NODES)
        dst = jax.random.randint(ks[2], (N_EDGES,), 0, N_NODES)
        edge_index = jnp.stack([src, dst]).astype(jnp.int64)
        edge_attr = jax.random.uniform(ks[3], (N_EDGES,), dtype=jnp.float32)
        s = 1.0 / np.sqrt(D)
        weight = jax.random.uniform(ks[4], (NUM_LAYERS, D, D), minval=-s, maxval=s, dtype=jnp.float32)
        w_ih = jax.random.uniform(ks[5], (3 * D, D), minval=-s, maxval=s, dtype=jnp.float32)
        w_hh = jax.random.uniform(ks[6], (3 * D, D), minval=-s, maxval=s, dtype=jnp.float32)
        b = jax.random.uniform(ks[7], (2, 3 * D), minval=-s, maxval=s, dtype=jnp.float32)
        return {'x': x, 'edge_index': edge_index, 'edge_attr': edge_attr, 'weight': weight, 'w_ih': w_ih, 'w_hh': w_hh, 'b_ih': b[0], 'b_hh': b[1]}
    _L0_gnn_all = _L0_gnn_setup()
    _L0_gnn_in = {k: v for k, v in _L0_gnn_all.items() if k in ('weight', 'w_ih', 'w_hh', 'b_ih', 'b_hh')}
    del _L0_gnn_all

    def _L0_ffn_setup():
        import jax, jax.numpy as jnp
        import numpy as np
        E, D, H, TOP_K = (6, 256, 256, 2)
        ROUTER_H = D // 2
        key = jax.random.key(seed)
        ks = jax.random.split(key, 12)
        s = 1.0 / np.sqrt(D)
        sh = 1.0 / np.sqrt(H)
        sr = 1.0 / np.sqrt(ROUTER_H)
        return {'features': jax.random.normal(ks[0], (8, 128, D), dtype=jnp.float32), 'router_w1': jax.random.uniform(ks[1], (D, ROUTER_H), jnp.float32, -s, s), 'router_b1': jnp.zeros((ROUTER_H,), jnp.float32), 'router_w2': jax.random.uniform(ks[2], (ROUTER_H, E), jnp.float32, -sr, sr), 'router_b2': jnp.zeros((E,), jnp.float32), 'expert_w1': jax.random.uniform(ks[3], (E, D, H), jnp.float32, -s, s), 'expert_b1': jnp.zeros((E, H), jnp.float32), 'expert_w2': jax.random.uniform(ks[4], (E, H, H), jnp.float32, -sh, sh), 'expert_b2': jnp.zeros((E, H), jnp.float32), 'expert_w3': jax.random.uniform(ks[5], (E, H, D), jnp.float32, -sh, sh), 'expert_b3': jnp.zeros((E, D), jnp.float32)}
    _L0_ffn_all = _L0_ffn_setup()
    _L0_ffn_in = {k: v for k, v in _L0_ffn_all.items() if k in ('router_w1', 'router_b1', 'router_w2', 'router_b2', 'expert_w1', 'expert_b1', 'expert_w2', 'expert_b2', 'expert_w3', 'expert_b3')}
    del _L0_ffn_all

    def _L1_gnn_setup():
        import jax, jax.numpy as jnp
        import numpy as np
        N_NODES = 625
        N_EDGES = 10000
        IN_DIM = 256
        OUT_DIM = 256
        N_HEADS = 4
        D_K = OUT_DIM // N_HEADS
        N_NTYPES = 4
        N_RELS = 8
        SQRT_DK = float(np.sqrt(D_K))

        def _typed_matmul(x, W, node_type):
            all_t = jnp.einsum('ni,tio->tno', x, W)
            return all_t[node_type, jnp.arange(x.shape[0])]
        key = jax.random.key(seed)
        ks = jax.random.split(key, 12)
        xav = lambda k, shape, fan: jax.random.normal(k, shape, jnp.float32) * (1.0 / np.sqrt(fan))
        return {'h': jax.random.normal(ks[0], (N_NODES, IN_DIM), jnp.float32), 'k_linears': xav(ks[1], (N_NTYPES, IN_DIM, OUT_DIM), IN_DIM), 'q_linears': xav(ks[2], (N_NTYPES, IN_DIM, OUT_DIM), IN_DIM), 'v_linears': xav(ks[3], (N_NTYPES, IN_DIM, OUT_DIM), IN_DIM), 'a_linears': xav(ks[4], (N_NTYPES, OUT_DIM, OUT_DIM), OUT_DIM), 'relation_att': xav(ks[5], (N_RELS, N_HEADS, D_K, D_K), D_K), 'relation_msg': xav(ks[6], (N_RELS, N_HEADS, D_K, D_K), D_K), 'relation_pri': jnp.ones((N_RELS, N_HEADS), jnp.float32), 'skip': jnp.ones((N_NTYPES,), jnp.float32), 'node_type': jax.random.randint(ks[7], (N_NODES,), 0, N_NTYPES), 'etype': jnp.sort(jax.random.randint(ks[8], (N_EDGES,), 0, N_RELS)), 'row_idx': jax.random.randint(ks[9], (N_EDGES,), 0, N_NODES), 'col_idx': jax.random.randint(ks[10], (N_EDGES,), 0, N_NODES)}
    _L1_gnn_all = _L1_gnn_setup()
    _L1_gnn_in = {k: v for k, v in _L1_gnn_all.items() if k in ('k_linears', 'q_linears', 'v_linears', 'a_linears', 'relation_att', 'relation_msg', 'relation_pri', 'skip')}
    del _L1_gnn_all

    def _L1_ffn_setup():
        import math
        import jax, jax.numpy as jnp
        import numpy as np
        CAPACITY_FACTOR = 1.25
        key = jax.random.key(seed)
        ks = jax.random.split(key, 5)
        B, L, D, F, E = (8, 256, 256, 1024, 8)
        h = jax.random.normal(ks[0], (B, L, D), dtype=jnp.float32)
        gate_w = jax.random.normal(ks[1], (D, E), dtype=jnp.float32) * 0.02
        gate_b = jnp.zeros((E,), dtype=jnp.float32)
        w1 = jax.random.normal(ks[2], (E, D, F), dtype=jnp.float32) * (1.0 / math.sqrt(D))
        b1 = jnp.zeros((E, F), dtype=jnp.float32)
        w2 = jax.random.normal(ks[3], (E, F, D), dtype=jnp.float32) * (1.0 / math.sqrt(F))
        b2 = jnp.zeros((E, D), dtype=jnp.float32)
        return {'h': h, 'gate_w': gate_w, 'gate_b': gate_b, 'w1': w1, 'b1': b1, 'w2': w2, 'b2': b2}
    _L1_ffn_all = _L1_ffn_setup()
    _L1_ffn_in = {k: v for k, v in _L1_ffn_all.items() if k in ('gate_w', 'gate_b', 'w1', 'b1', 'w2', 'b2')}
    del _L1_ffn_all
    return {'x': x, 'src': src, 'dst': dst, 'edge_type_8': edge_type_8, 'edge_weight': edge_weight, 'node_type_4': node_type_4, 'L0_gnn_weight': _L0_gnn_in['weight'], 'L0_gnn_w_ih': _L0_gnn_in['w_ih'], 'L0_gnn_w_hh': _L0_gnn_in['w_hh'], 'L0_gnn_b_ih': _L0_gnn_in['b_ih'], 'L0_gnn_b_hh': _L0_gnn_in['b_hh'], 'L0_ffn_router_w1': _L0_ffn_in['router_w1'], 'L0_ffn_router_b1': _L0_ffn_in['router_b1'], 'L0_ffn_router_w2': _L0_ffn_in['router_w2'], 'L0_ffn_router_b2': _L0_ffn_in['router_b2'], 'L0_ffn_expert_w1': _L0_ffn_in['expert_w1'], 'L0_ffn_expert_b1': _L0_ffn_in['expert_b1'], 'L0_ffn_expert_w2': _L0_ffn_in['expert_w2'], 'L0_ffn_expert_b2': _L0_ffn_in['expert_b2'], 'L0_ffn_expert_w3': _L0_ffn_in['expert_w3'], 'L0_ffn_expert_b3': _L0_ffn_in['expert_b3'], 'L1_gnn_k_linears': _L1_gnn_in['k_linears'], 'L1_gnn_q_linears': _L1_gnn_in['q_linears'], 'L1_gnn_v_linears': _L1_gnn_in['v_linears'], 'L1_gnn_a_linears': _L1_gnn_in['a_linears'], 'L1_gnn_relation_att': _L1_gnn_in['relation_att'], 'L1_gnn_relation_msg': _L1_gnn_in['relation_msg'], 'L1_gnn_relation_pri': _L1_gnn_in['relation_pri'], 'L1_gnn_skip': _L1_gnn_in['skip'], 'L1_ffn_gate_w': _L1_ffn_in['gate_w'], 'L1_ffn_gate_b': _L1_ffn_in['gate_b'], 'L1_ffn_w1': _L1_ffn_in['w1'], 'L1_ffn_b1': _L1_ffn_in['b1'], 'L1_ffn_w2': _L1_ffn_in['w2'], 'L1_ffn_b2': _L1_ffn_in['b2']}

def reference(x, src, dst, edge_type_8, edge_weight, node_type_4, L0_gnn_weight, L0_gnn_w_ih, L0_gnn_w_hh, L0_gnn_b_ih, L0_gnn_b_hh, L0_ffn_router_w1, L0_ffn_router_b1, L0_ffn_router_w2, L0_ffn_router_b2, L0_ffn_expert_w1, L0_ffn_expert_b1, L0_ffn_expert_w2, L0_ffn_expert_b2, L0_ffn_expert_w3, L0_ffn_expert_b3, L1_gnn_k_linears, L1_gnn_q_linears, L1_gnn_v_linears, L1_gnn_a_linears, L1_gnn_relation_att, L1_gnn_relation_msg, L1_gnn_relation_pri, L1_gnn_skip, L1_ffn_gate_w, L1_ffn_gate_b, L1_ffn_w1, L1_ffn_b1, L1_ffn_w2, L1_ffn_b2):
    import jax
    import jax.numpy as jnp

    def _L0_gnn_ref(x, edge_index, edge_attr, weight, w_ih, w_hh, b_ih, b_hh):
        import jax, jax.numpy as jnp
        import numpy as np
        N_NODES = 625
        N_EDGES = 10000
        D = 256
        NUM_LAYERS = 5

        def gru_cell(m, h, w_ih, w_hh, b_ih, b_hh):
            gi = m @ w_ih.T + b_ih
            gh = h @ w_hh.T + b_hh
            i_r, i_z, i_n = jnp.split(gi, 3, axis=1)
            h_r, h_z, h_n = jnp.split(gh, 3, axis=1)
            r = jax.nn.sigmoid(i_r + h_r)
            z = jax.nn.sigmoid(i_z + h_z)
            n = jnp.tanh(i_n + r * h_n)
            return (1.0 - z) * n + z * h
        src = edge_index[0]
        dst = edge_index[1]
        n_nodes = x.shape[0]
        h = x
        for i in range(weight.shape[0]):
            m = h @ weight[i]
            msgs = m[src] * edge_attr[:, None]
            agg = jax.ops.segment_sum(msgs, dst, num_segments=n_nodes)
            h = gru_cell(agg, h, w_ih, w_hh, b_ih, b_hh)
        return h

    def _L0_ffn_ref(features, router_w1, router_b1, router_w2, router_b2, expert_w1, expert_b1, expert_w2, expert_b2, expert_w3, expert_b3):
        import jax, jax.numpy as jnp
        import numpy as np
        E, D, H, TOP_K = (6, 256, 256, 2)
        ROUTER_H = D // 2
        rh = jax.nn.relu(features @ router_w1 + router_b1)
        expert_logits = jax.nn.softmax(rh @ router_w2 + router_b2, axis=-1)
        top_w, top_i = jax.lax.top_k(expert_logits, TOP_K)
        routing_weights = jax.nn.softmax(top_w, axis=-1)
        h1 = jax.nn.relu(jnp.einsum('bsd,edh->bseh', features, expert_w1) + expert_b1)
        h2 = jax.nn.relu(jnp.einsum('bseh,ehf->bsef', h1, expert_w2) + expert_b2)
        expert_out = jnp.einsum('bsef,efo->bseo', h2, expert_w3) + expert_b3
        sel = jnp.take_along_axis(expert_out, top_i[:, :, :, None], axis=2)
        combined = jnp.sum(sel * routing_weights[..., None], axis=2)
        return combined

    def _L1_gnn_ref(h, k_linears, q_linears, v_linears, a_linears, relation_att, relation_msg, relation_pri, skip, node_type, etype, row_idx, col_idx):
        import jax, jax.numpy as jnp
        import numpy as np
        N_NODES = 625
        N_EDGES = 10000
        IN_DIM = 256
        OUT_DIM = 256
        N_HEADS = 4
        D_K = OUT_DIM // N_HEADS
        N_NTYPES = 4
        N_RELS = 8
        SQRT_DK = float(np.sqrt(D_K))

        def _typed_matmul(x, W, node_type):
            all_t = jnp.einsum('ni,tio->tno', x, W)
            return all_t[node_type, jnp.arange(x.shape[0])]
        n = h.shape[0]
        k = _typed_matmul(h, k_linears, node_type).reshape(n, N_HEADS, D_K)
        q = _typed_matmul(h, q_linears, node_type).reshape(n, N_HEADS, D_K)
        v = _typed_matmul(h, v_linears, node_type).reshape(n, N_HEADS, D_K)
        q_att = jnp.einsum('nhd,rhde->rnhe', q, relation_att)
        v_msg = jnp.einsum('nhd,rhde->rnhe', v, relation_msg)
        aw_q_edge = q_att[etype, col_idx]
        msg_edge = v_msg[etype, row_idx]
        attn_score = jnp.sum(aw_q_edge * k[row_idx], axis=-1)
        score = attn_score * (relation_pri[etype] / SQRT_DK)
        m = jax.ops.segment_max(score, col_idx, num_segments=n)
        ex = jnp.exp(score - m[col_idx])
        denom = jax.ops.segment_sum(ex, col_idx, num_segments=n)
        alpha = ex / denom[col_idx]
        agg = jax.ops.segment_sum(alpha[..., None] * msg_edge, col_idx, num_segments=n)
        agg = agg.reshape(n, OUT_DIM)
        out = _typed_matmul(agg, a_linears, node_type)
        out = jax.nn.sigmoid(skip)[node_type][:, None] * out
        return out

    def _L1_ffn_ref(h, gate_w, gate_b, w1, b1, w2, b2):
        import math
        import jax, jax.numpy as jnp
        import numpy as np
        CAPACITY_FACTOR = 1.25
        B, L, D = h.shape
        E = gate_w.shape[1]
        T = B * L
        C = max(1, math.ceil(CAPACITY_FACTOR * T / E))
        x = h.reshape(T, D)
        logits = x @ gate_w + gate_b
        probs = jax.nn.softmax(logits, axis=-1)
        idx = jnp.argmax(probs, axis=-1)
        prb = jnp.take_along_axis(probs, idx[:, None], axis=1)[:, 0]
        one_hot = jax.nn.one_hot(idx, E, dtype=jnp.float32)
        pos = (jnp.cumsum(one_hot, axis=0) * one_hot).sum(-1).astype(jnp.int32) - 1
        kept = pos < C
        pos_safe = jnp.where(kept, pos, C)
        buf = jnp.zeros((E, C, D), dtype=h.dtype).at[idx, pos_safe].set(x, mode='drop')
        hmid = jax.nn.relu(jnp.einsum('ecd,edf->ecf', buf, w1) + b1[:, None, :])
        ybuf = jnp.einsum('ecf,efd->ecd', hmid, w2) + b2[:, None, :]
        pos_g = jnp.minimum(pos, C - 1)
        y_tok = ybuf[idx, pos_g] * (prb * kept)[:, None]
        y = y_tok.reshape(B, L, D)
        y = jnp.nan_to_num(y, nan=0.0, posinf=10000.0, neginf=-10000.0)
        return y
    edge_index = jnp.stack([src, dst])
    x = x + _L0_gnn_ref(_layernorm(x, axis=-1), edge_index, edge_weight, L0_gnn_weight, L0_gnn_w_ih, L0_gnn_w_hh, L0_gnn_b_ih, L0_gnn_b_hh)
    x = x + _L0_ffn_ref(_layernorm(x, axis=-1)[None], L0_ffn_router_w1, L0_ffn_router_b1, L0_ffn_router_w2, L0_ffn_router_b2, L0_ffn_expert_w1, L0_ffn_expert_b1, L0_ffn_expert_w2, L0_ffn_expert_b2, L0_ffn_expert_w3, L0_ffn_expert_b3)[0]
    x = x + _L1_gnn_ref(_layernorm(x, axis=-1), L1_gnn_k_linears, L1_gnn_q_linears, L1_gnn_v_linears, L1_gnn_a_linears, L1_gnn_relation_att, L1_gnn_relation_msg, L1_gnn_relation_pri, L1_gnn_skip, node_type_4, edge_type_8, src, dst)
    x = x + _L1_ffn_ref(_layernorm(x, axis=-1)[None], L1_ffn_gate_w, L1_ffn_gate_b, L1_ffn_w1, L1_ffn_b1, L1_ffn_w2, L1_ffn_b2)[0]
    return x

_drawn_inputs = setup_inputs


def setup_inputs(seed=0):
    import zlib

    import numpy as np

    out = dict(_drawn_inputs(seed))
    spreads = {'L0_ffn_router_b1': (0.0, 0.1),
     'L0_ffn_router_b2': (0.0, 0.1),
     'L0_ffn_expert_b1': (0.0, 0.396),
     'L0_ffn_expert_b2': (0.0, 0.1),
     'L0_ffn_expert_b3': (0.0, 0.1),
     'L1_gnn_relation_pri': (1.0, 0.2),
     'L1_gnn_skip': (1.0, 0.6),
     'L1_ffn_gate_b': (0.0, 0.1),
     'L1_ffn_b1': (0.0, 0.668),
     'L1_ffn_b2': (0.0, 0.467)}
    factors = {}
    for name, (base, spread) in spreads.items():
        noise = np.random.default_rng([zlib.crc32(name.encode()), seed]).standard_normal(out[name].shape)
        drawn = base * np.exp(spread * noise) if base else spread * noise
        out[name] = jnp.asarray(drawn.astype(out[name].dtype))
    for name, factor in factors.items():
        out[name] = (out[name] * factor).astype(out[name].dtype)
    return out
```

```python
from contextlib import ExitStack

import concourse.bass as bass
from concourse import mybir

ALU = mybir.AluOpType
ACT = mybir.ActivationFunctionType
AX = mybir.AxisListType
F32 = mybir.dt.float32
I32 = mybir.dt.int32
U32 = mybir.dt.uint32

N, D, E = 3125, 256, 53125
TP, NT, GT = 125, 25, 5
P = 128
FH = D // P
ET = -(-E // P)
EC = -(-ET // P)
NPAD = 3200
RING = 16
EIT = ET // RING
BL = 8
DVE, SP = mybir.EngineType.DVE, mybir.EngineType.SP
HR = RING // 2
PSR = 4
PAD_DST = 4000
WIN_MAX = N - P
LAYERS = 5
GC, NGC = 400, 8
EPS = 1e-5
BIG = 1e38


def wait_own(eng, s, sem, value):
    eng.wait_ge(sem, value)
    eng.sem_inc(s.passed, 1)


def load_bases(nc, eng_type, s, at, count):
    _, values = nc.values_load_multi_w_load_instructions(s.base[0:1, bass.ds(at, count)], engines=(eng_type,), min_val=0, max_val=WIN_MAX,
                                                         skip_runtime_bounds_check_because="phase_edges clips the bases")
    return values


class Shared:
    pass


def open_shared(nc, ctx, a):
    s = Shared()
    s.sb = lambda name, shape, dt=F32: ctx.enter_context(nc.sbuf_tensor(name, shape, dt))
    s.open_sems = []

    def sem(name):
        s.open_sems.append(nc.alloc_semaphore(name=name))
        return s.open_sems[-1]

    s.sem = sem
    s.passed = nc.alloc_semaphore(name="passed")
    s.x = s.sb("x", [TP, NT, D])
    s.ident = s.sb("ident", [P, P])
    s.iota_row = s.sb("iota_row", [P, P])
    s.first_row = s.sb("first_row", [P, P])
    s.dst_by_tile = s.sb("dst_by_tile", [P, EC, P])
    s.src_idx = s.sb("src_idx", [P, EC * P], I32)
    s.rel_idx = s.sb("rel_idx", [P, EC * P], I32)
    s.dst_rel = s.sb("dst_rel", [P, EC * P])
    s.weight = s.sb("weight", [P, EC * P])
    s.base = s.sb("base", [P, EC * P], I32)
    s.stats = s.sb("stats", [TP, NT, 6])
    s.mv = s.sb("mv", [TP, NT, 2])
    s.rstd = s.sb("rstd", [TP, NT])
    s.is_type = s.sb("is_type", [TP, NT, 4])
    s.skip_type = s.sb("skip_type", [TP, NT, 4])
    s.eps = s.sb("eps", [P, 1])
    s.bank = [ctx.enter_context(nc.psum_tensor(f"bank{i}", [P, 512], F32)) for i in range(8)]
    return s


def end_stage(nc, s):
    nc.all_engine_barrier()
    nc.clear_and_free_semaphores(s.open_sems)
    nc.all_engine_barrier()
    s.open_sems = []


def phase_edges(nc, s, a):
    with ExitStack() as ctx:
        def sb(name, shape, dt=F32):
            return ctx.enter_context(nc.sbuf_tensor(name, shape, dt))
        raw_i = sb("raw_i", [P, 3, EC, P], I32)
        raw_f = sb("raw_f", [P, 4, EC, P])
        dst_e = sb("dst_e", [P, EC * P])
        base_f = sb("base_f", [P, EC * P])
        cleared, loaded, converted = s.sem("e_cleared"), s.sem("e_loaded"), s.sem("e_converted")
        made, turned, copied, x_in = s.sem("e_made"), s.sem("e_turned"), s.sem("e_copied"), s.sem("x_in")
        full = ET - 1 - (EC - 1) * P
        rest = E - (ET - 1) * P
        block = ctx.enter_context(nc.Block())

        @block.sync
        def _(sp):
            sp.dma_start(s.x[:, :, :], a["x"].rearrange("(t p) f -> p t f", p=TP)).then_inc(x_in, 16)
            sp.wait_ge(cleared, 4)
            n = 0
            for k, name in enumerate(("src", "dst", "edge_type_8", "edge_weight")):
                to = raw_f[:, 3] if k == 3 else raw_i[:, k]
                for c in range(EC):
                    rows = P if c < EC - 1 else full
                    at = c * P * P
                    sp.dma_start(to[0:rows, c, :], a[name][at:at + rows * P].rearrange("(i p) -> i p", p=P)).then_inc(loaded, 16)
                    n += 16
                sp.dma_start(to[full:full + 1, EC - 1, 0:rest], a[name][(ET - 1) * P:E].rearrange("(i p) -> i p", i=1)).then_inc(loaded, 16)
                n += 16
            sp.wait_ge(loaded, n)
            sp.wait_ge(x_in, 16)

        @block.gpsimd
        def _(pool):
            pool.memset(s.ident[:, :], 0.0).then_inc(made, 1)
            pool.memset(s.first_row[:, :], 0.0).then_inc(made, 1)
            pool.iota(s.iota_row[:, :], pattern=[[1, P]], base=0, channel_multiplier=0,
                      allow_small_or_imprecise_dtypes=True).then_inc(made, 1)
            pool.wait_ge(made, 3)
            pool.affine_select(out=s.ident[:, :], in_=s.ident[:, :], compare_op=ALU.not_equal, fill=1.0, base=0,
                               pattern=[[-1, P]], channel_multiplier=1).then_inc(made, 1)
            pool.affine_select(out=s.first_row[:, :], in_=s.first_row[:, :], compare_op=ALU.not_equal, fill=1.0, base=0,
                               pattern=[[0, P]], channel_multiplier=1).then_inc(made, 1)

        @block.vector
        def _(dve):
            for k, fill in ((0, 0), (1, PAD_DST), (2, 0)):
                dve.memset(raw_i[:, k, EC - 1, :], fill).then_inc(cleared, 1)
            dve.memset(raw_f[:, 3, EC - 1, :], 0.0).then_inc(cleared, 1)
            dve.memset(s.eps[:, :], EPS).then_inc(cleared, 1)
            dve.wait_ge(loaded, 16 * 4 * (EC + 1))
            dve.tensor_copy(raw_f[:, 0], raw_i[:, 0]).then_inc(converted, 1)
            dve.tensor_copy(raw_f[:, 1], raw_i[:, 1]).then_inc(converted, 1)
            dve.tensor_copy(s.dst_by_tile[:, :, :], raw_i[:, 1]).then_inc(converted, 1)
            dve.wait_ge(converted, 1)
            dve.scalar_tensor_tensor(out=raw_f[:, 2], in0=raw_i[:, 2], scalar=float(N), in1=raw_f[:, 0],
                                     op0=ALU.mult, op1=ALU.add).then_inc(converted, 1)
            for k, to in ((0, s.src_idx), (1, dst_e), (2, s.rel_idx), (3, s.weight)):
                dve.wait_ge(turned, k + 1)
                dve.tensor_copy(to[:, :], s.bank[k][:, :]).then_inc(copied, 1)
            dve.wait_ge(turned, 5)
            dve.tensor_scalar(base_f[:, :], s.bank[4][:, :], float(WIN_MAX), None, ALU.min).then_inc(copied, 1)
            dve.wait_ge(copied, 5)
            dve.tensor_copy(s.base[:, :], base_f[:, :]).then_inc(copied, 1)
            dve.tensor_tensor(s.dst_rel[:, :], dst_e[:, :], base_f[:, :], ALU.subtract).then_inc(copied, 1)

        @block.tensor
        def _(pe):
            pe.wait_ge(made, 5)
            pe.wait_ge(converted, 4)
            for k in range(4):
                for c in range(EC):
                    mm = pe.transpose(s.bank[k][:, c * P:(c + 1) * P], raw_f[:, k, c, :], s.ident[:, :])
                mm.then_inc(turned, 1)
            pe.wait_ge(copied, 2)
            pe.matmul(s.bank[4][:, :], s.first_row[:, :], dst_e[:, :], start=True, stop=True).then_inc(turned, 1)


def phase_stats(nc, s, tag):
    with ExitStack() as ctx:
        done, root = s.sem(tag + "_stats"), s.sem(tag + "_root")
        std = ctx.enter_context(nc.sbuf_tensor(tag + "_std", [TP, NT], F32))
        block = ctx.enter_context(nc.Block())

        @block.vector
        def _(dve):
            with dve.Fori(0, NT) as t:
                dve.bn_stats(s.stats[:, bass.ds(t, 1), :], s.x[:, bass.ds(t, 1), :]).then_inc(done, 1)
            dve.wait_ge(done, NT)
            for t in range(NT):
                dve.bn_aggr(s.mv[:, t, :], s.stats[:, t, :]).then_inc(done, 1)
            dve.wait_ge(root, 1)
            dve.reciprocal(s.rstd[:, :], std[:, :]).then_inc(done, 1)

        @block.scalar
        def _(act):
            act.wait_ge(done, 2 * NT)
            act.activation(std[:, :], s.mv[:, :, 1], ACT.Sqrt, bias=s.eps[0:TP, :]).then_inc(root, 1)


def phase_norm_to_T(nc, s, hT, tag):
    with ExitStack() as ctx:
        xn = ctx.enter_context(nc.sbuf_tensor(tag + "_xn", [TP, GT, D], F32))
        clear, normed, turned, copied = s.sem(tag + "_clear"), s.sem(tag + "_normed"), s.sem(tag + "_turned"), s.sem(tag + "_copied")
        block = ctx.enter_context(nc.Block())

        @block.vector
        def _(dve):
            dve.memset(hT[:, :, N:], 0.0).then_inc(clear, 1)
            dve.sem_inc(turned, GT)
            with dve.Fori(0, NT // GT) as c:
                t = c * GT
                for k in range(GT):
                    dve.wait_ge(turned, t + k + 1)
                    dve.tensor_scalar(xn[:, k, :], s.x[:, bass.ds(t + k, 1), :], s.mv[:, bass.ds(t + k, 1), 0],
                                      s.rstd[:, bass.ds(t + k, 1)], ALU.subtract, ALU.mult).then_inc(normed, 1)

        @block.tensor
        def _(pe):
            with pe.Fori(0, NT // GT) as c:
                t = c * GT
                for k in range(GT):
                    pe.wait_ge(normed, t + k + 1)
                    pe.wait_ge(copied, t + k + 1)
                    for f in range(FH):
                        mm = pe.transpose(s.bank[k][:, f * TP:(f + 1) * TP], xn[:, k, f * P:(f + 1) * P], s.ident[0:TP, 0:TP])
                    mm.then_inc(turned, 1)

        @block.scalar
        def _(act):
            act.sem_inc(copied, GT)
            with act.Fori(0, NT // GT) as c:
                t = c * GT
                for k in range(GT):
                    act.wait_ge(turned, t + k + 1 + GT)
                    act.copy(hT[:, :, bass.ds((t + k) * TP, TP)],
                             s.bank[k][:, 0:FH * TP].rearrange("p (f n) -> p f n", f=FH)).then_inc(copied, 1)


def phase_gated_gnn(nc, s, a, m_dram):
    with ExitStack() as ctx:
        def sb(name, shape, dt=F32):
            return ctx.enter_context(nc.sbuf_tensor(name, shape, dt))
        hT = sb("hT", [P, FH, NPAD])
        aggT = sb("aggT", [P, FH, NPAD])
        w_msg = sb("w_msg", [P, LAYERS, FH, D])
        w_ih = sb("w_ih", [P, FH, 3 * D])
        w_hh = sb("w_hh", [P, FH, 3 * D])
        b_ih = sb("b_ih", [P, 6])
        b_hh = sb("b_hh", [P, 6])
        b_sum = sb("b_sum", [P, 6])
        h_tile = sb("h_tile", [P, GT, FH, TP])
        m_out = sb("m_out", [TP, NT, D])
        rows = sb("rows", [P, RING, D])
        idx = sb("idx", [P, RING], I32)
        sel = sb("sel", [P, PSR, P])
        r = sb("r", [P, 2, GC])
        z = sb("z", [P, 2, GC])
        n_ = sb("n_", [P, 2, GC])
        t1 = sb("t1", [P, 2, GC])
        new = sb("new", [P, 2, GC])

        phase_stats(nc, s, "s0")
        phase_norm_to_T(nc, s, hT, "n0")

        w_in, b_ready = s.sem("g_w_in"), s.sem("g_b_ready")
        tile_ready, m_done, m_copied = s.sem("g_tile_ready"), s.sem("g_m_done"), s.sem("g_m_copied")
        m_stored = s.sem("g_m_stored")
        row_in = [s.sem(f"g_row_in{k}") for k in range(RING)]
        idx_ready = s.sem("g_idx_ready")
        sel_ready, mm_done, added = s.sem("g_sel_ready"), s.sem("g_mm_done"), s.sem("g_added")
        gate_mm, gate_act, gate_dve, h_done, cleared = s.sem("g_gate_mm"), s.sem("g_gate_act"), s.sem("g_gate_dve"), s.sem("g_h_done"), s.sem("g_cleared")
        out_turned, out_added = s.sem("g_out_turned"), s.sem("g_out_added")
        block = ctx.enter_context(nc.Block())

        @block.sync
        def _(sp):
            sp.dma_start(w_msg[:, :, :, :], a["L0_gnn_weight"].rearrange("l (f p) n -> p l f n", p=P)).then_inc(w_in, 16)
            sp.dma_start(w_ih[:, :, :], a["w_ihT"].rearrange("(f p) g -> p f g", p=P)).then_inc(w_in, 16)
            sp.dma_start(w_hh[:, :, :], a["w_hhT"].rearrange("(f p) g -> p f g", p=P)).then_inc(w_in, 16)
            sp.dma_start(b_ih[:, :], a["b_ih_cols"]).then_inc(w_in, 16)
            sp.dma_start(b_hh[:, :], a["b_hh_cols"]).then_inc(w_in, 16)
            with sp.Fori(0, LAYERS) as l:
                with sp.Fori(0, NT // GT) as c:
                    for k in range(GT):
                        sp.wait_ge(m_copied, l * NT + c * GT + (k + 2))
                        sp.dma_start(m_dram[bass.ds((c * GT + k) * TP, TP), :], m_out[:, bass.ds(c * GT + k, 1), :].rearrange("p t n -> p (t n)")).then_inc(m_stored, 16)
            sp.wait_ge(m_stored, 16 * NT * LAYERS)

        @block.gpsimd
        def _(pool):
            with pool.Fori(0, LAYERS) as l:
                wait_own(pool, s, m_stored, l * (16 * NT) + 16 * NT)
                with pool.Fori(0, EIT) as j:
                    i = j * RING
                    for k in range(RING):
                        if k % HR == 0:
                            wait_own(pool, s, idx_ready, (l * EIT + j) * 2 + (k // HR + 1))
                        pool.indirect_dma_start(out=rows[:, k, :], out_offset=None, in_=m_dram,
                                                in_offset=bass.IndirectOffsetOnAxis(ap=idx[:, k:k + 1], axis=0)).then_inc(row_in[k], 16)

        @block.scalar
        def _(act):
            def stage(t0, k, left, count):
                act.wait_ge(left, count)
                act.copy(h_tile[:, k], hT[:, :, bass.ds((t0 + k) * TP, TP)]).then_inc(tile_ready, 1)

            act.sem_inc(m_done, GT)
            act.wait_ge(w_in, 16 * 5)
            act.wait_ge(b_ready, 1)
            with act.Fori(0, LAYERS) as l:
                wait_own(act, s, h_done, l * NGC + 1)
                with act.Fori(0, NT // GT) as c:
                    for k in range(GT):
                        stage(c * GT, k, m_done, l * NT + c * GT + k + 1)
                with act.Fori(0, EIT) as j:
                    for half in range(2):
                        wait_own(act, s, mm_done, l * ET + j * RING + (half + 1) * HR)
                        act.copy(idx[:, half * HR:(half + 1) * HR], s.src_idx[:, bass.ds(j * RING + half * HR, HR)]).then_inc(idx_ready, 1)
                with act.Fori(0, NGC) as c:
                    for g in range(FH):
                        b = (l * NGC + c) * FH + g
                        act.wait_ge(gate_mm, b * 4 + 1)
                        act.wait_ge(h_done, l * NGC + c + 1)
                        act.activation(r[:, g], s.bank[4 * g][:, 0:GC], ACT.Sigmoid, bias=b_sum[:, g:g + 1]).then_inc(gate_act, 1)
                        act.wait_ge(gate_mm, b * 4 + 4)
                        act.activation(z[:, g], s.bank[4 * g + 3][:, 0:GC], ACT.Sigmoid, bias=b_sum[:, 2 + g:3 + g]).then_inc(gate_act, 1)
                        act.wait_ge(gate_dve, b * 5 + 2)
                        act.activation(n_[:, g], t1[:, g], ACT.Tanh, bias=b_ih[:, 4 + g:5 + g]).then_inc(gate_act, 1)
            act.wait_ge(h_done, LAYERS * NGC + 1)
            act.wait_ge(m_done, LAYERS * NT + GT)
            act.sem_inc(out_turned, GT)
            with act.Fori(0, NT // GT) as c:
                for k in range(GT):
                    stage(c * GT, k, out_turned, c * GT + k + 1)

        @block.vector
        def _(dve):
            dve.sem_inc(mm_done, RING)
            dve.sem_inc(added, PSR)
            for one in (h_done, m_copied, out_added):
                dve.sem_inc(one, 1)
            pass
            dve.wait_ge(w_in, 16 * 5)
            dve.tensor_tensor(b_sum[:, :], b_ih[:, :], b_hh[:, :], ALU.add).then_inc(b_ready, 1)
            with dve.Fori(0, LAYERS) as l:
                wait_own(dve, s, h_done, l * NGC + 1)
                dve.memset(aggT[:, :, :], 0.0).then_inc(cleared, 1)
                with dve.Fori(0, NT // GT) as c:
                    for k in range(GT):
                        wait_own(dve, s, m_done, l * NT + c * GT + (k + 1 + GT))
                        dve.tensor_copy(m_out[:, bass.ds(c * GT + k, 1), :].rearrange("p t n -> p (t n)"), s.bank[k][0:TP, 0:D]).then_inc(m_copied, 1)

                def select(i, k):
                    dve.tensor_scalar(sel[:, k % PSR, :], s.iota_row[:, :], s.dst_rel[:, bass.ds(i + k, 1)],
                                      s.weight[:, bass.ds(i + k, 1)], ALU.is_equal, ALU.mult).then_inc(sel_ready, 1)

                def add(i, k):
                    win = aggT[:, :, bass.ds(base[k], P)]
                    dve.wait_ge(mm_done, l * ET + i + (k + 1 + RING))
                    dve.wait_ge(added, l * ET + i + (k + PSR))
                    dve.tensor_tensor(win, win, s.bank[k % PSR][:, 0:D].rearrange("p (f n) -> p f n", f=FH), ALU.add).then_inc(added, 1)

                wait_own(dve, s, cleared, l + 1)
                with dve.Fori(0, EIT) as j:
                    i = j * RING
                    base = []
                    for k in range(RING):
                        if k % BL == 0:
                            base += load_bases(nc, DVE, s, i + k, BL)
                        if k == 0:
                            dve.wait_ge(mm_done, l * ET + i + (k + 1 + RING - PSR))
                        select(i, k)
                        if k >= 2:
                            add(i, k - 2)
                    add(i, RING - 2)
                    add(i, RING - 1)
                with dve.Fori(0, NGC) as c:
                    for g in range(FH):
                        b = (l * NGC + c) * FH + g
                        old = hT[:, g, bass.ds(c * GC, GC)]
                        dve.wait_ge(gate_act, b * 3 + 1)
                        dve.wait_ge(gate_mm, b * 4 + 2)
                        dve.scalar_tensor_tensor(out=t1[:, g], in0=s.bank[4 * g + 1][:, 0:GC], scalar=b_hh[:, 4 + g:5 + g], in1=r[:, g],
                                                 op0=ALU.add, op1=ALU.mult).then_inc(gate_dve, 1)
                        dve.wait_ge(gate_dve, b * 5 + 1)
                        dve.wait_ge(gate_mm, b * 4 + 3)
                        dve.tensor_tensor(t1[:, g], t1[:, g], s.bank[4 * g + 2][:, 0:GC], ALU.add).then_inc(gate_dve, 1)
                        dve.wait_ge(gate_act, b * 3 + 3)
                        dve.tensor_tensor(r[:, g], old, n_[:, g], ALU.subtract).then_inc(gate_dve, 1)
                        dve.wait_ge(gate_dve, b * 5 + 3)
                        dve.tensor_tensor(r[:, g], r[:, g], z[:, g], ALU.mult).then_inc(gate_dve, 1)
                        dve.wait_ge(gate_dve, b * 5 + 4)
                        dve.tensor_tensor(new[:, g], r[:, g], n_[:, g], ALU.add).then_inc(gate_dve, 1)
                    wait_own(dve, s, gate_dve, (l * NGC + c) * 10 + 10)
                    dve.tensor_copy(hT[:, :, bass.ds(c * GC, GC)], new[:, :, :]).then_inc(h_done, 1)
            with dve.Fori(0, NT // GT) as c:
                for k in range(GT):
                    dve.wait_ge(out_turned, c * GT + (k + 1 + GT))
                    to = s.x[:, bass.ds(c * GT + k, 1), :].rearrange("p t n -> p (t n)")
                    dve.tensor_tensor(to, to, s.bank[k][0:TP, 0:D], ALU.add).then_inc(out_added, 1)

        @block.tensor
        def _(pe):
            pe.wait_ge(w_in, 16 * 5)
            pe.wait_ge(added, PSR)
            with pe.Fori(0, LAYERS) as l:
                with pe.Fori(0, NT // GT) as c:
                    for k in range(GT):
                        pe.wait_ge(tile_ready, l * NT + c * GT + k + 1)
                        if k == 0:
                            pe.wait_ge(m_copied, l * NT + c * GT + 1)
                        for f in range(FH):
                            mm = pe.matmul(s.bank[k][0:TP, 0:D], h_tile[:, k, f, :], w_msg[:, bass.ds(l, 1), f, :].rearrange("p l n -> p (l n)"),
                                           start=(f == 0), stop=(f == FH - 1))
                        mm.then_inc(m_done, 1)
                wait_own(pe, s, m_copied, l * NT + NT + 1)
                with pe.Fori(0, EIT) as j:
                    for k in range(RING):
                        i = j * RING + k
                        pe.wait_ge(row_in[k], (l * EIT + j + 1) * 16)
                        pe.wait_ge(sel_ready, l * ET + i + 1)
                        pe.wait_ge(added, l * ET + i + 1)
                        for f in range(FH):
                            mm = pe.matmul(s.bank[k % PSR][:, f * P:(f + 1) * P], rows[:, k, f * P:(f + 1) * P], sel[:, k % PSR, :],
                                           start=True, stop=True)
                        mm.then_inc(mm_done, 1)
                wait_own(pe, s, added, l * ET + ET + PSR)
                with pe.Fori(0, NGC) as c:
                    agg = [aggT[:, f, bass.ds(c * GC, GC)] for f in range(FH)]
                    old = [hT[:, f, bass.ds(c * GC, GC)] for f in range(FH)]
                    pe.wait_ge(h_done, l * NGC + c + 1)
                    for g in range(FH):
                        for q, (gate, ins) in enumerate(((0, (agg, old)), (2, (old,)), (2, (agg,)), (1, (agg, old)))):
                            terms = [(v, f) for v in ins for f in range(FH)]
                            for n, (v, f) in enumerate(terms):
                                w = w_ih if v is agg else w_hh
                                at = gate * D + g * P
                                mm = pe.matmul(s.bank[4 * g + q][:, 0:GC], w[:, f, at:at + P], v[f], start=(n == 0), stop=(n == len(terms) - 1))
                            mm.then_inc(gate_mm, 1)
            with pe.Fori(0, NT // GT) as c:
                for k in range(GT):
                    pe.wait_ge(tile_ready, LAYERS * NT + c * GT + k + 1)
                    if k == 0:
                        pe.wait_ge(out_added, c * GT + 1)
                    for f in range(FH):
                        mm = pe.transpose(s.bank[k][0:TP, f * P:(f + 1) * P], h_tile[:, k, f, :], s.ident[:, :])
                    mm.then_inc(out_turned, 1)


def phase_router(nc, s, a, xT, gate):
    EX, EP = 6, 8
    with ExitStack() as ctx:
        def sb(name, shape, dt=F32):
            return ctx.enter_context(nc.sbuf_tensor(name, shape, dt))
        w1, b1, w2, b2 = sb("rw1", [P, FH, P]), sb("rb1", [P, 1]), sb("rw2", [P, EX]), sb("rb2", [TP, EX])
        rh = sb("rh", [P, GT * TP])
        logits, probs, top, top_i, top_f = sb("logits", [TP, NT, EP]), sb("probs", [TP, NT, EP]), sb("top", [TP, NT, EP]), sb("top_i", [TP, NT, EP], U32), sb("top_f", [TP, NT, EP])
        one = [sb(f"r_one{n}", [TP, NT]) for n in range(4)]
        pick = sb("r_pick", [TP, NT, EP])
        w_in, hid, relu, lg, taken, v, e_done = (s.sem("r_" + n) for n in ("w_in", "hid", "relu", "lg", "taken", "v", "exp"))
        block = ctx.enter_context(nc.Block())
        CH = GT * TP
        cuts = ((0, 313), (313, CH - 313))

        @block.sync
        def _(sp):
            sp.dma_start(w1[:, :, :], a["L0_ffn_router_w1"].rearrange("(f p) n -> p f n", p=P)).then_inc(w_in, 16)
            sp.dma_start(b1[:, :], a["router_b1_cols"]).then_inc(w_in, 16)
            sp.dma_start(w2[:, :], a["L0_ffn_router_w2"]).then_inc(w_in, 16)
            sp.dma_start(b2[:, :], a["L0_ffn_router_b2"].rearrange("(o e) -> o e", o=1).broadcast_to([TP, EX])).then_inc(w_in, 16)
            sp.wait_ge(w_in, 64)

        @block.tensor
        def _(pe):
            pe.wait_ge(w_in, 64)
            with pe.Fori(0, NT // GT) as c:
                for h, (at, n) in enumerate(cuts):
                    for f in range(FH):
                        mm = pe.matmul(s.bank[h][:, 0:n], w1[:, f, :], xT[:, f, bass.ds(c * CH + at, n)], start=(f == 0), stop=(f == FH - 1))
                    mm.then_inc(hid, 1)
                for k in range(GT):
                    if k == 0:
                        pe.wait_ge(taken, c * GT + 1)
                        pe.wait_ge(relu, c * 2 + 2)
                    pe.matmul(s.bank[2 + k][0:TP, 0:EX], rh[:, k * TP:(k + 1) * TP], w2[:, :], start=True, stop=True).then_inc(lg, 1)

        @block.scalar
        def _(act):
            act.wait_ge(w_in, 64)
            with act.Fori(0, NT // GT) as c:
                act.wait_ge(taken, c * GT + 1)
                for h, (at, n) in enumerate(cuts):
                    act.wait_ge(hid, c * 2 + h + 1)
                    act.activation(rh[:, at:at + n], s.bank[h][:, 0:n], ACT.Relu, bias=b1[:, :]).then_inc(relu, 1)
            act.wait_ge(v, 5)
            act.activation(logits[:, :, 0:EX], logits[:, :, 0:EX], ACT.Exp).then_inc(e_done, 1)
            act.wait_ge(v, 9 + 2 * NT + 1)
            act.activation(one[1][:, :], one[1][:, :], ACT.Exp).then_inc(e_done, 1)

        @block.vector
        def _(dve):
            n = [0]

            def step(ins):
                n[0] += 1
                ins.then_inc(v, 1)
                dve.wait_ge(v, n[0])
            step(dve.memset(logits[:, :, :], 0.0))
            step(dve.memset(probs[:, :, :], -1.0))
            dve.sem_inc(taken, 1)
            dve.wait_ge(taken, 1)
            dve.wait_ge(w_in, 64)
            with dve.Fori(0, NT // GT) as c:
                for k in range(GT):
                    dve.wait_ge(lg, c * GT + k + 1)
                    dve.tensor_tensor(logits[:, bass.ds(c * GT + k, 1), 0:EX].rearrange("p t e -> p (t e)"), s.bank[2 + k][0:TP, 0:EX], b2[:, :], ALU.add).then_inc(taken, 1)
            dve.wait_ge(taken, NT + 1)
            L = logits[:, :, 0:EX]

            def wide(v2):
                return v2[:, :].rearrange("p (t o) -> p t o", o=1).broadcast_to([TP, NT, EX])
            step(dve.tensor_reduce(one[0][:, :], L, AX.X, ALU.max))
            step(dve.tensor_copy(pick[:, :, 0:EX], wide(one[0])))
            step(dve.tensor_tensor(L, L, pick[:, :, 0:EX], ALU.subtract))
            dve.wait_ge(e_done, 1)
            step(dve.tensor_reduce(one[0][:, :], L, AX.X, ALU.add))
            step(dve.reciprocal(one[2][:, :], one[0][:, :]))
            step(dve.tensor_copy(pick[:, :, 0:EX], wide(one[2])))
            step(dve.tensor_tensor(probs[:, :, 0:EX], L, pick[:, :, 0:EX], ALU.mult))
            for t in range(NT):
                step(dve.max(top[:, t, :], probs[:, t, :]))
                step(dve.max_index(top_i[:, t, :], top[:, t, :], probs[:, t, :]))
            step(dve.tensor_tensor(one[1][:, :], top[:, :, 1], top[:, :, 0], ALU.subtract))
            step(dve.tensor_copy(top_f[:, :, :], top_i[:, :, :]))
            dve.wait_ge(e_done, 2)
            step(dve.tensor_scalar(one[0][:, :], one[1][:, :], 1.0, None, ALU.add))
            step(dve.reciprocal(one[2][:, :], one[0][:, :]))
            step(dve.tensor_tensor(one[3][:, :], one[1][:, :], one[2][:, :], ALU.mult))
            for t in range(NT):
                step(dve.tensor_scalar(gate[:, t, :], s.iota_row[0:TP, 0:EP], top_f[:, t, 0:1], one[2][:, t:t + 1], ALU.is_equal, ALU.mult))
                step(dve.tensor_scalar(pick[:, t, :], s.iota_row[0:TP, 0:EP], top_f[:, t, 1:2], one[3][:, t:t + 1], ALU.is_equal, ALU.mult))
            step(dve.tensor_tensor(gate[:, :, :], gate[:, :, :], pick[:, :, :], ALU.add))


def phase_experts(nc, s, a, xT, gate):
    EX = 6
    CH = GT * TP
    cuts = ((0, 313), (313, CH - 313))
    with ExitStack() as ctx:
        def sb(name, shape, dt=F32):
            return ctx.enter_context(nc.sbuf_tensor(name, shape, dt))
        w = [sb(f"ew{n}", [P, EX, FH, D]) for n in (1, 2, 3)]
        b = [sb(f"eb{n}", [P, EX * FH]) for n in (1, 2)]
        b3 = sb("eb3", [EX, D])
        h1, h2 = sb("eh1", [P, 2, FH, CH]), sb("eh2", [P, 2, FH, CH])
        gT = sb("gT", [8, CH])
        gate_now = sb("gate_now", [TP, GT, 8])
        w_in, mm, ev, om, oa, gt, gc = (s.sem("f_" + n) for n in ("w_in", "mm", "ev", "om", "oa", "gt", "gc"))
        block = ctx.enter_context(nc.Block())
        order = []
        for e in range(EX + 2):
            if e < EX:
                order += [("h", 0, e, m, q) for m in range(FH) for q in range(2)]
            if 1 <= e <= EX:
                order += [("h", 1, e - 1, m, q) for m in range(FH) for q in range(2)]
            if e >= 2:
                order += [("o", e - 2, k) for k in range(GT)]
        order += [("b", k) for k in range(GT)]
        hidden = [g for g in order if g[0] == "h"]
        outs = [g for g in order if g[0] != "h"]
        NH, NO = len(hidden), len(outs)
        HB, OB = 4, 3

        @block.sync
        def _(sp):
            for n in (1, 2, 3):
                for e in range(EX):
                    sp.dma_start(w[n - 1][:, e], a[f"L0_ffn_expert_w{n}"][e].rearrange("(f p) n -> p f n", p=P)).then_inc(w_in, 16)
            for n in (1, 2):
                sp.dma_start(b[n - 1][:, :], a[f"expert_b{n}_cols"]).then_inc(w_in, 16)
            sp.dma_start(b3[:, :], a["L0_ffn_expert_b3"]).then_inc(w_in, 16)
            sp.wait_ge(w_in, 16 * (3 * EX + 3))

        @block.tensor
        def _(pe):
            pe.wait_ge(w_in, 16 * (3 * EX + 3))
            with pe.Fori(0, NT // GT) as c:
                nh = no = 0
                pe.wait_ge(oa, c * NO + 1)
                for k in range(GT):
                    if k == 0:
                        pe.wait_ge(gc, c * (GT + 1) + 1)
                    else:
                        pe.wait_ge(gc, c * (GT + 1) + k + 1)
                    pe.transpose(s.bank[7][0:8, 0:TP], gate_now[:, k, :], s.ident[0:TP, 0:TP]).then_inc(gt, 1)
                for g in order:
                    if g[0] == "h":
                        _, layer, e, m, q = g
                        at, n = cuts[q]
                        if nh >= HB:
                            pe.wait_ge(ev, c * NH + nh - HB + 1)
                        if layer == 1:
                            pe.wait_ge(ev, c * NH + hidden.index(("h", 0, e, FH - 1, 1)) + 1)
                        for f in range(FH):
                            rhs = xT[:, f, bass.ds(c * CH + at, n)] if layer == 0 else h1[:, e % 2, f, at:at + n]
                            i = pe.matmul(s.bank[nh % HB][:, 0:n], w[layer][:, e, f, m * P:(m + 1) * P], rhs, start=(f == 0), stop=(f == FH - 1))
                        i.then_inc(mm, 1)
                        nh += 1
                        continue
                    bank = s.bank[HB + no % OB][0:TP, 0:D]
                    if no >= OB:
                        pe.wait_ge(oa, c * NO + no - OB + 2)
                    if g[0] == "o":
                        _, e, k = g
                        if k == 0:
                            pe.wait_ge(ev, c * NH + hidden.index(("h", 1, e, FH - 1, 1)) + 1)
                        for f in range(FH):
                            i = pe.matmul(bank, h2[:, e % 2, f, k * TP:(k + 1) * TP], w[2][:, e, f, :], start=(f == 0), stop=(f == FH - 1))
                    else:
                        k = g[1]
                        pe.wait_ge(gc, (c + 1) * (GT + 1))
                        i = pe.matmul(bank, gT[0:EX, k * TP:(k + 1) * TP], b3[:, :], start=True, stop=True)
                    i.then_inc(om, 1)
                    no += 1

        @block.scalar
        def _(act):
            act.wait_ge(w_in, 16 * (3 * EX + 3))
            with act.Fori(0, NT // GT) as c:
                for n, (_, layer, e, m, q) in enumerate(hidden):
                    at, size = cuts[q]
                    act.wait_ge(mm, c * NH + n + 1)
                    to = (h1 if layer == 0 else h2)[:, e % 2, m, at:at + size]
                    act.activation(to, s.bank[n % HB][:, 0:size], ACT.Relu, bias=b[layer][:, e * FH + m:e * FH + m + 1]).then_inc(ev, 1)

        @block.vector
        def _(dve):
            dve.sem_inc(oa, 1)
            with dve.Fori(0, NT // GT) as c:
                wait_own(dve, s, oa, c * NO + 1)
                dve.tensor_copy(gate_now[:, :, :], gate[:, bass.ds(c * GT, GT), :]).then_inc(gc, 1)
                for k in range(GT):
                    dve.wait_ge(gt, c * GT + k + 1)
                    dve.tensor_copy(gT[:, k * TP:(k + 1) * TP], s.bank[7][0:8, 0:TP]).then_inc(gc, 1)
                for n, g in enumerate(outs):
                    k = g[-1]
                    to = s.x[:, bass.ds(c * GT + k, 1), :].rearrange("p t n -> p (t n)")
                    bank = s.bank[HB + n % OB][0:TP, 0:D]
                    dve.wait_ge(om, c * NO + n + 1)
                    if n >= GT:
                        dve.wait_ge(oa, c * NO + n - GT + 2)
                    if g[0] == "o":
                        dve.scalar_tensor_tensor(out=to, in0=bank, scalar=gate_now[:, k, g[1]:g[1] + 1], in1=to, op0=ALU.mult, op1=ALU.add).then_inc(oa, 1)
                    else:
                        dve.tensor_tensor(to, to, bank, ALU.add).then_inc(oa, 1)


def phase_ffn0(nc, s, a):
    with ExitStack() as ctx:
        xT = ctx.enter_context(nc.sbuf_tensor("xT0", [P, FH, NPAD], F32))
        gate = ctx.enter_context(nc.sbuf_tensor("gate", [TP, NT, 8], F32))
        phase_stats(nc, s, "s1")
        phase_norm_to_T(nc, s, xT, "n1")
        phase_router(nc, s, a, xT, gate)
        phase_experts(nc, s, a, xT, gate)


RELS, TYPES, HEADS, DK = 8, 4, 4, 64


def phase_types(nc, s, a):
    with ExitStack() as ctx:
        raw = ctx.enter_context(nc.sbuf_tensor("nt_raw", [NT, TP], I32))
        flt = ctx.enter_context(nc.sbuf_tensor("nt_flt", [NT, TP], F32))
        typ = ctx.enter_context(nc.sbuf_tensor("nt_typ", [TP, NT], F32))
        skip = ctx.enter_context(nc.sbuf_tensor("nt_skip", [TP, TYPES], F32))
        loaded, v, p, sg = s.sem("y_loaded"), s.sem("y_v"), s.sem("y_p"), s.sem("y_sg")
        block = ctx.enter_context(nc.Block())

        @block.sync
        def _(sp):
            sp.dma_start(raw[:, :], a["node_type_4"].rearrange("(t p) -> t p", p=TP)).then_inc(loaded, 16)
            sp.dma_start(skip[:, :], a["L1_gnn_skip"].rearrange("(o t) -> o t", o=1).broadcast_to([TP, TYPES])).then_inc(loaded, 16)
            sp.wait_ge(loaded, 32)

        @block.scalar
        def _(act):
            act.wait_ge(loaded, 32)
            act.activation(skip[:, :], skip[:, :], ACT.Sigmoid).then_inc(sg, 1)

        @block.tensor
        def _(pe):
            pe.wait_ge(v, 1)
            pe.transpose(s.bank[0][0:TP, 0:NT], flt[:, :], s.ident[0:NT, 0:NT]).then_inc(p, 1)

        @block.vector
        def _(dve):
            dve.wait_ge(loaded, 32)
            dve.tensor_copy(flt[:, :], raw[:, :]).then_inc(v, 1)
            dve.wait_ge(p, 1)
            dve.tensor_copy(typ[:, :], s.bank[0][0:TP, 0:NT]).then_inc(v, 1)
            dve.wait_ge(v, 2)
            dve.wait_ge(sg, 1)
            for t in range(TYPES):
                dve.tensor_scalar(s.is_type[:, :, t], typ[:, :], float(t), None, ALU.is_equal).then_inc(v, 1)
                dve.tensor_scalar(s.skip_type[:, :, t], typ[:, :], float(t), skip[:, t:t + 1], ALU.is_equal, ALU.mult).then_inc(v, 1)


def phase_tables(nc, s, a, q_dram, k_dram, v_dram):
    W3 = 3 * D
    with ExitStack() as ctx:
        def sb(name, shape, dt=F32):
            return ctx.enter_context(nc.sbuf_tensor(name, shape, dt))
        xT = sb("xT1", [P, FH, N + TP])
        w = sb("wqkv", [P, FH, TYPES, W3])
        rel = sb("rel", [P, 2, FH, RELS, P])
        pri = sb("pri", [P, FH * RELS])
        x_tile = sb("x_tile", [P, 2, FH, TP])
        qkv = sb("qkv", [TP, 2, W3])
        kvT = sb("kvT", [P, 2, 2 * FH, TP])
        tab = sb("tab", [TP, 2, 2, RELS, D])
        phase_stats(nc, s, "s2")
        phase_norm_to_T(nc, s, xT, "n2")
        names = ("w_in", "z", "scaled", "staged", "mm", "summed", "turned", "kv", "tm", "te")
        w_in, z, scaled, staged, mm, summed, turned, kv, tm, te = (s.sem("t_" + n) for n in names)
        q_stored = [s.sem(f"t_q_stored{n}") for n in range(2)]
        t_stored = [s.sem(f"t_t_stored{n}") for n in range(2)]
        block = ctx.enter_context(nc.Block())
        NW = 3 * TYPES + 3 * HEADS
        PAIRS = NT // 2
        k_rows = k_dram.rearrange("(r n) f -> n r f", r=RELS)
        v_rows = v_dram.rearrange("(r n) f -> n r f", r=RELS)

        @block.sync
        def _(sp):
            for n, name in enumerate(("q", "k", "v")):
                for t in range(TYPES):
                    sp.dma_start(w[:, :, t, n * D:(n + 1) * D], a[f"L1_gnn_{name}_linears"][t].rearrange("(f p) n -> p f n", p=P)).then_inc(w_in, 16)
            sp.wait_ge(z, 1)
            for h in range(HEADS):
                at = DK * (h % 2)
                sp.dma_start(rel[at:at + DK, 0, h // 2, :, at:at + DK], a["rel_attT"][:, h].rearrange("r e d -> e r d")).then_inc(w_in, 16)
                sp.dma_start(rel[at:at + DK, 1, h // 2, :, at:at + DK], a["L1_gnn_relation_msg"][:, h].rearrange("r d e -> d r e")).then_inc(w_in, 16)
                sp.dma_start(pri[at:at + DK, (h // 2) * RELS:(h // 2 + 1) * RELS], a["priT"][h:h + 1, :].broadcast_to([DK, RELS])).then_inc(w_in, 16)

            def store(t, k):
                rows = bass.ds(t * TP, TP)
                sp.wait_ge(summed, t * 8 + 12)
                sp.dma_start(q_dram[rows, :], qkv[:, k, 0:D]).then_inc(q_stored[k], 16)
                sp.wait_ge(te, t * 8 + 9)
                sp.dma_start(k_rows[rows], tab[:, k, 0]).then_inc(t_stored[k], 16)
                sp.dma_start(v_rows[rows], tab[:, k, 1]).then_inc(t_stored[k], 16)

            with sp.Fori(0, PAIRS) as j:
                store(j * 2, 0)
                store(j * 2 + 1, 1)
            store(NT - 1, 0)
            sp.wait_ge(q_stored[0], 16 * (PAIRS + 1))
            sp.wait_ge(q_stored[1], 16 * PAIRS)
            sp.wait_ge(t_stored[0], 32 * (PAIRS + 1))
            sp.wait_ge(t_stored[1], 32 * PAIRS)

        @block.scalar
        def _(act):
            def evacuate(t, k, j):
                act.wait_ge(turned, t + 1)
                act.copy(kvT[:, k], s.bank[4][:, 0:4 * TP].rearrange("p (f n) -> p f n", f=4)).then_inc(kv, 1)
                if j is not None:
                    wait_own(act, s, t_stored[k], j * 32)
                for n in range(8):
                    which, f, quad = n // 4, n // 2 % 2, n % 2
                    act.wait_ge(tm, t * 8 + n + 1)
                    act.copy(tab[:, k, which, 4 * quad:4 * quad + 4, f * P:(f + 1) * P],
                             s.bank[5 + n % 3][0:TP, :].rearrange("p (r d) -> p r d", r=4)).then_inc(te, 1)

            act.wait_ge(scaled, 2)
            act.sem_inc(te, 1)
            for k in range(2):
                act.copy(x_tile[:, k], xT[:, :, k * TP:(k + 1) * TP]).then_inc(staged, 1)
            def round_of(j, first):
                for k in range(2):
                    evacuate(j * 2 + k, k, None if first else j)
                    act.wait_ge(mm, j * 8 + (4 * k + 4))
                    act.copy(x_tile[:, k], xT[:, :, bass.ds(j * (2 * TP) + (2 + k) * TP, TP)]).then_inc(staged, 1)

            round_of(0, True)
            with act.Fori(1, PAIRS) as j:
                round_of(j, False)
            evacuate(NT - 1, 0, PAIRS)

        @block.vector
        def _(dve):
            dve.memset(rel[:, :, :, :, :], 0.0).then_inc(z, 1)
            dve.sem_inc(summed, 4)
            dve.wait_ge(w_in, 16 * NW)
            att = rel[:, 0].rearrange("p f r d -> p (f r) d")
            dve.scalar_tensor_tensor(out=att, in0=att, scalar=1.0 / DK ** 0.5,
                                     in1=pri[:, :].rearrange("p (r o) -> p r o", o=1).broadcast_to([P, FH * RELS, P]),
                                     op0=ALU.mult, op1=ALU.mult).then_inc(scaled, 2)

            def accumulate(t, k, j):
                if j is not None:
                    wait_own(dve, s, q_stored[k], j * 16)
                for y in range(TYPES):
                    dve.wait_ge(mm, t * 4 + y + 1)
                    one = s.is_type[:, bass.ds(t, 1), y]
                    for part, (lo, hi) in enumerate(((0, 512), (512, W3))):
                        bank, to = s.bank[2 * (y % 2) + part][0:TP, 0:hi - lo], qkv[:, k, lo:hi]
                        if y == 0:
                            dve.tensor_scalar(to, bank, one, None, ALU.mult).then_inc(summed, 1)
                        else:
                            dve.wait_ge(summed, t * 8 + 2 * y + part - 1 + 4)
                            dve.scalar_tensor_tensor(out=to, in0=bank, scalar=one, in1=to, op0=ALU.mult, op1=ALU.add).then_inc(summed, 1)

            accumulate(0, 0, None)
            accumulate(1, 1, None)
            with dve.Fori(1, PAIRS) as j:
                accumulate(j * 2, 0, j)
                accumulate(j * 2 + 1, 1, j)
            accumulate(NT - 1, 0, PAIRS)

        @block.tensor
        def _(pe):
            def typed(t, k):
                pe.wait_ge(staged, t + 1)
                for y in range(TYPES):
                    pe.wait_ge(summed, t * 8 + 2 * y + 2)
                    for part, (lo, hi) in enumerate(((0, 512), (512, W3))):
                        for f in range(FH):
                            i = pe.matmul(s.bank[2 * (y % 2) + part][0:TP, 0:hi - lo], x_tile[:, k, f, :], w[:, f, y, lo:hi], start=(f == 0), stop=(f == FH - 1))
                    i.then_inc(mm, 1)

            def turn(t, k):
                pe.wait_ge(summed, t * 8 + 12)
                pe.wait_ge(kv, t + 1)
                for n in range(4):
                    i = pe.transpose(s.bank[4][:, n * TP:(n + 1) * TP], qkv[:, k, D + n * P:D + (n + 1) * P], s.ident[0:TP, 0:TP])
                i.then_inc(turned, 1)

            def tables(t, k):
                pe.wait_ge(kv, t + 2)
                for n in range(8):
                    which, f, quad = n // 4, n // 2 % 2, n % 2
                    pe.wait_ge(te, t * 8 + (1 if n < 3 else n - 3 + 2))
                    pe.matmul(s.bank[5 + n % 3][0:TP, :], kvT[:, k, 2 * which + f, :], rel[:, which, f, 4 * quad:4 * quad + 4, :].rearrange("p r d -> p (r d)"),
                              start=True, stop=True).then_inc(tm, 1)

            pe.wait_ge(w_in, 16 * NW)
            pe.wait_ge(scaled, 2)
            typed(0, 0)
            turn(0, 0)
            with pe.Fori(0, PAIRS) as j:
                typed(j * 2 + 1, 1)
                tables(j * 2, 0)
                turn(j * 2 + 1, 1)
                typed(j * 2 + 2, 0)
                tables(j * 2 + 1, 1)
                turn(j * 2 + 2, 0)
            tables(NT - 1, 0)

        @block.gpsimd
        def _(pool):
            pool.sem_inc(kv, 1)


def phase_scores(nc, s, q_dram, k_dram, score):
    QR = 8
    with ExitStack() as ctx:
        def sb(name, shape, dt=F32):
            return ctx.enter_context(nc.sbuf_tensor(name, shape, dt))
        rows = sb("c_rows", [P, RING, D])
        idx = sb("c_idx", [P, RING], I32)
        q_win = sb("q_win", [P, QR, D])
        sel, selT = sb("c_sel", [P, PSR, P]), sb("c_selT", [P, PSR, P])
        prod = sb("c_prod", [P, 2, D])
        names = ("idx_ready", "sel_ready", "turned", "selT_ready", "q_done", "prod_done", "red_done", "up")
        idx_ready, sel_ready, turned, selT_ready, q_done, prod_done, red_done, up = (s.sem("c_" + n) for n in names)
        row_in = [s.sem(f"c_row_in{k}") for k in range(RING)]
        q_in = [s.sem(f"c_q_in{k}") for k in range(QR)]
        block = ctx.enter_context(nc.Block())

        @block.gpsimd
        def _(pool):
            pool.wait_ge(up, 4)
            with pool.Fori(0, EIT) as j:
                for k in range(RING):
                    if k % HR == 0:
                        wait_own(pool, s, idx_ready, j * 2 + (k // HR + 1))
                    pool.indirect_dma_start(out=rows[:, k, :], out_offset=None, in_=k_dram,
                                            in_offset=bass.IndirectOffsetOnAxis(ap=idx[:, k:k + 1], axis=0)).then_inc(row_in[k], 16)

        @block.sync
        def _(sp):
            sp.wait_ge(up, 4)
            with sp.Fori(0, EIT) as j:
                for k in range(RING):
                    if k % BL == 0:
                        base = load_bases(nc, SP, s, j * RING + k, BL)
                    sp.wait_ge(q_done, j * RING + (k + 1))
                    sp.dma_start(q_win[:, k % QR, :], q_dram[bass.ds(base[k % BL], P), :]).then_inc(q_in[k % QR], 16)

        @block.scalar
        def _(act):
            def stage(j, half):
                wait_own(act, s, prod_done, j * RING + (half + 1) * HR)
                act.copy(idx[:, half * HR:(half + 1) * HR], s.rel_idx[:, bass.ds(j * RING + half * HR, HR)]).then_inc(idx_ready, 1)

            def evacuate(i, k):
                act.wait_ge(q_done, i + (QR - PSR + 1) + 0)
                act.wait_ge(turned, i + 1)
                act.copy(selT[:, k % PSR, :], s.bank[k % 2][:, 0:P]).then_inc(selT_ready, 1)

            act.wait_ge(up, 4)
            act.copy(idx[:, 0:HR], s.rel_idx[:, 0:HR]).then_inc(idx_ready, 1)
            act.wait_ge(turned, 1)
            act.copy(selT[:, 0, :], s.bank[0][:, 0:P]).then_inc(selT_ready, 1)
            with act.Fori(0, EIT) as j:
                for k in range(RING):
                    if k == 0:
                        stage(j, 1)
                    if k == HR:
                        stage(j + 1, 0)
                    evacuate(j * RING + (k + 1), k + 1)

        @block.vector
        def _(dve):
            def select(i, k):
                dve.tensor_scalar(sel[:, k % PSR, :], s.iota_row[:, :], s.dst_rel[:, bass.ds(i, 1)], None, ALU.is_equal).then_inc(sel_ready, 1)

            dve.memset(score[:, :, :], 0.0).then_inc(up, 1)
            dve.sem_inc(prod_done, RING)
            dve.sem_inc(q_done, QR)
            dve.sem_inc(up, 3)
            dve.wait_ge(up, 4)
            select(0, 0)
            select(1, 1)
            with dve.Fori(0, EIT) as j:
                for k in range(RING):
                    i = j * RING + k
                    select(i + 2, k + 2)
                    dve.wait_ge(row_in[k], (j + 1) * 16)
                    dve.wait_ge(q_done, i + (1 + QR))
                    dve.tensor_tensor(prod[:, k % 2, :], rows[:, k, :], s.bank[2 + k % PSR][:, 0:D], ALU.mult).then_inc(prod_done, 1)
                    dve.wait_ge(prod_done, i + (1 + RING))
                    dve.tensor_reduce(score[:, :, bass.ds(i, 1)].rearrange("p h o -> p (h o)"), prod[:, k % 2, :].rearrange("p (h d) -> p h d", h=HEADS), AX.X, ALU.add).then_inc(red_done, 1)

        @block.tensor
        def _(pe):
            def turn(i, k):
                pe.wait_ge(sel_ready, i + 1)
                pe.transpose(s.bank[k % 2][:, 0:P], sel[:, k % PSR, :], s.ident[:, :]).then_inc(turned, 1)

            pe.wait_ge(up, 4)
            turn(0, 0)
            with pe.Fori(0, EIT) as j:
                for k in range(RING):
                    i = j * RING + k
                    pe.wait_ge(selT_ready, i + 1)
                    turn(i + 1, k + 1)
                    pe.wait_ge(q_in[k % QR], (j * 2 + (k // QR + 1)) * 16)
                    pe.wait_ge(prod_done, i + (1 + RING - PSR))
                    pe.matmul(s.bank[2 + k % PSR][:, 0:D], selT[:, k % PSR, :], q_win[:, k % QR, :], start=True, stop=True).then_inc(q_done, 1)


def phase_softmax(nc, s, score, alpha):
    TILE = [P, EC, HEADS, P]
    with ExitStack() as ctx:
        def sb(name, shape, dt=F32):
            return ctx.enter_context(nc.sbuf_tensor("m_" + name, shape, dt))
        sc, same_f, same_b, pen_f, pen_b, fwd, bwd, seg, ex = (sb(n, TILE) for n in ("sc", "same_f", "same_b", "pen_f", "pen_b", "fwd", "bwd", "seg", "ex"))
        same, out_first, out_last = (sb(n, [P, EC, P]) for n in ("same", "out_first", "out_last"))
        ends = sb("ends", [P, EC, 4, HEADS])
        whole = sb("whole", [P, EC, HEADS])
        tot = sb("tot", [P, EC, 2, HEADS])
        SEQ = 2 * EC * P
        val, key, t_f, t_b, t_same_f, t_same_b, t_pen_f, t_pen_b = (sb(n, [HEADS, SEQ]) for n in ("val", "key", "t_f", "t_b", "t_same_f", "t_same_b", "t_pen_f", "t_pen_b"))
        v, p, e_done = s.sem("m_v"), s.sem("m_p"), s.sem("m_e")
        block = ctx.enter_context(nc.Block())
        marks = {}

        def flat(t):
            return t[:, :, :, :].rearrange("p c h e -> p (c h e)")

        def seq(t, c):
            return t[:, c * 2 * P:(c + 1) * 2 * P].rearrange("h (i w) -> h w i", w=2)

        @block.vector
        def _(dve):
            n = [0]

            def step(ins):
                n[0] += 1
                ins.then_inc(v, 1)
                dve.wait_ge(v, n[0])

            keys = s.dst_by_tile
            dve.wait_ge(p, 1)
            for h in range(HEADS):
                step(dve.tensor_copy(sc[:, :, h, :], s.bank[h][:, :].rearrange("p (c e) -> p c e", c=EC)))
            step(dve.memset(same[:, :, 0:1], 0.0))
            step(dve.tensor_tensor(same[:, :, 1:P], keys[:, :, 1:P], keys[:, :, 0:P - 1], ALU.is_equal))
            step(dve.memset(flat(same_b), 0.0))
            for h in range(HEADS):
                step(dve.tensor_copy(same_f[:, :, h, :], same[:, :, :]))
                step(dve.tensor_copy(same_b[:, :, h, 0:P - 1], same[:, :, 1:P]))
            step(dve.tensor_scalar(flat(pen_f), flat(same_f), 1.0, BIG, ALU.subtract, ALU.mult))
            step(dve.tensor_scalar(flat(pen_b), flat(same_b), 1.0, BIG, ALU.subtract, ALU.mult))
            for c in range(EC):
                step(dve.tensor_scalar(out_first[:, c, :], keys[:, c, :], keys[:, c, 0:1], 1.0, ALU.is_equal, ALU.subtract))
                step(dve.tensor_scalar(out_last[:, c, :], keys[:, c, :], keys[:, c, P - 1:P], 1.0, ALU.is_equal, ALU.subtract))
                step(dve.tensor_copy(ends[:, c, 2, :], keys[:, c, 0:1].broadcast_to([P, HEADS])))
                step(dve.tensor_copy(ends[:, c, 3, :], keys[:, c, P - 1:P].broadcast_to([P, HEADS])))
            step(dve.tensor_scalar(out_first[:, :, :], out_first[:, :, :], BIG, None, ALU.mult))
            step(dve.tensor_scalar(out_last[:, :, :], out_last[:, :, :], BIG, None, ALU.mult))
            step(dve.tensor_tensor(whole[:, :, :], ends[:, :, 2, :], ends[:, :, 3, :], ALU.not_equal))

            def across(last, scan):
                step(dve.tensor_copy(ends[:, :, 0, :], seg[:, :, :, 0]))
                step(dve.tensor_copy(ends[:, :, 1, :], seg[:, :, :, P - 1]))
                if scan == "add":
                    step(dve.tensor_tensor(ends[:, :, 1, :], ends[:, :, 1, :], whole[:, :, :], ALU.mult))
                marks["ends", scan] = n[0]
                dve.wait_ge(p, last + 1)
                for c in range(EC):
                    b = s.bank[c][0:HEADS, :].rearrange("h (w i) -> h w i", w=4)
                    step(dve.tensor_copy(seq(val, c), b[:, 0:2, :]))
                    if scan == "max":
                        step(dve.tensor_copy(seq(key, c), b[:, 2:4, :]))
                if scan == "max":
                    step(dve.memset(t_same_f[:, 0:1], 0.0))
                    step(dve.memset(t_same_b[:, SEQ - 1:SEQ], 0.0))
                    step(dve.tensor_tensor(t_same_f[:, 1:SEQ], key[:, 1:SEQ], key[:, 0:SEQ - 1], ALU.is_equal))
                    step(dve.tensor_copy(t_same_b[:, 0:SEQ - 1], t_same_f[:, 1:SEQ]))
                    step(dve.tensor_scalar(t_pen_f[:, :], t_same_f[:, :], 1.0, BIG, ALU.subtract, ALU.mult))
                    step(dve.tensor_scalar(t_pen_b[:, :], t_same_b[:, :], 1.0, BIG, ALU.subtract, ALU.mult))
                    both(t_f[:, :], t_b[:, :], val[:, :], t_pen_f[:, :], t_pen_b[:, :], "max")
                    step(dve.tensor_tensor(val[:, :], t_f[:, :], t_b[:, :], ALU.max))
                else:
                    both(t_f[:, :], t_b[:, :], val[:, :], t_same_f[:, :], t_same_b[:, :], "add")
                    step(dve.tensor_tensor(t_f[:, :], t_f[:, :], t_b[:, :], ALU.add))
                    step(dve.tensor_tensor(val[:, :], t_f[:, :], val[:, :], ALU.subtract))
                marks["tot", scan] = n[0]
                dve.wait_ge(p, last + 2)
                step(dve.tensor_copy(tot[:, :, :, :].rearrange("p c w h -> p (c w h)"), s.bank[4][:, 0:EC * 2 * HEADS]))
                for w, outside in enumerate((out_first, out_last)):
                    for c in range(EC):
                        for h in range(HEADS):
                            step(dve.scalar_tensor_tensor(out=seg[:, c, h, :], in0=outside[:, c, :], scalar=tot[:, c, w, h:h + 1], in1=seg[:, c, h, :],
                                                          op0=ALU.add, op1=ALU.max))

            def both(f, b, x, m_f, m_b, scan):
                op0, op1 = (ALU.add, ALU.max) if scan == "max" else (ALU.mult, ALU.add)
                init = -BIG if scan == "max" else 0.0
                step(dve.tensor_tensor_scan(f, m_f, x, init, op0, op1))
                step(dve.tensor_tensor_scan(b[:, ::-1], m_b[:, ::-1], x[:, ::-1], init, op0, op1))

            both(flat(fwd), flat(bwd), flat(sc), flat(pen_f), flat(pen_b), "max")
            step(dve.tensor_tensor(flat(seg), flat(fwd), flat(bwd), ALU.max))
            across(1, "max")
            step(dve.tensor_tensor(flat(sc), flat(sc), flat(seg), ALU.subtract))
            marks["shifted"] = n[0]
            dve.wait_ge(e_done, 1)
            both(flat(fwd), flat(bwd), flat(ex), flat(same_f), flat(same_b), "add")
            step(dve.tensor_tensor(flat(seg), flat(fwd), flat(bwd), ALU.add))
            step(dve.tensor_tensor(flat(seg), flat(seg), flat(ex), ALU.subtract))
            across(3, "add")
            step(dve.reciprocal(flat(fwd), flat(seg)))
            step(dve.tensor_tensor(flat(ex), flat(ex), flat(fwd), ALU.mult))
            marks["alpha"] = n[0]
            dve.wait_ge(p, 6)
            for h in range(HEADS):
                step(dve.tensor_copy(alpha[:, h, :], s.bank[h][:, :]))

        @block.scalar
        def _(act):
            act.wait_ge(v, marks["shifted"])
            act.activation(flat(ex), flat(sc), ACT.Exp).then_inc(e_done, 1)

        @block.tensor
        def _(pe):
            for h in range(HEADS):
                for c in range(EC):
                    i = pe.transpose(s.bank[h][:, c * P:(c + 1) * P], score[:, h, c * P:(c + 1) * P], s.ident[:, :])
            i.then_inc(p, 1)
            for scan in ("max", "add"):
                pe.wait_ge(v, marks["ends", scan])
                for c in range(EC):
                    for w in range(4):
                        i = pe.transpose(s.bank[c][0:HEADS, w * P:(w + 1) * P], ends[:, c, w, :], s.ident[:, :])
                i.then_inc(p, 1)
                pe.wait_ge(v, marks["tot", scan])
                for c in range(EC):
                    for w in range(2):
                        at = (c * 2 + w) * HEADS
                        i = pe.transpose(s.bank[4][:, at:at + HEADS], seq(val, c)[:, w, :], s.ident[0:HEADS, 0:HEADS])
                i.then_inc(p, 1)
            pe.wait_ge(v, marks["alpha"])
            for h in range(HEADS):
                for c in range(EC):
                    i = pe.transpose(s.bank[h][:, c * P:(c + 1) * P], ex[:, c, h, :], s.ident[:, :])
            i.then_inc(p, 1)


def phase_messages(nc, s, v_dram, alpha, aggT):
    with ExitStack() as ctx:
        def sb(name, shape, dt=F32):
            return ctx.enter_context(nc.sbuf_tensor(name, shape, dt))
        rows = sb("d_rows", [P, RING, D])
        idx = sb("d_idx", [P, RING], I32)
        sel = sb("d_sel", [P, PSR, P])
        msg = sb("d_msg", [P, PSR, D])
        idx_ready, msg_ready, mm_done, added, up = (s.sem("d_" + n) for n in ("idx_ready", "msg_ready", "mm_done", "added", "up"))
        row_in = [s.sem(f"d_row_in{k}") for k in range(RING)]
        block = ctx.enter_context(nc.Block())

        @block.gpsimd
        def _(pool):
            pool.wait_ge(up, 1)
            with pool.Fori(0, EIT) as j:
                for k in range(RING):
                    if k % HR == 0:
                        wait_own(pool, s, idx_ready, j * 2 + (k // HR + 1))
                    pool.indirect_dma_start(out=rows[:, k, :], out_offset=None, in_=v_dram,
                                            in_offset=bass.IndirectOffsetOnAxis(ap=idx[:, k:k + 1], axis=0)).then_inc(row_in[k], 16)

        @block.scalar
        def _(act):
            act.wait_ge(up, 1)
            with act.Fori(0, EIT) as j:
                for half in range(2):
                    wait_own(act, s, msg_ready, j * RING + (half + 1) * HR)
                    act.copy(idx[:, half * HR:(half + 1) * HR], s.rel_idx[:, bass.ds(j * RING + half * HR, HR)]).then_inc(idx_ready, 1)

        @block.vector
        def _(dve):
            def weigh(j, k):
                i = j * RING + k
                dve.tensor_scalar(sel[:, k % PSR, :], s.iota_row[:, :], s.dst_rel[:, bass.ds(i, 1)], None, ALU.is_equal).then_inc(up, 1)
                dve.wait_ge(row_in[k], (j + 1) * 16)
                dve.tensor_tensor(msg[:, k % PSR, :].rearrange("p (h d) -> p h d", h=HEADS), rows[:, k, :].rearrange("p (h d) -> p h d", h=HEADS),
                                  alpha[:, :, bass.ds(i, 1)].broadcast_to([P, HEADS, DK]), ALU.mult).then_inc(msg_ready, 1)

            def add(j, k, base):
                i = j * RING + k
                win = aggT[:, :, bass.ds(base[k], P)]
                dve.wait_ge(mm_done, i + 1)
                dve.wait_ge(added, i + PSR)
                dve.tensor_tensor(win, win, s.bank[k % PSR][:, 0:D].rearrange("p (f n) -> p f n", f=FH), ALU.add).then_inc(added, 1)

            dve.memset(aggT[:, :, :], 0.0).then_inc(added, PSR)
            dve.wait_ge(added, PSR)
            dve.sem_inc(msg_ready, RING)
            dve.sem_inc(up, 1)
            with dve.Fori(0, EIT) as j:
                base = []
                for k in range(RING):
                    if k % BL == 0:
                        base += load_bases(nc, DVE, s, j * RING + k, BL)
                    weigh(j, k)
                    if k >= 2:
                        add(j, k - 2, base)
                add(j, RING - 2, base)
                add(j, RING - 1, base)

        @block.tensor
        def _(pe):
            pe.wait_ge(up, 1)
            with pe.Fori(0, EIT) as j:
                for k in range(RING):
                    i = j * RING + k
                    pe.wait_ge(msg_ready, i + (1 + RING))
                    pe.wait_ge(added, i + 1)
                    for f in range(FH):
                        mm = pe.matmul(s.bank[k % PSR][:, f * P:(f + 1) * P], msg[:, k % PSR, f * P:(f + 1) * P], sel[:, k % PSR, :], start=True, stop=True)
                    mm.then_inc(mm_done, 1)


def phase_project(nc, s, a, aggT):
    with ExitStack() as ctx:
        w = ctx.enter_context(nc.sbuf_tensor("wa", [P, FH, TYPES, D], F32))
        tile = ctx.enter_context(nc.sbuf_tensor("a_tile", [P, GT, FH, TP], F32))
        w_in, staged, mm, added = (s.sem("a_" + n) for n in ("w_in", "staged", "mm", "added"))
        block = ctx.enter_context(nc.Block())

        @block.sync
        def _(sp):
            for t in range(TYPES):
                sp.dma_start(w[:, :, t, :], a["L1_gnn_a_linears"][t].rearrange("(f p) n -> p f n", p=P)).then_inc(w_in, 16)
            sp.wait_ge(w_in, 16 * TYPES)

        @block.scalar
        def _(act):
            act.sem_inc(mm, 2 * GT)
            with act.Fori(0, NT // GT) as c:
                for k in range(GT):
                    act.wait_ge(mm, (c * GT + k) * 2 + 2)
                    act.copy(tile[:, k], aggT[:, :, bass.ds((c * GT + k) * TP, TP)]).then_inc(staged, 1)

        @block.tensor
        def _(pe):
            pe.wait_ge(w_in, 16 * TYPES)
            with pe.Fori(0, NT // GT) as c:
                for k in range(GT):
                    pe.wait_ge(staged, c * GT + k + 1)
                    for half in range(2):
                        n = k * 2 + half
                        pe.wait_ge(added, ((c * GT + k) * 2 + half) * 2 + 2)
                        for f in range(FH):
                            i = pe.matmul(s.bank[n % 5][0:TP, :], tile[:, k, f, :], w[:, f, 2 * half:2 * half + 2, :].rearrange("p t n -> p (t n)"), start=(f == 0), stop=(f == FH - 1))
                        i.then_inc(mm, 1)

        @block.vector
        def _(dve):
            dve.sem_inc(added, 10)
            with dve.Fori(0, NT // GT) as c:
                for k in range(GT):
                    to = s.x[:, bass.ds(c * GT + k, 1), :].rearrange("p t n -> p (t n)")
                    for y in range(TYPES):
                        n = k * 2 + y // 2
                        dve.wait_ge(mm, (c * GT + k) * 2 + y // 2 + 1 + 2 * GT)
                        dve.wait_ge(added, (c * GT + k) * 4 + y + 10)
                        dve.scalar_tensor_tensor(out=to, in0=s.bank[n % 5][0:TP, (y % 2) * D:(y % 2 + 1) * D], scalar=s.skip_type[:, bass.ds(c * GT + k, 1), y], in1=to,
                                                 op0=ALU.mult, op1=ALU.add).then_inc(added, 1)


def phase_attention(nc, s, a):
    q_dram = nc.dram_tensor("q_dram", [N, D], F32, kind="Internal").ap()
    k_dram = nc.dram_tensor("k_dram", [RELS * N, D], F32, kind="Internal").ap()
    v_dram = nc.dram_tensor("v_dram", [RELS * N, D], F32, kind="Internal").ap()
    phase_types(nc, s, a)
    phase_tables(nc, s, a, q_dram, k_dram, v_dram)
    with ExitStack() as ctx:
        alpha = ctx.enter_context(nc.sbuf_tensor("alpha", [P, HEADS, EC * P], F32))
        score = ctx.enter_context(nc.sbuf_tensor("score", [P, HEADS, EC * P], F32))
        phase_scores(nc, s, q_dram, k_dram, score)
        phase_softmax(nc, s, score, alpha)
        aggT = ctx.enter_context(nc.sbuf_tensor("aggT1", [P, FH, NPAD], F32))
        phase_messages(nc, s, v_dram, alpha, aggT)
        phase_project(nc, s, a, aggT)


MX, MF = 8, 1024
CAP = 489
BUF = 31 * P
FAR = 100000.0
assert CAP == -(-5 * N // (4 * MX)) and BUF >= MX * CAP


def phase_switch_route(nc, s, a, buf_dram, slot_in, slot_out, keep):
    with ExitStack() as ctx:
        def sb(name, shape, dt=F32):
            return ctx.enter_context(nc.sbuf_tensor("z_" + name, shape, dt))
        xT = sb("xT", [P, FH, NPAD])
        wg, bg = sb("wg", [P, FH, MX]), sb("bg", [TP, MX])
        x_tile = sb("x_tile", [P, GT, FH, TP])
        probs, spread, hot, count, before = (sb(n, [TP, NT, MX]) for n in ("probs", "spread", "hot", "count", "before"))
        top, top_i = sb("top", [TP, NT, 8]), sb("top_i", [TP, NT, 8], U32)
        best, pos, kept, far, red = (sb(n, [TP, NT]) for n in ("best", "pos", "kept", "far", "red"))
        upto, ones = sb("upto", [TP, TP]), sb("ones", [TP, TP])
        zero_row, zero_seq = sb("zero_row", [P, D]), sb("zero_seq", [TP, NT])
        phase_stats(nc, s, "s3")
        phase_norm_to_T(nc, s, xT, "n3")
        w_in, staged, lg, taken, v, e_done, made, p, zeroed, z_up = (s.sem("z_" + n) for n in ("w_in", "staged", "lg", "taken", "v", "e_done", "made", "p", "zeroed", "z_up"))
        marks = {}
        block = ctx.enter_context(nc.Block())

        @block.gpsimd
        def _(pool):
            pool.memset(ones[:, :], 1.0).then_inc(made, 1)
            pool.memset(upto[:, :], 1.0).then_inc(made, 1)
            pool.wait_ge(made, 2)
            pool.affine_select(out=upto[:, :], in_=upto[:, :], compare_op=ALU.is_ge, fill=0.0, base=0, pattern=[[1, TP]], channel_multiplier=-1).then_inc(made, 1)
            pool.memset(zero_row[:, :], 0.0).then_inc(z_up, 1)

        @block.sync
        def _(sp):
            sp.dma_start(wg[:, :, :], a["L1_ffn_gate_w"].rearrange("(f p) n -> p f n", p=P)).then_inc(w_in, 16)
            sp.dma_start(bg[:, :], a["L1_ffn_gate_b"].rearrange("(o e) -> o e", o=1).broadcast_to([TP, MX])).then_inc(w_in, 16)
            sp.wait_ge(z_up, 1)
            sp.dma_start(buf_dram.rearrange("(p r) f -> p r f", p=P), zero_row[:, :].rearrange("p (o f) -> p o f", o=1).broadcast_to([P, BUF // P, D])).then_inc(zeroed, 16)
            sp.wait_ge(w_in, 32)
            sp.wait_ge(zeroed, 16)

        @block.vector
        def _(dve):
            n = [0]

            def step(ins):
                n[0] += 1
                ins.then_inc(v, 1)
                dve.wait_ge(v, n[0])

            def wide(v2):
                return v2[:, :].rearrange("p (t o) -> p t o", o=1).broadcast_to([TP, NT, MX])

            dve.sem_inc(taken, GT)
            step(dve.memset(zero_seq[:, :], 0.0))
            dve.wait_ge(w_in, 32)
            with dve.Fori(0, NT // GT) as c:
                for k in range(GT):
                    dve.wait_ge(lg, c * GT + (k + 1 + GT))
                    dve.tensor_tensor(probs[:, bass.ds(c * GT + k, 1), :].rearrange("p t e -> p (t e)"), s.bank[k][0:TP, 0:MX], bg[:, :], ALU.add).then_inc(taken, 1)
            dve.wait_ge(taken, NT + GT)
            step(dve.tensor_reduce(red[:, :], probs[:, :, :], AX.X, ALU.max))
            step(dve.tensor_copy(spread[:, :, :], wide(red)))
            step(dve.tensor_tensor(probs[:, :, :], probs[:, :, :], spread[:, :, :], ALU.subtract))
            marks["shifted"] = n[0]
            dve.wait_ge(e_done, 1)
            step(dve.tensor_reduce(red[:, :], probs[:, :, :], AX.X, ALU.add))
            step(dve.reciprocal(best[:, :], red[:, :]))
            step(dve.tensor_copy(spread[:, :, :], wide(best)))
            step(dve.tensor_tensor(probs[:, :, :], probs[:, :, :], spread[:, :, :], ALU.mult))
            for t in range(NT):
                step(dve.max(top[:, t, :], probs[:, t, :]))
                step(dve.max_index(top_i[:, t, :], top[:, t, :], probs[:, t, :]))
            step(dve.tensor_copy(best[:, :], top_i[:, :, 0]))
            for t in range(NT):
                step(dve.tensor_scalar(hot[:, t, :], s.iota_row[0:TP, 0:MX], best[:, t:t + 1], None, ALU.is_equal))
            marks["hot"] = n[0]
            dve.wait_ge(p, 1)
            step(dve.tensor_copy(count[:, :, :], s.bank[6][0:TP, 0:NT * MX].rearrange("p (t e) -> p t e", e=MX)))
            for e in range(MX):
                step(dve.tensor_tensor_scan(before[:, :, e], zero_seq[:, :], count[:, :, e], 0.0, ALU.add, ALU.add))
            step(dve.tensor_tensor(before[:, :, :], before[:, :, :], count[:, :, :], ALU.subtract))
            step(dve.tensor_tensor(before[:, :, :], before[:, :, :], s.bank[5][0:TP, 0:NT * MX].rearrange("p (t e) -> p t e", e=MX), ALU.add))
            step(dve.tensor_tensor(before[:, :, :], before[:, :, :], hot[:, :, :], ALU.mult))
            step(dve.tensor_reduce(pos[:, :], before[:, :, :], AX.X, ALU.add))
            step(dve.tensor_scalar(kept[:, :], pos[:, :], float(CAP), None, ALU.is_le))
            step(dve.tensor_tensor(keep[:, :], kept[:, :], top[:, :, 0], ALU.mult))
            step(dve.tensor_scalar(far[:, :], kept[:, :], -FAR, FAR, ALU.mult, ALU.add))
            step(dve.tensor_scalar(red[:, :], pos[:, :], float(CAP), 1.0, ALU.min, ALU.subtract))
            step(dve.scalar_tensor_tensor(out=red[:, :], in0=best[:, :], scalar=float(CAP), in1=red[:, :], op0=ALU.mult, op1=ALU.add))
            step(dve.tensor_copy(slot_out[:, :], red[:, :]))
            step(dve.tensor_tensor(red[:, :], red[:, :], far[:, :], ALU.add))
            step(dve.tensor_copy(slot_in[:, :], red[:, :]))

        @block.scalar
        def _(act):
            act.sem_inc(lg, GT)
            with act.Fori(0, NT // GT) as c:
                for k in range(GT):
                    act.wait_ge(lg, c * GT + k + 1)
                    act.copy(x_tile[:, k], xT[:, :, bass.ds((c * GT + k) * TP, TP)]).then_inc(staged, 1)
            act.wait_ge(v, marks["shifted"])
            act.activation(probs[:, :, :], probs[:, :, :], ACT.Exp).then_inc(e_done, 1)

        @block.tensor
        def _(pe):
            pe.wait_ge(w_in, 32)
            with pe.Fori(0, NT // GT) as c:
                for k in range(GT):
                    pe.wait_ge(staged, c * GT + k + 1)
                    pe.wait_ge(taken, c * GT + k + 1)
                    for f in range(FH):
                        i = pe.matmul(s.bank[k][0:TP, 0:MX], x_tile[:, k, f, :], wg[:, f, :], start=(f == 0), stop=(f == FH - 1))
                    i.then_inc(lg, 1)
            pe.wait_ge(made, 3)
            pe.wait_ge(v, marks["hot"])
            everyone = hot[:, :, :].rearrange("p t e -> p (t e)")
            pe.matmul(s.bank[5][0:TP, 0:NT * MX], upto[:, :], everyone, start=True, stop=True)
            pe.matmul(s.bank[6][0:TP, 0:NT * MX], ones[:, :], everyone, start=True, stop=True).then_inc(p, 1)


def phase_dispatch(nc, s, buf_dram, slot_in):
    with ExitStack() as ctx:
        xn = ctx.enter_context(nc.sbuf_tensor("xn", [TP, NT, D], F32))
        normed, sent = s.sem("i_normed"), s.sem("i_sent")
        block = ctx.enter_context(nc.Block())

        @block.vector
        def _(dve):
            for t in range(NT):
                dve.tensor_scalar(xn[:, t, :], s.x[:, t, :], s.mv[:, t, 0:1], s.rstd[:, t:t + 1], ALU.subtract, ALU.mult).then_inc(normed, 1)

        @block.gpsimd
        def _(pool):
            for t in range(NT):
                pool.wait_ge(normed, t + 1)
                pool.indirect_dma_start(out=buf_dram, out_offset=bass.IndirectOffsetOnAxis(ap=slot_in[:, t:t + 1], axis=0), in_=xn[:, t, :],
                                        in_offset=None, bounds_check=MX * CAP - 1, oob_is_err=False).then_inc(sent, 16)
            pool.wait_ge(sent, 16 * NT)


def phase_switch_experts(nc, s, a, buf_dram, y_dram):
    HM, RT = MF // P, -(-CAP // P)
    WHOLE = CAP // P
    REST = CAP - WHOLE * P
    with ExitStack() as ctx:
        def sb(name, shape, dt=F32):
            return ctx.enter_context(nc.sbuf_tensor("x_" + name, shape, dt))
        w1, w2 = sb("w1", [P, 2, FH, MF]), sb("w2", [P, 2, HM, D])
        b1, b2 = sb("b1", [P, MX * HM]), sb("b2", [P, MX, D])
        rows, rowsT = sb("rows", [P, 2, RT, D]), sb("rowsT", [P, 2, FH, CAP])
        hid, y = sb("hid", [P, 2, HM, CAP]), sb("y", [P, 2, RT, D])
        b_in, turned, te, hm, he, ym, ye = (s.sem("x_" + n) for n in ("b_in", "turned", "te", "hm", "he", "ym", "ye"))
        e_in = [s.sem(f"x_in{k}") for k in range(2)]
        stored = [s.sem(f"x_stored{k}") for k in range(2)]
        block = ctx.enter_context(nc.Block())
        PAIRS = MX // 2

        def size(r):
            return P if r < WHOLE else REST

        @block.sync
        def _(sp):
            def load(e, k):
                one = bass.ds(e, 1)
                sp.dma_start(w1[:, k], a["L1_ffn_w1"][one].rearrange("o (f p) n -> p (o f) n", p=P)).then_inc(e_in[k], 16)
                sp.dma_start(w2[:, k], a["L1_ffn_w2"][one].rearrange("o (j p) n -> p (o j) n", p=P)).then_inc(e_in[k], 16)
                sp.dma_start(rows[:, k, 0:WHOLE, :], buf_dram[bass.ds(e * CAP, WHOLE * P), :].rearrange("(r p) f -> p r f", p=P)).then_inc(e_in[k], 16)
                sp.dma_start(rows[0:REST, k, WHOLE, :], buf_dram[bass.ds(e * CAP + WHOLE * P, REST), :]).then_inc(e_in[k], 16)

            def store(e, k):
                sp.wait_ge(ye, e * RT + (RT + 2))
                sp.dma_start(y_dram[bass.ds(e * CAP, WHOLE * P), :].rearrange("(r p) f -> p r f", p=P), y[:, k, 0:WHOLE, :]).then_inc(stored[k], 16)
                sp.dma_start(y_dram[bass.ds(e * CAP + WHOLE * P, REST), :], y[0:REST, k, WHOLE, :]).then_inc(stored[k], 16)

            load(0, 0)
            load(1, 1)
            sp.dma_start(b1[:, :], a["moe_b1_cols"]).then_inc(b_in, 16)
            sp.dma_start(b2[:, :, :], a["L1_ffn_b2"].rearrange("(o e) n -> o e n", o=1).broadcast_to([P, MX, D])).then_inc(b_in, 16)
            with sp.Fori(0, PAIRS - 1) as j:
                for k in range(2):
                    sp.wait_ge(ym, (j * 2 + k) * RT + RT)
                    load(j * 2 + (k + 2), k)
                    store(j * 2 + k, k)
            store(MX - 2, 0)
            store(MX - 1, 1)
            for k in range(2):
                sp.wait_ge(stored[k], 32 * PAIRS)

        @block.tensor
        def _(pe):
            def hidden(e, k, j):
                wait_own(pe, s, e_in[k], j * 64 + 64)
                for r in range(RT):
                    pe.wait_ge(te, e * RT + r + 1)
                    for f in range(FH):
                        i = pe.transpose(s.bank[6 + r % 2][:, f * P:f * P + size(r)], rows[0:size(r), k, r, f * P:(f + 1) * P], s.ident[0:size(r), 0:size(r)])
                    i.then_inc(turned, 1)
                wait_own(pe, s, te, e * RT + (RT + 2))
                for m in range(HM):
                    pe.wait_ge(he, e * HM + m + 1)
                    for f in range(FH):
                        i = pe.matmul(s.bank[m % 4][:, 0:CAP], w1[:, k, f, m * P:(m + 1) * P], rowsT[:, k, f, :], start=(f == 0), stop=(f == FH - 1))
                    i.then_inc(hm, 1)

            def output(e, k):
                wait_own(pe, s, he, e * HM + (HM + 4))
                for r in range(RT):
                    pe.wait_ge(ye, e * RT + r + 1)
                    for m in range(HM):
                        i = pe.matmul(s.bank[4 + r % 2][0:size(r), 0:D], hid[:, k, m, r * P:r * P + size(r)], w2[:, k, m, :], start=(m == 0), stop=(m == HM - 1))
                    i.then_inc(ym, 1)

            hidden(0, 0, 0)
            with pe.Fori(0, PAIRS - 1) as j:
                hidden(j * 2 + 1, 1, j)
                output(j * 2, 0)
                hidden(j * 2 + 2, 0, j + 1)
                output(j * 2 + 1, 1)
            hidden(MX - 1, 1, PAIRS - 1)
            output(MX - 2, 0)
            output(MX - 1, 1)

        @block.scalar
        def _(act):
            act.sem_inc(te, 2)
            act.sem_inc(he, 4)
            act.wait_ge(b_in, 32)
            with act.Fori(0, PAIRS) as j:
                for k in range(2):
                    e = j * 2 + k
                    for r in range(RT):
                        act.wait_ge(turned, e * RT + r + 1)
                        act.copy(rowsT[:, k, :, r * P:r * P + size(r)], s.bank[6 + r % 2][:, 0:FH * P].rearrange("p (f n) -> p f n", f=FH)[:, :, 0:size(r)]).then_inc(te, 1)
                    for m in range(HM):
                        act.wait_ge(hm, e * HM + m + 1)
                        act.activation(hid[:, k, m, :], s.bank[m % 4][:, 0:CAP], ACT.Relu, bias=b1[:, bass.ds(e * HM + m, 1)]).then_inc(he, 1)

        @block.vector
        def _(dve):
            dve.sem_inc(ye, 2)
            dve.wait_ge(b_in, 32)

            def add_bias(j, first):
                for k in range(2):
                    e = j * 2 + k
                    if not first:
                        wait_own(dve, s, stored[k], j * 32)
                    for r in range(RT):
                        dve.wait_ge(ym, e * RT + r + 1)
                        dve.tensor_tensor(y[0:size(r), k, r, :], s.bank[4 + r % 2][0:size(r), 0:D], b2[0:size(r), bass.ds(e, 1), :].rearrange("p o n -> p (o n)"), ALU.add).then_inc(ye, 1)

            add_bias(0, True)
            with dve.Fori(1, PAIRS) as j:
                add_bias(j, False)


def phase_combine(nc, s, y_dram, slot_out, keep, out):
    with ExitStack() as ctx:
        def sb(name, shape):
            return ctx.enter_context(nc.sbuf_tensor("o_" + name, shape, F32))
        rows = sb("rows", [TP, NT, D])
        number, mask_hi, mask_lo = (sb(n, [TP, GT, D]) for n in ("number", "mask_hi", "mask_lo"))
        hi, lo = sb("hi", [TP, GT, D]), sb("lo", [TP, GT, D])
        row_in = [s.sem(f"o_row_in{c}") for c in range(NT // GT)]
        v, added, stored = s.sem("o_v"), s.sem("o_added"), s.sem("o_stored")
        block = ctx.enter_context(nc.Block())
        out_rows = out.rearrange("(t p) f -> p t f", p=TP)
        FMAX = 3.4028234663852886e38

        @block.gpsimd
        def _(pool):
            for t in range(NT):
                pool.indirect_dma_start(out=rows[:, t, :], out_offset=None, in_=y_dram,
                                        in_offset=bass.IndirectOffsetOnAxis(ap=slot_out[:, t:t + 1], axis=0)).then_inc(row_in[t // GT], 16)

        @block.vector
        def _(dve):
            n = [0]

            def step(ins):
                n[0] += 1
                ins.then_inc(v, 1)
                dve.wait_ge(v, n[0])

            step(dve.memset(hi[:, :, :], 10000.0))
            step(dve.memset(lo[:, :, :], -10000.0))
            for c in range(NT // GT):
                group = slice(c * GT, (c + 1) * GT)
                y = rows[:, group, :]
                dve.wait_ge(row_in[c], 16 * GT)
                for k in range(GT):
                    step(dve.tensor_scalar(rows[:, c * GT + k, :], rows[:, c * GT + k, :], keep[:, c * GT + k:c * GT + k + 1], None, ALU.mult))
                step(dve.tensor_scalar(number[:, :, :], y, 0.0, None, ALU.max))
                step(dve.scalar_tensor_tensor(out=number[:, :, :], in0=y, scalar=0.0, in1=number[:, :, :], op0=ALU.min, op1=ALU.add))
                step(dve.tensor_scalar(mask_hi[:, :, :], number[:, :, :], FMAX, None, ALU.is_gt))
                step(dve.tensor_scalar(mask_lo[:, :, :], number[:, :, :], -FMAX, None, ALU.is_lt))
                step(dve.copy_predicated(number[:, :, :], mask_hi[:, :, :].bitcast(I32), hi[:, :, :]))
                step(dve.copy_predicated(number[:, :, :], mask_lo[:, :, :].bitcast(I32), lo[:, :, :]))
                dve.tensor_tensor(s.x[:, group, :], s.x[:, group, :], number[:, :, :], ALU.add).then_inc(added, 1)

        @block.sync
        def _(sp):
            for c in range(NT // GT):
                sp.wait_ge(added, c + 1)
                sp.dma_start(out_rows[:, c * GT:(c + 1) * GT, :], s.x[:, c * GT:(c + 1) * GT, :]).then_inc(stored, 16)
            sp.wait_ge(stored, 16 * (NT // GT))


def phase_switch(nc, s, a, out):
    buf_dram = nc.dram_tensor("buf_dram", [BUF, D], F32, kind="Internal").ap()
    y_dram = nc.dram_tensor("y_dram", [MX * CAP, D], F32, kind="Internal").ap()
    with ExitStack() as ctx:
        slot_in = ctx.enter_context(nc.sbuf_tensor("slot_in", [TP, NT], I32))
        slot_out = ctx.enter_context(nc.sbuf_tensor("slot_out", [TP, NT], I32))
        keep = ctx.enter_context(nc.sbuf_tensor("keep", [TP, NT], F32))
        phase_switch_route(nc, s, a, buf_dram, slot_in, slot_out, keep)
        phase_dispatch(nc, s, buf_dram, slot_in)
        phase_switch_experts(nc, s, a, buf_dram, y_dram)
        phase_combine(nc, s, y_dram, slot_out, keep, out)


def build(nc, a, out, stop="0123"):
    m_dram = nc.dram_tensor("m_dram", [N, D], F32, kind="Internal").ap()
    with ExitStack() as ctx:
        s = open_shared(nc, ctx, a)
        phase_edges(nc, s, a)
        if "0" in stop:
            phase_gated_gnn(nc, s, a, m_dram)
            end_stage(nc, s)
        if "1" in stop:
            phase_ffn0(nc, s, a)
            end_stage(nc, s)
        if "2" in stop:
            phase_attention(nc, s, a)
            end_stage(nc, s)
        if "3" in stop:
            phase_switch(nc, s, a, out)
            return
        stored = s.sem("stored")
        with nc.Block() as block:
            @block.sync
            def _(sp):
                sp.dma_start(out.rearrange("(t p) f -> p t f", p=TP), s.x[:, :, :]).then_inc(stored, 16)
                sp.wait_ge(stored, 16)


_INS = ["x", "src", "dst", "edge_type_8", "edge_weight", "node_type_4", "L0_gnn_weight", "w_ihT", "w_hhT", "b_ih_cols", "b_hh_cols",
        "L0_ffn_router_w1", "router_b1_cols", "L0_ffn_router_w2", "L0_ffn_router_b2", "L0_ffn_expert_w1", "expert_b1_cols", "L0_ffn_expert_w2",
        "expert_b2_cols", "L0_ffn_expert_w3", "L0_ffn_expert_b3",
        "L1_gnn_k_linears", "L1_gnn_q_linears", "L1_gnn_v_linears", "L1_gnn_a_linears", "rel_attT", "L1_gnn_relation_msg", "priT", "L1_gnn_skip",
        "L1_ffn_gate_w", "L1_ffn_gate_b", "L1_ffn_w1", "moe_b1_cols", "L1_ffn_w2", "L1_ffn_b2"]
_OUTS = [((3125, 256), "float32")]


def kernel(**inputs):
    import numpy as _np
    import concourse.bacc as _bacc
    from concourse import mybir as _mybir
    from concourse.bass_utils import run_bass_kernel_spmd as _run

    inputs["w_ihT"] = _np.asarray(inputs["L0_gnn_w_ih"]).T
    inputs["w_hhT"] = _np.asarray(inputs["L0_gnn_w_hh"]).T
    for name in ("router_b1", "expert_b1", "expert_b2"):
        inputs[f"{name}_cols"] = _np.asarray(inputs[f"L0_ffn_{name}"]).reshape(-1, P).T
    inputs["rel_attT"] = _np.asarray(inputs["L1_gnn_relation_att"]).transpose(0, 1, 3, 2)
    inputs["priT"] = _np.asarray(inputs["L1_gnn_relation_pri"]).T
    inputs["moe_b1_cols"] = _np.asarray(inputs["L1_ffn_b1"]).reshape(-1, P).T
    for side in ("ih", "hh"):
        inputs[f"b_{side}_cols"] = _np.asarray(inputs[f"L0_gnn_b_{side}"]).reshape(-1, P).T
    nc = _bacc.Bacc("TRN2", target_bir_lowering=False, num_devices=1)
    arrays, args = {}, {}
    for name in _INS:
        v = _np.ascontiguousarray(inputs[name])
        arrays[f"in_{name}_dram"] = v
        args[name] = nc.dram_tensor(f"in_{name}_dram", v.shape, _mybir.dt.from_np(v.dtype), kind="ExternalInput").ap()
    out = nc.dram_tensor("out_0_dram", _OUTS[0][0], _mybir.dt.from_np(_np.dtype(_OUTS[0][1])), kind="ExternalOutput").ap()
    build(nc, args, out)
    r = _run(nc, [arrays], core_ids=[0])
    return r.results[0]["out_0_dram"]
```

```python
from contextlib import ExitStack

import concourse.bass as bass
from concourse import mybir

ALU = mybir.AluOpType
ACT = mybir.ActivationFunctionType
AX = mybir.AxisListType
F32 = mybir.dt.float32
I32 = mybir.dt.int32
U32 = mybir.dt.uint32

N, D, E = 3125, 256, 53125
TP, NT, GT = 125, 25, 5
P = 128
FH = D // P
ET = -(-E // P)
EC = -(-ET // P)
NPAD = 3200
RING = 16
EIT = ET // RING
BL = 8
DVE, SP = mybir.EngineType.DVE, mybir.EngineType.SP
HR = RING // 2
PSR = 4
PAD_DST = 4000
WIN_MAX = N - P
LAYERS = 5
NG, GN = NT // GT, GT * TP
CUTS = (-(-GN // 2), GN // 2)
GATES = 6
GHC = -(-N // EIT)
NR = GHC * EIT
EPS = 1e-5
BIG = 1e38


def wait_own(eng, s, sem, value):
    eng.wait_ge(sem, value)
    eng.sem_inc(s.passed, 1)


def load_bases(nc, eng_type, s, at, count):
    _, values = nc.values_load_multi_w_load_instructions(s.base[0:1, bass.ds(at, count)], engines=(eng_type,), min_val=0, max_val=WIN_MAX,
                                                         skip_runtime_bounds_check_because="phase_edges clips the bases")
    return values


class Shared:
    pass


def open_shared(nc, ctx, a):
    s = Shared()
    s.sb = lambda name, shape, dt=F32: ctx.enter_context(nc.sbuf_tensor(name, shape, dt))
    s.open_sems = []

    def sem(name):
        s.open_sems.append(nc.alloc_semaphore(name=name))
        return s.open_sems[-1]

    s.sem = sem
    s.passed = nc.alloc_semaphore(name="passed")
    s.x = s.sb("x", [TP, NT, D])
    s.ident = s.sb("ident", [P, P])
    s.iota_row = s.sb("iota_row", [P, P])
    s.first_row = s.sb("first_row", [P, P])
    s.dst_by_tile = s.sb("dst_by_tile", [P, EC, P])
    s.src_idx = s.sb("src_idx", [P, EC * P], I32)
    s.rel_idx = s.sb("rel_idx", [P, EC * P], I32)
    s.dst_rel = s.sb("dst_rel", [P, EC * P])
    s.weight = s.sb("weight", [P, EC * P])
    s.base = s.sb("base", [P, EC * P], I32)
    s.stats = s.sb("stats", [TP, NT, 6])
    s.mv = s.sb("mv", [TP, NT, 2])
    s.rstd = s.sb("rstd", [TP, NT])
    s.is_type = s.sb("is_type", [TP, NT, 4])
    s.skip_type = s.sb("skip_type", [TP, NT, 4])
    s.eps = s.sb("eps", [P, 1])
    s.zero = s.sb("zero", [P, 1])
    s.bank = [ctx.enter_context(nc.psum_tensor(f"bank{i}", [P, 512], F32)) for i in range(8)]
    return s


def end_stage(nc, s):
    nc.all_engine_barrier()
    nc.clear_and_free_semaphores(s.open_sems)
    nc.all_engine_barrier()
    s.open_sems = []


def phase_edges(nc, s, a):
    with ExitStack() as ctx:
        def sb(name, shape, dt=F32):
            return ctx.enter_context(nc.sbuf_tensor(name, shape, dt))
        raw_i = sb("raw_i", [P, 3, EC, P], I32)
        raw_f = sb("raw_f", [P, 4, EC, P])
        dst_e = sb("dst_e", [P, EC * P])
        base_f = sb("base_f", [P, EC * P])
        cleared, loaded, converted = s.sem("e_cleared"), s.sem("e_loaded"), s.sem("e_converted")
        made, turned, copied, x_in = s.sem("e_made"), s.sem("e_turned"), s.sem("e_copied"), s.sem("x_in")
        full = ET - 1 - (EC - 1) * P
        rest = E - (ET - 1) * P
        block = ctx.enter_context(nc.Block())

        @block.sync
        def _(sp):
            sp.dma_start(s.x[:, :, :], a["x"].rearrange("(t p) f -> p t f", p=TP)).then_inc(x_in, 16)
            sp.wait_ge(cleared, 4)
            n = 0
            for k, name in enumerate(("src", "dst", "edge_type_8", "edge_weight")):
                to = raw_f[:, 3] if k == 3 else raw_i[:, k]
                for c in range(EC):
                    rows = P if c < EC - 1 else full
                    at = c * P * P
                    sp.dma_start(to[0:rows, c, :], a[name][at:at + rows * P].rearrange("(i p) -> i p", p=P)).then_inc(loaded, 16)
                    n += 16
                sp.dma_start(to[full:full + 1, EC - 1, 0:rest], a[name][(ET - 1) * P:E].rearrange("(i p) -> i p", i=1)).then_inc(loaded, 16)
                n += 16
            sp.wait_ge(loaded, n)
            sp.wait_ge(x_in, 16)

        @block.gpsimd
        def _(pool):
            pool.memset(s.ident[:, :], 0.0).then_inc(made, 1)
            pool.memset(s.first_row[:, :], 0.0).then_inc(made, 1)
            pool.iota(s.iota_row[:, :], pattern=[[1, P]], base=0, channel_multiplier=0,
                      allow_small_or_imprecise_dtypes=True).then_inc(made, 1)
            pool.wait_ge(made, 3)
            pool.affine_select(out=s.ident[:, :], in_=s.ident[:, :], compare_op=ALU.not_equal, fill=1.0, base=0,
                               pattern=[[-1, P]], channel_multiplier=1).then_inc(made, 1)
            pool.affine_select(out=s.first_row[:, :], in_=s.first_row[:, :], compare_op=ALU.not_equal, fill=1.0, base=0,
                               pattern=[[0, P]], channel_multiplier=1).then_inc(made, 1)

        @block.vector
        def _(dve):
            for k, fill in ((0, 0), (1, PAD_DST), (2, 0)):
                dve.memset(raw_i[:, k, EC - 1, :], fill).then_inc(cleared, 1)
            dve.memset(raw_f[:, 3, EC - 1, :], 0.0).then_inc(cleared, 1)
            dve.memset(s.eps[:, :], EPS).then_inc(cleared, 1)
            dve.memset(s.zero[:, :], 0.0).then_inc(cleared, 1)
            dve.wait_ge(loaded, 16 * 4 * (EC + 1))
            dve.tensor_copy(raw_f[:, 0], raw_i[:, 0]).then_inc(converted, 1)
            dve.tensor_copy(raw_f[:, 1], raw_i[:, 1]).then_inc(converted, 1)
            dve.tensor_copy(s.dst_by_tile[:, :, :], raw_i[:, 1]).then_inc(converted, 1)
            dve.wait_ge(converted, 1)
            dve.scalar_tensor_tensor(out=raw_f[:, 2], in0=raw_i[:, 2], scalar=float(NR), in1=raw_f[:, 0],
                                     op0=ALU.mult, op1=ALU.add).then_inc(converted, 1)
            for k, to in ((0, s.src_idx), (1, dst_e), (2, s.rel_idx), (3, s.weight)):
                dve.wait_ge(turned, k + 1)
                dve.tensor_copy(to[:, :], s.bank[k][:, :]).then_inc(copied, 1)
            dve.wait_ge(turned, 5)
            dve.tensor_scalar(base_f[:, :], s.bank[4][:, :], float(WIN_MAX), None, ALU.min).then_inc(copied, 1)
            dve.wait_ge(copied, 5)
            dve.tensor_copy(s.base[:, :], base_f[:, :]).then_inc(copied, 1)
            dve.tensor_tensor(s.dst_rel[:, :], dst_e[:, :], base_f[:, :], ALU.subtract).then_inc(copied, 1)

        @block.tensor
        def _(pe):
            pe.wait_ge(made, 5)
            pe.wait_ge(converted, 4)
            for k in range(4):
                for c in range(EC):
                    mm = pe.transpose(s.bank[k][:, c * P:(c + 1) * P], raw_f[:, k, c, :], s.ident[:, :])
                mm.then_inc(turned, 1)
            pe.wait_ge(copied, 2)
            pe.matmul(s.bank[4][:, :], s.first_row[:, :], dst_e[:, :], start=True, stop=True).then_inc(turned, 1)


def phase_norm_to_T(nc, s, hT, tag, load=None):
    with ExitStack() as ctx:
        xn = ctx.enter_context(nc.sbuf_tensor(tag + "_xn", [TP, GT, D], F32))
        std = ctx.enter_context(nc.sbuf_tensor(tag + "_std", [TP, NT], F32))
        done, root = s.sem(tag + "_stats"), s.sem(tag + "_root")
        clear, normed, turned, copied = s.sem(tag + "_clear"), s.sem(tag + "_normed"), s.sem(tag + "_turned"), s.sem(tag + "_copied")
        block = ctx.enter_context(nc.Block())
        if load:
            @block.sync
            def _(sp):
                load(sp)

        @block.vector
        def _(dve):
            dve.memset(hT[:, :, N:], 0.0).then_inc(clear, 1)
            dve.sem_inc(turned, GT)
            with dve.Fori(0, NT // GT) as c:
                for k in range(GT):
                    dve.bn_stats(s.stats[:, bass.ds(c * GT + k, 1), :], s.x[:, bass.ds(c * GT + k, 1), :]).then_inc(done, 1)
            dve.wait_ge(done, NT)
            for t in range(NT):
                dve.bn_aggr(s.mv[:, t, :], s.stats[:, t, :]).then_inc(done, 1)
            dve.wait_ge(root, 1)
            dve.reciprocal(s.rstd[:, :], std[:, :]).then_inc(done, 1)
            dve.wait_ge(done, 2 * NT + 1)
            with dve.Fori(0, NT // GT) as c:
                t = c * GT
                for k in range(GT):
                    dve.wait_ge(turned, t + k + 1)
                    dve.tensor_scalar(xn[:, k, :], s.x[:, bass.ds(t + k, 1), :], s.mv[:, bass.ds(t + k, 1), 0],
                                      s.rstd[:, bass.ds(t + k, 1)], ALU.subtract, ALU.mult).then_inc(normed, 1)

        @block.tensor
        def _(pe):
            with pe.Fori(0, NT // GT) as c:
                t = c * GT
                for k in range(GT):
                    pe.wait_ge(normed, t + k + 1)
                    pe.wait_ge(copied, t + k + 1)
                    for f in range(FH):
                        mm = pe.transpose(s.bank[k][:, f * TP:(f + 1) * TP], xn[:, k, f * P:(f + 1) * P], s.ident[0:TP, 0:TP])
                    mm.then_inc(turned, 1)

        @block.scalar
        def _(act):
            act.sem_inc(copied, GT)
            act.wait_ge(done, 2 * NT)
            act.activation(std[:, :], s.mv[:, :, 1], ACT.Sqrt, bias=s.eps[0:TP, :]).then_inc(root, 1)
            with act.Fori(0, NT // GT) as c:
                t = c * GT
                for k in range(GT):
                    act.wait_ge(turned, t + k + 1 + GT)
                    act.copy(hT[:, :, bass.ds((t + k) * TP, TP)],
                             s.bank[k][:, 0:FH * TP].rearrange("p (f n) -> p f n", f=FH)).then_inc(copied, 1)


def phase_gated_gnn(nc, s, a, m_dram):
    with ExitStack() as ctx:
        def sb(name, shape, dt=F32):
            return ctx.enter_context(nc.sbuf_tensor(name, shape, dt))
        hT = sb("hT", [P, FH, NPAD])
        w_msg = sb("w_msg", [P, FH, D])
        w_ih = sb("w_ih", [P, FH, 3 * D])
        w_hh = sb("w_hh", [P, FH, 3 * D])
        b_ih = sb("b_ih", [P, GATES])
        b_hh = sb("b_hh", [P, GATES])
        b_sum = sb("b_sum", [P, GATES])
        w_in, w_msg_in = s.sem("g_w_in"), s.sem("g_w_msg_in")

        def load(sp):
            sp.dma_start(w_msg[:, :, :], a["L0_gnn_weight"][0].rearrange("(f p) n -> p f n", p=P)).then_inc(w_msg_in, 16)
            sp.dma_start(w_ih[:, :, :], a["w_ihT"].rearrange("(f p) g -> p f g", p=P)).then_inc(w_in, 16)
            sp.dma_start(w_hh[:, :, :], a["w_hhT"].rearrange("(f p) g -> p f g", p=P)).then_inc(w_in, 16)
            sp.dma_start(b_ih[:, :], a["b_ih_cols"]).then_inc(w_in, 16)
            sp.dma_start(b_hh[:, :], a["b_hh_cols"]).then_inc(w_in, 16)

        phase_norm_to_T(nc, s, hT, "n0", load)

        aggT = sb("aggT", [P, FH, NPAD])
        gh = sb("gh", [P, GATES, GHC * EIT])
        h_group = sb("h_group", [P, FH, GN])
        m_out = sb("m_out", [TP, GT, D])
        rows = sb("rows", [P, RING, D])
        idx = sb("idx", [P, RING], I32)
        sel = sb("sel", [P, PSR, P])

        b_ready = s.sem("g_b_ready")
        staged, tile_done, tile_left = s.sem("g_staged"), s.sem("g_tile_done"), s.sem("g_tile_left")
        m_stored, m_out_free = s.sem("g_m_stored"), s.sem("g_m_out_free")
        row_in = [s.sem(f"g_row_in{k}") for k in range(RING)]
        idx_ready = s.sem("g_idx_ready")
        sel_ready, mm_done, added = s.sem("g_sel_ready"), s.sem("g_mm_done"), s.sem("g_added")
        gh_mm, gh_copied = s.sem("g_gh_mm"), s.sem("g_gh_copied")
        gi_done, gate_act, gate_dve, cleared = s.sem("g_gi_done"), s.sem("g_gate_act"), s.sem("g_gate_dve"), s.sem("g_cleared")
        OPS = 14
        m_banks = s.bank[6:8]
        block = ctx.enter_context(nc.Block())

        def cut_columns(c, cut):
            return bass.ds(c * GN + cut * CUTS[0], CUTS[cut])

        @block.sync
        def _(sp):
            def store_group(group, c):
                sp.wait_ge(tile_left, group * GT + (GT + 1))
                sp.dma_start(m_dram[bass.ds(c * GN, GN), :].rearrange("(k p) n -> p k n", p=TP), m_out[:, :, :]).then_inc(m_stored, 16)
                sp.wait_ge(m_stored, group * 16 + 16)
                sp.sem_inc(m_out_free, 1)

            with sp.Fori(0, NG) as c:
                store_group(c, c)
            with sp.Fori(0, LAYERS - 1) as l:
                sp.dma_start(w_msg[:, :, :], a["L0_gnn_weight"][bass.ds(l + 1, 1)].rearrange("l (f p) n -> p (l f) n", p=P)).then_inc(w_msg_in, 16)
                with sp.Fori(0, NG) as c:
                    store_group(l * NG + c + NG, c)

        @block.gpsimd
        def _(pool):
            with pool.Fori(0, LAYERS) as l:
                wait_own(pool, s, m_stored, l * (16 * NG) + 16 * NG)
                with pool.Fori(0, EIT) as j:
                    for k in range(RING):
                        if k % HR == 0:
                            wait_own(pool, s, idx_ready, (l * EIT + j) * 2 + (k // HR + 1))
                        pool.indirect_dma_start(out=rows[:, k, :], out_offset=None, in_=m_dram,
                                                in_offset=bass.IndirectOffsetOnAxis(ap=idx[:, k:k + 1], axis=0)).then_inc(row_in[k], 16)

        @block.scalar
        def _(act):
            def stage_group(group, c):
                act.wait_ge(tile_done, group * GT + GT)
                act.copy(h_group[:, :, :], hT[:, :, bass.ds(c * GN, GN)]).then_inc(staged, 1)

            def copy_m(group):
                wait_own(act, s, m_out_free, group + 1)
                for k in range(GT):
                    act.wait_ge(tile_done, group * GT + (k + 1 + GT))
                    act.copy(m_out[:, k, :], m_banks[k % 2][0:TP, 0:D]).then_inc(tile_left, 1)

            def gather(l):
                with act.Fori(0, EIT) as j:
                    for half in range(2):
                        wait_own(act, s, mm_done, l * ET + j * RING + (half + 1) * HR)
                        act.copy(idx[:, half * HR:(half + 1) * HR], s.src_idx[:, bass.ds(j * RING + half * HR, HR)]).then_inc(idx_ready, 1)
                    for half in range(2):
                        wait_own(act, s, gh_mm, (l * EIT + j) * 2 + (half + 1))
                        act.copy(gh[:, 3 * half:3 * half + 3, bass.ds(j * GHC, GHC)],
                                 s.bank[4 + half][:, 0:3 * GHC].rearrange("p (q n) -> p q n", q=3)).then_inc(gh_copied, 1)

            def gates(l, c, cut, between=None):
                q = l * (2 * NG) + c * 2 + cut
                for part in range(GATES):
                    if part == 4 and between:
                        between()
                    wait_own(act, s, gate_dve, q * OPS + (OPS + (part + 1 if part < 4 else part + 3)))
                    at = gh[:, part, cut_columns(c, cut)]
                    act.activation(at, at, ACT.Sigmoid if part < 4 else ACT.Tanh,
                                   bias=(b_sum if part < 4 else b_ih)[:, part:part + 1]).then_inc(gate_act, 1)

            def lagging(l, c, last):
                gates(l, c + 1, 0, between=lambda: stage_group(l * NG + c + NG, c))
                if not last:
                    copy_m(l * NG + c + NG)
                gates(l, c + 1, 1)

            def layer(l, last):
                gather(l)
                gates(l, 0, 0)
                gates(l, 0, 1)
                with act.Fori(0, NG - 1) as c:
                    lagging(l, c, last)
                act.wait_ge(gate_dve, (l + 1) * (2 * NG * OPS) + OPS)
                stage_group(l * NG + (2 * NG - 1), NG - 1)
                if not last:
                    copy_m(l * NG + (2 * NG - 1))

            act.sem_inc(tile_done, GT)
            act.sem_inc(m_out_free, 1)
            act.wait_ge(w_in, 16 * 4)
            act.wait_ge(b_ready, 1)
            with act.Fori(0, NG) as c:
                stage_group(c, c)
                copy_m(c)
            with act.Fori(0, LAYERS - 1) as l:
                layer(l, False)
            layer(LAYERS - 1, True)

        @block.vector
        def _(dve):
            def select(i, k):
                dve.tensor_scalar(sel[:, k % PSR, :], s.iota_row[:, :], s.dst_rel[:, bass.ds(i + k, 1)],
                                  s.weight[:, bass.ds(i + k, 1)], ALU.is_equal, ALU.mult).then_inc(sel_ready, 1)

            def add(l, i, k, base):
                win = aggT[:, :, bass.ds(base[k], P)]
                dve.wait_ge(mm_done, l * ET + i + (k + 1 + RING))
                dve.wait_ge(added, l * ET + i + (k + PSR))
                dve.tensor_tensor(win, win, s.bank[k % PSR][:, 0:D].rearrange("p (f n) -> p f n", f=FH), ALU.add).then_inc(added, 1)

            def gather(l):
                wait_own(dve, s, cleared, l * (2 * NG) + 1)
                with dve.Fori(0, EIT) as j:
                    i = j * RING
                    base = []
                    for k in range(RING):
                        if k % BL == 0:
                            base += load_bases(nc, DVE, s, i + k, BL)
                        if k == 0:
                            dve.wait_ge(mm_done, l * ET + i + (k + 1 + RING - PSR))
                        select(i, k)
                        if k >= 2:
                            add(l, i, k - 2, base)
                    add(l, i, RING - 2, base)
                    add(l, i, RING - 1, base)

            def gru(l, c, cut):
                q = l * (2 * NG) + c * 2 + cut
                w = CUTS[cut]
                part = [gh[:, p, cut_columns(c, cut)] for p in range(GATES)]
                old = [hT[:, g, cut_columns(c, cut)] for g in range(FH)]
                for p in range(4):
                    dve.wait_ge(gi_done, q * GATES + (p + 1))
                    dve.tensor_tensor(part[p], part[p], s.bank[p][:, 0:w], ALU.add).then_inc(gate_dve, 1)
                for g in range(FH):
                    dve.wait_ge(gate_act, q * GATES + (g + 1))
                    dve.scalar_tensor_tensor(out=part[4 + g], in0=part[4 + g], scalar=b_hh[:, 4 + g:5 + g], in1=part[g],
                                             op0=ALU.add, op1=ALU.mult).then_inc(gate_dve, 1)
                for g in range(FH):
                    dve.wait_ge(gi_done, q * GATES + (g + 5))
                    dve.wait_ge(gate_dve, q * OPS + (OPS + 5 + g))
                    dve.tensor_tensor(part[4 + g], part[4 + g], s.bank[4 + g][:, 0:w], ALU.add).then_inc(gate_dve, 1)
                for g in range(FH):
                    dve.wait_ge(gate_act, q * GATES + (g + 5))
                    dve.tensor_tensor(part[g], old[g], part[4 + g], ALU.subtract).then_inc(gate_dve, 1)
                for g in range(FH):
                    dve.wait_ge(gate_dve, q * OPS + (OPS + 9 + g))
                    dve.tensor_tensor(part[g], part[g], part[2 + g], ALU.mult).then_inc(gate_dve, 1)
                for g in range(FH):
                    dve.wait_ge(gate_dve, q * OPS + (OPS + 11 + g))
                    dve.tensor_tensor(old[g], part[g], part[4 + g], ALU.add).then_inc(gate_dve, 1)
                dve.tensor_copy(aggT[:, :, cut_columns(c, cut)], s.zero[:, 0:1].unsqueeze(1).to_broadcast([P, FH, w])).then_inc(cleared, 1)

            def add_out(c):
                group = LAYERS * NG + c
                for k in range(GT):
                    dve.wait_ge(tile_done, group * GT + (k + 1 + GT))
                    to = s.x[:, bass.ds(c * GT + k, 1), :].rearrange("p t n -> p (t n)")
                    dve.tensor_tensor(to, to, m_banks[k % 2][0:TP, 0:D], ALU.add).then_inc(tile_left, 1)

            def layer(l, last):
                gather(l)
                wait_own(dve, s, gh_copied, (l + 1) * (2 * EIT) + 2)
                gru(l, 0, 0)
                gru(l, 0, 1)
                with dve.Fori(0, NG - 1) as c:
                    gru(l, c + 1, 0)
                    if last:
                        add_out(c)
                    gru(l, c + 1, 1)
                if last:
                    add_out(NG - 1)

            dve.sem_inc(mm_done, RING)
            dve.sem_inc(added, PSR)
            dve.sem_inc(gh_copied, 2)
            dve.sem_inc(gate_dve, OPS)
            dve.sem_inc(tile_left, 1)
            dve.memset(aggT[:, :, :], 0.0).then_inc(cleared, 1)
            dve.wait_ge(w_in, 16 * 4)
            dve.tensor_tensor(b_sum[:, :], b_ih[:, :], b_hh[:, :], ALU.add).then_inc(b_ready, 1)
            with dve.Fori(0, LAYERS - 1) as l:
                layer(l, False)
            layer(LAYERS - 1, True)

        @block.tensor
        def _(pe):
            def group_tiles(group, last):
                pe.wait_ge(staged, group + 1)
                for k in range(GT):
                    pe.wait_ge(tile_left, group * GT + max(1, k))
                    for f in range(FH):
                        h = h_group[:, f, k * TP:(k + 1) * TP]
                        if last:
                            mm = pe.transpose(m_banks[k % 2][0:TP, f * P:(f + 1) * P], h, s.ident[:, :])
                        else:
                            mm = pe.matmul(m_banks[k % 2][0:TP, 0:D], h, w_msg[:, f, :], start=(f == 0), stop=(f == FH - 1))
                    mm.then_inc(tile_done, 1)

            def hidden_gates(l, j, part):
                half, at = part // 3, part % 3 * GHC
                if part % 3 == 0:
                    pe.wait_ge(gh_copied, (l * EIT + j) * 2 + (half + 1))
                for f in range(FH):
                    mm = pe.matmul(s.bank[4 + half][:, at:at + GHC], w_hh[:, f, part * P:(part + 1) * P],
                                   hT[:, f, bass.ds(j * GHC, GHC)], start=(f == 0), stop=(f == FH - 1))
                if part % 3 == 2:
                    mm.then_inc(gh_mm, 1)

            def gather(l):
                wait_own(pe, s, gate_dve, l * (2 * NG * OPS) + OPS)
                with pe.Fori(0, EIT) as j:
                    for k in range(RING):
                        i = j * RING + k
                        pe.wait_ge(row_in[k], (l * EIT + j + 1) * 16)
                        pe.wait_ge(sel_ready, l * ET + i + 1)
                        pe.wait_ge(added, l * ET + i + 1)
                        for f in range(FH):
                            mm = pe.matmul(s.bank[k % PSR][:, f * P:(f + 1) * P], rows[:, k, f * P:(f + 1) * P], sel[:, k % PSR, :],
                                           start=True, stop=True)
                        mm.then_inc(mm_done, 1)
                        if k < GATES:
                            hidden_gates(l, j, k)

            def inputs(l, c, cut):
                q = l * (2 * NG) + c * 2 + cut
                for part in range(GATES):
                    if part in (0, 4):
                        pe.wait_ge(gate_dve, q * OPS + (4 if part == 0 else 8))
                    for f in range(FH):
                        mm = pe.matmul(s.bank[part][:, 0:CUTS[cut]], w_ih[:, f, part * P:(part + 1) * P], aggT[:, f, cut_columns(c, cut)],
                                       start=(f == 0), stop=(f == FH - 1))
                    mm.then_inc(gi_done, 1)

            def layer(l, last):
                gather(l)
                wait_own(pe, s, added, l * ET + ET + PSR)
                wait_own(pe, s, gh_copied, (l + 1) * (2 * EIT) + 2)
                if not last:
                    wait_own(pe, s, w_msg_in, l * 16 + 32)
                inputs(l, 0, 0)
                inputs(l, 0, 1)
                with pe.Fori(0, NG - 1) as c:
                    inputs(l, c + 1, 0)
                    group_tiles(l * NG + c + NG, last)
                    inputs(l, c + 1, 1)
                group_tiles(l * NG + (2 * NG - 1), last)

            pe.wait_ge(w_in, 16 * 4)
            pe.wait_ge(w_msg_in, 16)
            pe.wait_ge(added, PSR)
            with pe.Fori(0, NG) as c:
                group_tiles(c, False)
            with pe.Fori(0, LAYERS - 1) as l:
                layer(l, False)
            layer(LAYERS - 1, True)


def phase_router(nc, s, xT, gate, weights):
    EX, EP = 6, 8
    with ExitStack() as ctx:
        def sb(name, shape, dt=F32):
            return ctx.enter_context(nc.sbuf_tensor(name, shape, dt))
        w1, b1, w2, b2, w_in = weights
        rh = sb("rh", [P, GT * TP])
        logits, probs, top, top_i, top_f = sb("logits", [TP, NT, EP]), sb("probs", [TP, NT, EP]), sb("top", [TP, NT, EP]), sb("top_i", [TP, NT, EP], U32), sb("top_f", [TP, NT, EP])
        one = [sb(f"r_one{n}", [TP, NT]) for n in range(4)]
        pick = sb("r_pick", [TP, NT, EP])
        hid, relu, lg, taken, v, e_done = (s.sem("r_" + n) for n in ("hid", "relu", "lg", "taken", "v", "exp"))
        block = ctx.enter_context(nc.Block())
        CH = GT * TP
        cuts = ((0, 313), (313, CH - 313))

        @block.tensor
        def _(pe):
            pe.wait_ge(w_in, 64)
            with pe.Fori(0, NT // GT) as c:
                for h, (at, n) in enumerate(cuts):
                    for f in range(FH):
                        mm = pe.matmul(s.bank[h][:, 0:n], w1[:, f, :], xT[:, f, bass.ds(c * CH + at, n)], start=(f == 0), stop=(f == FH - 1))
                    mm.then_inc(hid, 1)
                for k in range(GT):
                    if k == 0:
                        pe.wait_ge(taken, c * GT + 1)
                        pe.wait_ge(relu, c * 2 + 2)
                    pe.matmul(s.bank[2 + k][0:TP, 0:EX], rh[:, k * TP:(k + 1) * TP], w2[:, :], start=True, stop=True).then_inc(lg, 1)

        @block.scalar
        def _(act):
            act.wait_ge(w_in, 64)
            with act.Fori(0, NT // GT) as c:
                act.wait_ge(taken, c * GT + 1)
                for h, (at, n) in enumerate(cuts):
                    act.wait_ge(hid, c * 2 + h + 1)
                    act.activation(rh[:, at:at + n], s.bank[h][:, 0:n], ACT.Relu, bias=b1[:, :]).then_inc(relu, 1)
            act.wait_ge(v, 5)
            act.activation(logits[:, :, 0:EX], logits[:, :, 0:EX], ACT.Exp).then_inc(e_done, 1)
            act.wait_ge(v, 9 + 2 * NT + 1)
            act.activation(one[1][:, :], one[1][:, :], ACT.Exp).then_inc(e_done, 1)

        @block.vector
        def _(dve):
            n = [0]

            def step(ins):
                n[0] += 1
                ins.then_inc(v, 1)
                dve.wait_ge(v, n[0])
            step(dve.memset(logits[:, :, :], 0.0))
            step(dve.memset(probs[:, :, :], -1.0))
            dve.sem_inc(taken, 1)
            dve.wait_ge(taken, 1)
            dve.wait_ge(w_in, 64)
            with dve.Fori(0, NT // GT) as c:
                for k in range(GT):
                    dve.wait_ge(lg, c * GT + k + 1)
                    dve.tensor_tensor(logits[:, bass.ds(c * GT + k, 1), 0:EX].rearrange("p t e -> p (t e)"), s.bank[2 + k][0:TP, 0:EX], b2[:, :], ALU.add).then_inc(taken, 1)
            dve.wait_ge(taken, NT + 1)
            L = logits[:, :, 0:EX]

            def wide(v2):
                return v2[:, :].rearrange("p (t o) -> p t o", o=1).broadcast_to([TP, NT, EX])
            step(dve.tensor_reduce(one[0][:, :], L, AX.X, ALU.max))
            step(dve.tensor_copy(pick[:, :, 0:EX], wide(one[0])))
            step(dve.tensor_tensor(L, L, pick[:, :, 0:EX], ALU.subtract))
            dve.wait_ge(e_done, 1)
            step(dve.tensor_reduce(one[0][:, :], L, AX.X, ALU.add))
            step(dve.reciprocal(one[2][:, :], one[0][:, :]))
            step(dve.tensor_copy(pick[:, :, 0:EX], wide(one[2])))
            step(dve.tensor_tensor(probs[:, :, 0:EX], L, pick[:, :, 0:EX], ALU.mult))
            for t in range(NT):
                step(dve.max(top[:, t, :], probs[:, t, :]))
                step(dve.max_index(top_i[:, t, :], top[:, t, :], probs[:, t, :]))
            step(dve.tensor_tensor(one[1][:, :], top[:, :, 1], top[:, :, 0], ALU.subtract))
            step(dve.tensor_copy(top_f[:, :, :], top_i[:, :, :]))
            dve.wait_ge(e_done, 2)
            step(dve.tensor_scalar(one[0][:, :], one[1][:, :], 1.0, None, ALU.add))
            step(dve.reciprocal(one[2][:, :], one[0][:, :]))
            step(dve.tensor_tensor(one[3][:, :], one[1][:, :], one[2][:, :], ALU.mult))
            for t in range(NT):
                step(dve.tensor_scalar(gate[:, t, :], s.iota_row[0:TP, 0:EP], top_f[:, t, 0:1], one[2][:, t:t + 1], ALU.is_equal, ALU.mult))
                step(dve.tensor_scalar(pick[:, t, :], s.iota_row[0:TP, 0:EP], top_f[:, t, 1:2], one[3][:, t:t + 1], ALU.is_equal, ALU.mult))
            step(dve.tensor_tensor(gate[:, :, :], gate[:, :, :], pick[:, :, :], ALU.add))


def phase_experts(nc, s, xT, gate, weights):
    EX = 6
    CH = GT * TP
    cuts = ((0, 313), (313, CH - 313))
    with ExitStack() as ctx:
        def sb(name, shape, dt=F32):
            return ctx.enter_context(nc.sbuf_tensor(name, shape, dt))
        w, b, b3, w_in = weights
        h1, h2 = sb("eh1", [P, 2, FH, CH]), sb("eh2", [P, 2, FH, CH])
        gT = sb("gT", [8, CH])
        gate_now = sb("gate_now", [TP, GT, 8])
        mm, ev, om, oa, gt, gc = (s.sem("f_" + n) for n in ("mm", "ev", "om", "oa", "gt", "gc"))
        block = ctx.enter_context(nc.Block())
        order = []
        for e in range(EX + 2):
            if e < EX:
                order += [("h", 0, e, m, q) for m in range(FH) for q in range(2)]
            if 1 <= e <= EX:
                order += [("h", 1, e - 1, m, q) for m in range(FH) for q in range(2)]
            if e >= 2:
                order += [("o", e - 2, k) for k in range(GT)]
        order += [("b", k) for k in range(GT)]
        hidden = [g for g in order if g[0] == "h"]
        outs = [g for g in order if g[0] != "h"]
        NH, NO = len(hidden), len(outs)
        HB, OB = 4, 3

        @block.tensor
        def _(pe):
            pe.wait_ge(w_in, 16 * (3 * EX + 3))
            with pe.Fori(0, NT // GT) as c:
                nh = no = 0
                pe.wait_ge(oa, c * NO + 1)
                for k in range(GT):
                    if k == 0:
                        pe.wait_ge(gc, c * (GT + 1) + 1)
                    else:
                        pe.wait_ge(gc, c * (GT + 1) + k + 1)
                    pe.transpose(s.bank[7][0:8, 0:TP], gate_now[:, k, :], s.ident[0:TP, 0:TP]).then_inc(gt, 1)
                for g in order:
                    if g[0] == "h":
                        _, layer, e, m, q = g
                        at, n = cuts[q]
                        if nh >= HB:
                            pe.wait_ge(ev, c * NH + nh - HB + 1)
                        if layer == 1:
                            pe.wait_ge(ev, c * NH + hidden.index(("h", 0, e, FH - 1, 1)) + 1)
                        for f in range(FH):
                            rhs = xT[:, f, bass.ds(c * CH + at, n)] if layer == 0 else h1[:, e % 2, f, at:at + n]
                            i = pe.matmul(s.bank[nh % HB][:, 0:n], w[layer][:, e, f, m * P:(m + 1) * P], rhs, start=(f == 0), stop=(f == FH - 1))
                        i.then_inc(mm, 1)
                        nh += 1
                        continue
                    bank = s.bank[HB + no % OB][0:TP, 0:D]
                    if no >= OB:
                        pe.wait_ge(oa, c * NO + no - OB + 2)
                    if g[0] == "o":
                        _, e, k = g
                        if k == 0:
                            pe.wait_ge(ev, c * NH + hidden.index(("h", 1, e, FH - 1, 1)) + 1)
                        for f in range(FH):
                            i = pe.matmul(bank, h2[:, e % 2, f, k * TP:(k + 1) * TP], w[2][:, e, f, :], start=(f == 0), stop=(f == FH - 1))
                    else:
                        k = g[1]
                        pe.wait_ge(gc, (c + 1) * (GT + 1))
                        i = pe.matmul(bank, gT[0:EX, k * TP:(k + 1) * TP], b3[:, :], start=True, stop=True)
                    i.then_inc(om, 1)
                    no += 1

        @block.scalar
        def _(act):
            act.wait_ge(w_in, 16 * (3 * EX + 3))
            with act.Fori(0, NT // GT) as c:
                for n, (_, layer, e, m, q) in enumerate(hidden):
                    at, size = cuts[q]
                    act.wait_ge(mm, c * NH + n + 1)
                    to = (h1 if layer == 0 else h2)[:, e % 2, m, at:at + size]
                    act.activation(to, s.bank[n % HB][:, 0:size], ACT.Relu, bias=b[layer][:, e * FH + m:e * FH + m + 1]).then_inc(ev, 1)

        @block.vector
        def _(dve):
            dve.sem_inc(oa, 1)
            with dve.Fori(0, NT // GT) as c:
                wait_own(dve, s, oa, c * NO + 1)
                dve.tensor_copy(gate_now[:, :, :], gate[:, bass.ds(c * GT, GT), :]).then_inc(gc, 1)
                for k in range(GT):
                    dve.wait_ge(gt, c * GT + k + 1)
                    dve.tensor_copy(gT[:, k * TP:(k + 1) * TP], s.bank[7][0:8, 0:TP]).then_inc(gc, 1)
                for n, g in enumerate(outs):
                    k = g[-1]
                    to = s.x[:, bass.ds(c * GT + k, 1), :].rearrange("p t n -> p (t n)")
                    bank = s.bank[HB + n % OB][0:TP, 0:D]
                    dve.wait_ge(om, c * NO + n + 1)
                    if n >= GT:
                        dve.wait_ge(oa, c * NO + n - GT + 2)
                    if g[0] == "o":
                        dve.scalar_tensor_tensor(out=to, in0=bank, scalar=gate_now[:, k, g[1]:g[1] + 1], in1=to, op0=ALU.mult, op1=ALU.add).then_inc(oa, 1)
                    else:
                        dve.tensor_tensor(to, to, bank, ALU.add).then_inc(oa, 1)


def phase_ffn0(nc, s, a):
    with ExitStack() as ctx:
        xT = ctx.enter_context(nc.sbuf_tensor("xT0", [P, FH, NPAD], F32))
        gate = ctx.enter_context(nc.sbuf_tensor("gate", [TP, NT, 8], F32))

        def sb(name, shape):
            return ctx.enter_context(nc.sbuf_tensor(name, shape, F32))
        EX = 6
        rw1, rb1, rw2, rb2 = sb("rw1", [P, FH, P]), sb("rb1", [P, 1]), sb("rw2", [P, EX]), sb("rb2", [TP, EX])
        w = [sb(f"ew{n}", [P, EX, FH, D]) for n in (1, 2, 3)]
        b = [sb(f"eb{n}", [P, EX * FH]) for n in (1, 2)]
        b3 = sb("eb3", [EX, D])
        r_in, w_in = s.sem("r_w_in"), s.sem("f_w_in")

        def load(sp):
            sp.dma_start(rw1[:, :, :], a["L0_ffn_router_w1"].rearrange("(f p) n -> p f n", p=P)).then_inc(r_in, 16)
            sp.dma_start(rb1[:, :], a["router_b1_cols"]).then_inc(r_in, 16)
            sp.dma_start(rw2[:, :], a["L0_ffn_router_w2"]).then_inc(r_in, 16)
            sp.dma_start(rb2[:, :], a["L0_ffn_router_b2"].rearrange("(o e) -> o e", o=1).broadcast_to([TP, EX])).then_inc(r_in, 16)
            for n in (1, 2, 3):
                for e in range(EX):
                    sp.dma_start(w[n - 1][:, e], a[f"L0_ffn_expert_w{n}"][e].rearrange("(f p) n -> p f n", p=P)).then_inc(w_in, 16)
            for n in (1, 2):
                sp.dma_start(b[n - 1][:, :], a[f"expert_b{n}_cols"]).then_inc(w_in, 16)
            sp.dma_start(b3[:, :], a["L0_ffn_expert_b3"]).then_inc(w_in, 16)

        phase_norm_to_T(nc, s, xT, "n1", load)
        phase_router(nc, s, xT, gate, (rw1, rb1, rw2, rb2, r_in))
        phase_experts(nc, s, xT, gate, (w, b, b3, w_in))


RELS, TYPES, HEADS, DK = 8, 4, 4, 64


def phase_types(nc, s, a):
    with ExitStack() as ctx:
        raw = ctx.enter_context(nc.sbuf_tensor("nt_raw", [NT, TP], I32))
        flt = ctx.enter_context(nc.sbuf_tensor("nt_flt", [NT, TP], F32))
        typ = ctx.enter_context(nc.sbuf_tensor("nt_typ", [TP, NT], F32))
        skip = ctx.enter_context(nc.sbuf_tensor("nt_skip", [TP, TYPES], F32))
        loaded, v, p, sg = s.sem("y_loaded"), s.sem("y_v"), s.sem("y_p"), s.sem("y_sg")
        block = ctx.enter_context(nc.Block())

        @block.sync
        def _(sp):
            sp.dma_start(raw[:, :], a["node_type_4"].rearrange("(t p) -> t p", p=TP)).then_inc(loaded, 16)
            sp.dma_start(skip[:, :], a["L1_gnn_skip"].rearrange("(o t) -> o t", o=1).broadcast_to([TP, TYPES])).then_inc(loaded, 16)
            sp.wait_ge(loaded, 32)

        @block.scalar
        def _(act):
            act.wait_ge(loaded, 32)
            act.activation(skip[:, :], skip[:, :], ACT.Sigmoid).then_inc(sg, 1)

        @block.tensor
        def _(pe):
            pe.wait_ge(v, 1)
            pe.transpose(s.bank[0][0:TP, 0:NT], flt[:, :], s.ident[0:NT, 0:NT]).then_inc(p, 1)

        @block.vector
        def _(dve):
            dve.wait_ge(loaded, 32)
            dve.tensor_copy(flt[:, :], raw[:, :]).then_inc(v, 1)
            dve.wait_ge(p, 1)
            dve.tensor_copy(typ[:, :], s.bank[0][0:TP, 0:NT]).then_inc(v, 1)
            dve.wait_ge(v, 2)
            dve.wait_ge(sg, 1)
            for t in range(TYPES):
                dve.tensor_scalar(s.is_type[:, :, t], typ[:, :], float(t), None, ALU.is_equal).then_inc(v, 1)
                dve.tensor_scalar(s.skip_type[:, :, t], typ[:, :], float(t), skip[:, t:t + 1], ALU.is_equal, ALU.mult).then_inc(v, 1)


def phase_tables(nc, s, a, q_dram, k_dram, vT, rel_v):
    W3 = 3 * D
    with ExitStack() as ctx:
        def sb(name, shape, dt=F32):
            return ctx.enter_context(nc.sbuf_tensor(name, shape, dt))
        xT = sb("xT1", [P, FH, N + TP])
        w = sb("wqkv", [P, FH, TYPES, W3])
        rel_k = sb("rel_k", [P, FH, RELS, P])
        pri = sb("pri", [P, FH * RELS])
        x_tile = sb("x_tile", [P, 2, FH, TP])
        qkv = sb("qkv", [TP, 2, W3])
        kT = sb("kT", [P, 2, FH, TP])
        tab = sb("tab", [TP, 2, RELS, D])
        names = ("w_in", "z", "scaled", "staged", "mm", "summed", "turned", "kv", "tm", "te")
        w_in, z, scaled, staged, mm, summed, turned, kv, tm, te = (s.sem("t_" + n) for n in names)
        q_stored = [s.sem(f"t_q_stored{n}") for n in range(2)]
        t_stored = [s.sem(f"t_t_stored{n}") for n in range(2)]
        NW = 3 * TYPES + 3 * HEADS + 1
        PAIRS = NT // 2
        k_rows = k_dram.rearrange("(r n) f -> n r f", r=RELS)

        with nc.Block() as block:

            @block.vector
            def _(dve):
                dve.memset(rel_k[:, :, :, :], 0.0).then_inc(z, 1)
                dve.memset(rel_v[:, :, :, :], 0.0).then_inc(z, 1)
                dve.memset(vT[:, :, N:], 0.0).then_inc(z, 1)
                dve.memset(tab[0:NR - N, 0], 0.0).then_inc(z, 1)

            @block.sync
            def _(sp):
                for n, name in enumerate(("q", "k", "v")):
                    for t in range(TYPES):
                        sp.dma_start(w[:, :, t, n * D:(n + 1) * D], a[f"L1_gnn_{name}_linears"][t].rearrange("(f p) n -> p f n", p=P)).then_inc(w_in, 16)
                sp.wait_ge(z, 4)
                sp.dma_start(k_rows[N:NR], tab[0:NR - N, 0]).then_inc(w_in, 16)
                for h in range(HEADS):
                    at = DK * (h % 2)
                    sp.dma_start(rel_k[at:at + DK, h // 2, :, at:at + DK], a["rel_attT"][:, h].rearrange("r e d -> e r d")).then_inc(w_in, 16)
                    sp.dma_start(rel_v[at:at + DK, h // 2, :, at:at + DK], a["L1_gnn_relation_msg"][:, h].rearrange("r d e -> d r e")).then_inc(w_in, 16)
                    sp.dma_start(pri[at:at + DK, (h // 2) * RELS:(h // 2 + 1) * RELS], a["priT"][h:h + 1, :].broadcast_to([DK, RELS])).then_inc(w_in, 16)

        phase_norm_to_T(nc, s, xT, "n2")
        block = ctx.enter_context(nc.Block())

        @block.sync
        def _(sp):
            def store(t, k):
                rows = bass.ds(t * TP, TP)
                sp.wait_ge(summed, t * 8 + 12)
                sp.dma_start(q_dram[rows, :], qkv[:, k, 0:D]).then_inc(q_stored[k], 16)
                sp.wait_ge(te, t * 4 + 5)
                sp.dma_start(k_rows[rows], tab[:, k]).then_inc(t_stored[k], 16)

            with sp.Fori(0, PAIRS) as j:
                store(j * 2, 0)
                store(j * 2 + 1, 1)
            store(NT - 1, 0)
            sp.wait_ge(q_stored[0], 16 * (PAIRS + 1))
            sp.wait_ge(q_stored[1], 16 * PAIRS)
            sp.wait_ge(t_stored[0], 16 * (PAIRS + 1))
            sp.wait_ge(t_stored[1], 16 * PAIRS)

        @block.scalar
        def _(act):
            def evacuate(t, k, j):
                act.wait_ge(turned, t + 1)
                act.copy(kT[:, k], s.bank[4][:, 0:FH * TP].rearrange("p (f n) -> p f n", f=FH)).then_inc(kv, 1)
                act.copy(vT[:, :, bass.ds(t * TP, TP)], s.bank[4][:, FH * TP:2 * FH * TP].rearrange("p (f n) -> p f n", f=FH)).then_inc(kv, 1)
                if j is not None:
                    wait_own(act, s, t_stored[k], j * 16)
                for n in range(4):
                    f, quad = n // 2, n % 2
                    act.wait_ge(tm, t * 4 + n + 1)
                    act.copy(tab[:, k, 4 * quad:4 * quad + 4, f * P:(f + 1) * P],
                             s.bank[5 + n % 3][0:TP, :].rearrange("p (r d) -> p r d", r=4)).then_inc(te, 1)

            act.wait_ge(scaled, 2)
            act.sem_inc(te, 1)
            for k in range(2):
                act.copy(x_tile[:, k], xT[:, :, k * TP:(k + 1) * TP]).then_inc(staged, 1)
            def round_of(j, first):
                for k in range(2):
                    evacuate(j * 2 + k, k, None if first else j)
                    act.wait_ge(mm, j * 8 + (4 * k + 4))
                    act.copy(x_tile[:, k], xT[:, :, bass.ds(j * (2 * TP) + (2 + k) * TP, TP)]).then_inc(staged, 1)

            round_of(0, True)
            with act.Fori(1, PAIRS) as j:
                round_of(j, False)
            evacuate(NT - 1, 0, PAIRS)

        @block.vector
        def _(dve):
            dve.sem_inc(summed, 4)
            dve.wait_ge(w_in, 16 * NW)
            att = rel_k[:, :, :, :].rearrange("p f r d -> p (f r) d")
            dve.scalar_tensor_tensor(out=att, in0=att, scalar=1.0 / DK ** 0.5,
                                     in1=pri[:, :].rearrange("p (r o) -> p r o", o=1).broadcast_to([P, FH * RELS, P]),
                                     op0=ALU.mult, op1=ALU.mult).then_inc(scaled, 2)

            def accumulate(t, k, j):
                if j is not None:
                    wait_own(dve, s, q_stored[k], j * 16)
                for y in range(TYPES):
                    dve.wait_ge(mm, t * 4 + y + 1)
                    one = s.is_type[:, bass.ds(t, 1), y]
                    for part, (lo, hi) in enumerate(((0, 512), (512, W3))):
                        bank, to = s.bank[2 * (y % 2) + part][0:TP, 0:hi - lo], qkv[:, k, lo:hi]
                        if y == 0:
                            dve.tensor_scalar(to, bank, one, None, ALU.mult).then_inc(summed, 1)
                        else:
                            dve.wait_ge(summed, t * 8 + 2 * y + part - 1 + 4)
                            dve.scalar_tensor_tensor(out=to, in0=bank, scalar=one, in1=to, op0=ALU.mult, op1=ALU.add).then_inc(summed, 1)

            accumulate(0, 0, None)
            accumulate(1, 1, None)
            with dve.Fori(1, PAIRS) as j:
                accumulate(j * 2, 0, j)
                accumulate(j * 2 + 1, 1, j)
            accumulate(NT - 1, 0, PAIRS)

        @block.tensor
        def _(pe):
            def typed(t, k):
                pe.wait_ge(staged, t + 1)
                for y in range(TYPES):
                    pe.wait_ge(summed, t * 8 + 2 * y + 2)
                    for part, (lo, hi) in enumerate(((0, 512), (512, W3))):
                        for f in range(FH):
                            i = pe.matmul(s.bank[2 * (y % 2) + part][0:TP, 0:hi - lo], x_tile[:, k, f, :], w[:, f, y, lo:hi], start=(f == 0), stop=(f == FH - 1))
                    i.then_inc(mm, 1)

            def turn(t, k):
                pe.wait_ge(summed, t * 8 + 12)
                pe.wait_ge(kv, t * 2 + 2)
                for n in range(4):
                    i = pe.transpose(s.bank[4][:, n * TP:(n + 1) * TP], qkv[:, k, D + n * P:D + (n + 1) * P], s.ident[0:TP, 0:TP])
                i.then_inc(turned, 1)

            def tables(t, k):
                pe.wait_ge(kv, t * 2 + 4)
                for n in range(4):
                    f, quad = n // 2, n % 2
                    pe.wait_ge(te, t * 4 + (1 if n < 3 else n - 3 + 2))
                    pe.matmul(s.bank[5 + n % 3][0:TP, :], kT[:, k, f, :], rel_k[:, f, 4 * quad:4 * quad + 4, :].rearrange("p r d -> p (r d)"),
                              start=True, stop=True).then_inc(tm, 1)

            pe.wait_ge(w_in, 16 * NW)
            pe.wait_ge(scaled, 2)
            typed(0, 0)
            turn(0, 0)
            with pe.Fori(0, PAIRS) as j:
                typed(j * 2 + 1, 1)
                tables(j * 2, 0)
                turn(j * 2 + 1, 1)
                typed(j * 2 + 2, 0)
                tables(j * 2 + 1, 1)
                turn(j * 2 + 2, 0)
            tables(NT - 1, 0)

        @block.gpsimd
        def _(pool):
            pool.sem_inc(kv, 2)


def phase_scores(nc, s, q_dram, k_dram, v_dram, vT, rel_v, score):
    QR = 8
    V_MM, V_OUT = (1, 3, 5, 7), (2, 4, 6, 8)
    with ExitStack() as ctx:
        def sb(name, shape, dt=F32):
            return ctx.enter_context(nc.sbuf_tensor(name, shape, dt))
        rows = sb("c_rows", [P, RING, D])
        idx = sb("c_idx", [P, RING], I32)
        q_win = sb("q_win", [P, QR, D])
        sel, selT = sb("c_sel", [P, PSR, P]), sb("c_selT", [P, PSR, P])
        prod = sb("c_prod", [P, 2, D])
        v_tile = sb("v_tile", [P, FH, GHC])
        tab = sb("v_tab", [GHC, RELS, D])
        v_rows = v_dram.rearrange("(r n) f -> n r f", r=RELS)
        v_staged, v_mm, v_left, v_stored = (s.sem("c_" + n) for n in ("v_staged", "v_mm", "v_left", "v_stored"))
        names = ("idx_ready", "sel_ready", "turned", "selT_ready", "q_done", "prod_done", "red_done", "up")
        idx_ready, sel_ready, turned, selT_ready, q_done, prod_done, red_done, up = (s.sem("c_" + n) for n in names)
        row_in = [s.sem(f"c_row_in{k}") for k in range(RING)]
        q_in = [s.sem(f"c_q_in{k}") for k in range(QR)]
        block = ctx.enter_context(nc.Block())

        @block.gpsimd
        def _(pool):
            pool.wait_ge(up, 4)
            with pool.Fori(0, EIT) as j:
                for k in range(RING):
                    if k % HR == 0:
                        wait_own(pool, s, idx_ready, j * 2 + (k // HR + 1))
                    pool.indirect_dma_start(out=rows[:, k, :], out_offset=None, in_=k_dram,
                                            in_offset=bass.IndirectOffsetOnAxis(ap=idx[:, k:k + 1], axis=0)).then_inc(row_in[k], 16)

        @block.sync
        def _(sp):
            sp.wait_ge(up, 4)
            with sp.Fori(0, EIT) as j:
                for k in range(RING):
                    if k % BL == 0:
                        base = load_bases(nc, SP, s, j * RING + k, BL)
                    sp.wait_ge(q_done, j * RING + (k + 1))
                    sp.dma_start(q_win[:, k % QR, :], q_dram[bass.ds(base[k % BL], P), :]).then_inc(q_in[k % QR], 16)

        @block.scalar
        def _(act):
            def stage(j, half):
                wait_own(act, s, prod_done, j * RING + (half + 1) * HR)
                act.copy(idx[:, half * HR:(half + 1) * HR], s.rel_idx[:, bass.ds(j * RING + half * HR, HR)]).then_inc(idx_ready, 1)

            def evacuate(i, k):
                act.wait_ge(q_done, i + (QR - PSR + 1) + 0)
                act.wait_ge(turned, i + 1)
                act.copy(selT[:, k % PSR, :], s.bank[k % 2][:, 0:P]).then_inc(selT_ready, 1)

            def stage_v(j):
                wait_own(act, s, v_mm, j * 4 + 4)
                act.copy(v_tile[:, :, :], vT[:, :, bass.ds(j * GHC, GHC)]).then_inc(v_staged, 1)

            def evacuate_v(j, n):
                f, quad = n // 2, n % 2
                act.wait_ge(v_mm, j * 4 + (n + 5))
                act.copy(tab[:, 4 * quad:4 * quad + 4, f * P:(f + 1) * P],
                         s.bank[6 + n % 2][0:GHC, :].rearrange("p (r d) -> p r d", r=4)).then_inc(v_left, 1)

            act.wait_ge(up, 4)
            act.sem_inc(v_mm, 4)
            act.sem_inc(v_left, 2)
            act.copy(idx[:, 0:HR], s.rel_idx[:, 0:HR]).then_inc(idx_ready, 1)
            act.wait_ge(turned, 1)
            act.copy(selT[:, 0, :], s.bank[0][:, 0:P]).then_inc(selT_ready, 1)
            with act.Fori(0, EIT) as j:
                for k in range(RING):
                    if k == 0:
                        stage(j, 1)
                    if k == HR:
                        stage(j + 1, 0)
                    evacuate(j * RING + (k + 1), k + 1)
                    if k == 0:
                        stage_v(j)
                    if k in V_OUT:
                        evacuate_v(j, V_OUT.index(k))
                    if k == V_OUT[-1]:
                        act.wait_ge(v_left, j * 4 + 6)
                        act.dma_start(v_rows[bass.ds(j * GHC, GHC)], tab[:, :, :]).then_inc(v_stored, 16)
                    if k == RING - 1:
                        wait_own(act, s, v_stored, j * 16 + 16)

        @block.vector
        def _(dve):
            def select(i, k):
                dve.tensor_scalar(sel[:, k % PSR, :], s.iota_row[:, :], s.dst_rel[:, bass.ds(i, 1)], None, ALU.is_equal).then_inc(sel_ready, 1)

            dve.memset(score[:, :, :], 0.0).then_inc(up, 1)
            dve.sem_inc(prod_done, RING)
            dve.sem_inc(q_done, QR)
            dve.sem_inc(up, 3)
            dve.wait_ge(up, 4)
            select(0, 0)
            select(1, 1)
            select(2, 2)
            with dve.Fori(0, EIT) as j:
                for k in range(RING):
                    i = j * RING + k
                    dve.wait_ge(row_in[k], (j + 1) * 16)
                    dve.wait_ge(q_done, i + (1 + QR))
                    dve.tensor_tensor(prod[:, k % 2, :], rows[:, k, :], s.bank[2 + k % PSR][:, 0:D], ALU.mult).then_inc(prod_done, 1)
                    select(i + 3, k + 3)
                    dve.wait_ge(prod_done, i + (1 + RING))
                    dve.tensor_reduce(score[:, :, bass.ds(i, 1)].rearrange("p h o -> p (h o)"), prod[:, k % 2, :].rearrange("p (h d) -> p h d", h=HEADS), AX.X, ALU.add).then_inc(red_done, 1)

        @block.tensor
        def _(pe):
            def turn(i, k):
                pe.wait_ge(sel_ready, i + 1)
                pe.transpose(s.bank[k % 2][:, 0:P], sel[:, k % PSR, :], s.ident[:, :]).then_inc(turned, 1)

            pe.wait_ge(up, 4)
            turn(0, 0)
            with pe.Fori(0, EIT) as j:
                for k in range(RING):
                    i = j * RING + k
                    pe.wait_ge(selT_ready, i + 1)
                    turn(i + 1, k + 1)
                    pe.wait_ge(q_in[k % QR], (j * 2 + (k // QR + 1)) * 16)
                    pe.wait_ge(prod_done, i + (1 + RING - PSR))
                    pe.matmul(s.bank[2 + k % PSR][:, 0:D], selT[:, k % PSR, :], q_win[:, k % QR, :], start=True, stop=True).then_inc(q_done, 1)
                    if k in V_MM:
                        n = V_MM.index(k)
                        if n == 0:
                            pe.wait_ge(v_staged, j + 1)
                        pe.wait_ge(v_left, j * 4 + (n + 1))
                        pe.matmul(s.bank[6 + n % 2][0:GHC, :], v_tile[:, n // 2, :], rel_v[:, n // 2, n % 2 * 4:n % 2 * 4 + 4, :].rearrange("p r d -> p (r d)"),
                                  start=True, stop=True).then_inc(v_mm, 1)


def phase_softmax(nc, s, score, alpha):
    TILE = [P, EC, HEADS, P]
    with ExitStack() as ctx:
        def sb(name, shape, dt=F32):
            return ctx.enter_context(nc.sbuf_tensor("m_" + name, shape, dt))
        sc, same_f, same_b, pen_f, pen_b, fwd, bwd, seg, ex = (sb(n, TILE) for n in ("sc", "same_f", "same_b", "pen_f", "pen_b", "fwd", "bwd", "seg", "ex"))
        same, out_first, out_last = (sb(n, [P, EC, P]) for n in ("same", "out_first", "out_last"))
        ends = sb("ends", [P, EC, 4, HEADS])
        whole = sb("whole", [P, EC, HEADS])
        tot = sb("tot", [P, EC, 2, HEADS])
        SEQ = 2 * EC * P
        val, key, t_f, t_b, t_same_f, t_same_b, t_pen_f, t_pen_b = (sb(n, [HEADS, SEQ]) for n in ("val", "key", "t_f", "t_b", "t_same_f", "t_same_b", "t_pen_f", "t_pen_b"))
        v, p, e_done = s.sem("m_v"), s.sem("m_p"), s.sem("m_e")
        block = ctx.enter_context(nc.Block())
        marks = {}

        def flat(t):
            return t[:, :, :, :].rearrange("p c h e -> p (c h e)")

        def seq(t, c):
            return t[:, c * 2 * P:(c + 1) * 2 * P].rearrange("h (i w) -> h w i", w=2)

        @block.vector
        def _(dve):
            n = [0]

            def step(ins):
                n[0] += 1
                ins.then_inc(v, 1)
                dve.wait_ge(v, n[0])

            keys = s.dst_by_tile
            dve.wait_ge(p, 1)
            for h in range(HEADS):
                step(dve.tensor_copy(sc[:, :, h, :], s.bank[h][:, :].rearrange("p (c e) -> p c e", c=EC)))
            step(dve.memset(same[:, :, 0:1], 0.0))
            step(dve.tensor_tensor(same[:, :, 1:P], keys[:, :, 1:P], keys[:, :, 0:P - 1], ALU.is_equal))
            step(dve.memset(flat(same_b), 0.0))
            for h in range(HEADS):
                step(dve.tensor_copy(same_f[:, :, h, :], same[:, :, :]))
                step(dve.tensor_copy(same_b[:, :, h, 0:P - 1], same[:, :, 1:P]))
            step(dve.tensor_scalar(flat(pen_f), flat(same_f), 1.0, BIG, ALU.subtract, ALU.mult))
            step(dve.tensor_scalar(flat(pen_b), flat(same_b), 1.0, BIG, ALU.subtract, ALU.mult))
            for c in range(EC):
                step(dve.tensor_scalar(out_first[:, c, :], keys[:, c, :], keys[:, c, 0:1], 1.0, ALU.is_equal, ALU.subtract))
                step(dve.tensor_scalar(out_last[:, c, :], keys[:, c, :], keys[:, c, P - 1:P], 1.0, ALU.is_equal, ALU.subtract))
                step(dve.tensor_copy(ends[:, c, 2, :], keys[:, c, 0:1].broadcast_to([P, HEADS])))
                step(dve.tensor_copy(ends[:, c, 3, :], keys[:, c, P - 1:P].broadcast_to([P, HEADS])))
            step(dve.tensor_scalar(out_first[:, :, :], out_first[:, :, :], BIG, None, ALU.mult))
            step(dve.tensor_scalar(out_last[:, :, :], out_last[:, :, :], BIG, None, ALU.mult))
            step(dve.tensor_tensor(whole[:, :, :], ends[:, :, 2, :], ends[:, :, 3, :], ALU.not_equal))

            def across(last, scan):
                step(dve.tensor_copy(ends[:, :, 0, :], seg[:, :, :, 0]))
                step(dve.tensor_copy(ends[:, :, 1, :], seg[:, :, :, P - 1]))
                if scan == "add":
                    step(dve.tensor_tensor(ends[:, :, 1, :], ends[:, :, 1, :], whole[:, :, :], ALU.mult))
                marks["ends", scan] = n[0]
                dve.wait_ge(p, last + 1)
                for c in range(EC):
                    b = s.bank[c][0:HEADS, :].rearrange("h (w i) -> h w i", w=4)
                    step(dve.tensor_copy(seq(val, c), b[:, 0:2, :]))
                    if scan == "max":
                        step(dve.tensor_copy(seq(key, c), b[:, 2:4, :]))
                if scan == "max":
                    step(dve.memset(t_same_f[:, 0:1], 0.0))
                    step(dve.memset(t_same_b[:, SEQ - 1:SEQ], 0.0))
                    step(dve.tensor_tensor(t_same_f[:, 1:SEQ], key[:, 1:SEQ], key[:, 0:SEQ - 1], ALU.is_equal))
                    step(dve.tensor_copy(t_same_b[:, 0:SEQ - 1], t_same_f[:, 1:SEQ]))
                    step(dve.tensor_scalar(t_pen_f[:, :], t_same_f[:, :], 1.0, BIG, ALU.subtract, ALU.mult))
                    step(dve.tensor_scalar(t_pen_b[:, :], t_same_b[:, :], 1.0, BIG, ALU.subtract, ALU.mult))
                    both(t_f[:, :], t_b[:, :], val[:, :], t_pen_f[:, :], t_pen_b[:, :], "max")
                    step(dve.tensor_tensor(val[:, :], t_f[:, :], t_b[:, :], ALU.max))
                else:
                    both(t_f[:, :], t_b[:, :], val[:, :], t_same_f[:, :], t_same_b[:, :], "add")
                    step(dve.tensor_tensor(t_f[:, :], t_f[:, :], t_b[:, :], ALU.add))
                    step(dve.tensor_tensor(val[:, :], t_f[:, :], val[:, :], ALU.subtract))
                marks["tot", scan] = n[0]
                dve.wait_ge(p, last + 2)
                step(dve.tensor_copy(tot[:, :, :, :].rearrange("p c w h -> p (c w h)"), s.bank[4][:, 0:EC * 2 * HEADS]))
                for w, outside in enumerate((out_first, out_last)):
                    for c in range(EC):
                        for h in range(HEADS):
                            step(dve.scalar_tensor_tensor(out=seg[:, c, h, :], in0=outside[:, c, :], scalar=tot[:, c, w, h:h + 1], in1=seg[:, c, h, :],
                                                          op0=ALU.add, op1=ALU.max))

            def both(f, b, x, m_f, m_b, scan):
                op0, op1 = (ALU.add, ALU.max) if scan == "max" else (ALU.mult, ALU.add)
                init = -BIG if scan == "max" else 0.0
                step(dve.tensor_tensor_scan(f, m_f, x, init, op0, op1))
                step(dve.tensor_tensor_scan(b[:, ::-1], m_b[:, ::-1], x[:, ::-1], init, op0, op1))

            both(flat(fwd), flat(bwd), flat(sc), flat(pen_f), flat(pen_b), "max")
            step(dve.tensor_tensor(flat(seg), flat(fwd), flat(bwd), ALU.max))
            across(1, "max")
            step(dve.tensor_tensor(flat(sc), flat(sc), flat(seg), ALU.subtract))
            marks["shifted"] = n[0]
            dve.wait_ge(e_done, 1)
            both(flat(fwd), flat(bwd), flat(ex), flat(same_f), flat(same_b), "add")
            step(dve.tensor_tensor(flat(seg), flat(fwd), flat(bwd), ALU.add))
            step(dve.tensor_tensor(flat(seg), flat(seg), flat(ex), ALU.subtract))
            across(3, "add")
            step(dve.reciprocal(flat(fwd), flat(seg)))
            step(dve.tensor_tensor(flat(ex), flat(ex), flat(fwd), ALU.mult))
            marks["alpha"] = n[0]
            dve.wait_ge(p, 6)
            for h in range(HEADS):
                step(dve.tensor_copy(alpha[:, h, :], s.bank[h][:, :]))

        @block.scalar
        def _(act):
            act.wait_ge(v, marks["shifted"])
            act.activation(flat(ex), flat(sc), ACT.Exp).then_inc(e_done, 1)

        @block.tensor
        def _(pe):
            for h in range(HEADS):
                for c in range(EC):
                    i = pe.transpose(s.bank[h][:, c * P:(c + 1) * P], score[:, h, c * P:(c + 1) * P], s.ident[:, :])
            i.then_inc(p, 1)
            for scan in ("max", "add"):
                pe.wait_ge(v, marks["ends", scan])
                for c in range(EC):
                    for w in range(4):
                        i = pe.transpose(s.bank[c][0:HEADS, w * P:(w + 1) * P], ends[:, c, w, :], s.ident[:, :])
                i.then_inc(p, 1)
                pe.wait_ge(v, marks["tot", scan])
                for c in range(EC):
                    for w in range(2):
                        at = (c * 2 + w) * HEADS
                        i = pe.transpose(s.bank[4][:, at:at + HEADS], seq(val, c)[:, w, :], s.ident[0:HEADS, 0:HEADS])
                i.then_inc(p, 1)
            pe.wait_ge(v, marks["alpha"])
            for h in range(HEADS):
                for c in range(EC):
                    i = pe.transpose(s.bank[h][:, c * P:(c + 1) * P], ex[:, c, h, :], s.ident[:, :])
            i.then_inc(p, 1)


def phase_messages(nc, s, a, v_dram, alpha, aggT, wa, wa_in):
    with ExitStack() as ctx:
        def sb(name, shape, dt=F32):
            return ctx.enter_context(nc.sbuf_tensor(name, shape, dt))
        rows = sb("d_rows", [P, RING, D])
        idx = sb("d_idx", [P, RING], I32)
        sel = sb("d_sel", [P, PSR, P])
        msg = sb("d_msg", [P, PSR, D])
        idx_ready, msg_ready, mm_done, added, up = (s.sem("d_" + n) for n in ("idx_ready", "msg_ready", "mm_done", "added", "up"))
        row_in = [s.sem(f"d_row_in{k}") for k in range(RING)]
        block = ctx.enter_context(nc.Block())

        @block.sync
        def _(sp):
            for t in range(TYPES):
                sp.dma_start(wa[:, :, t, :], a["L1_gnn_a_linears"][t].rearrange("(f p) n -> p f n", p=P)).then_inc(wa_in, 16)

        @block.gpsimd
        def _(pool):
            pool.wait_ge(up, 1)
            with pool.Fori(0, EIT) as j:
                for k in range(RING):
                    if k % HR == 0:
                        wait_own(pool, s, idx_ready, j * 2 + (k // HR + 1))
                    pool.indirect_dma_start(out=rows[:, k, :], out_offset=None, in_=v_dram,
                                            in_offset=bass.IndirectOffsetOnAxis(ap=idx[:, k:k + 1], axis=0)).then_inc(row_in[k], 16)

        @block.scalar
        def _(act):
            act.wait_ge(up, 1)
            with act.Fori(0, EIT) as j:
                for half in range(2):
                    wait_own(act, s, msg_ready, j * RING + (half + 1) * HR)
                    act.copy(idx[:, half * HR:(half + 1) * HR], s.rel_idx[:, bass.ds(j * RING + half * HR, HR)]).then_inc(idx_ready, 1)

        @block.vector
        def _(dve):
            def weigh(j, k):
                i = j * RING + k
                dve.tensor_scalar(sel[:, k % PSR, :], s.iota_row[:, :], s.dst_rel[:, bass.ds(i, 1)], None, ALU.is_equal).then_inc(up, 1)
                dve.wait_ge(row_in[k], (j + 1) * 16)
                dve.tensor_tensor(msg[:, k % PSR, :].rearrange("p (h d) -> p h d", h=HEADS), rows[:, k, :].rearrange("p (h d) -> p h d", h=HEADS),
                                  alpha[:, :, bass.ds(i, 1)].broadcast_to([P, HEADS, DK]), ALU.mult).then_inc(msg_ready, 1)

            def add(j, k, base):
                i = j * RING + k
                win = aggT[:, :, bass.ds(base[k], P)]
                dve.wait_ge(mm_done, i + 1)
                dve.wait_ge(added, i + PSR)
                dve.tensor_tensor(win, win, s.bank[k % PSR][:, 0:D].rearrange("p (f n) -> p f n", f=FH), ALU.add).then_inc(added, 1)

            dve.memset(aggT[:, :, :], 0.0).then_inc(added, PSR)
            dve.wait_ge(added, PSR)
            dve.sem_inc(msg_ready, RING)
            dve.sem_inc(up, 1)
            with dve.Fori(0, EIT) as j:
                base = []
                for k in range(RING):
                    if k % BL == 0:
                        base += load_bases(nc, DVE, s, j * RING + k, BL)
                    weigh(j, k)
                    if k >= 2:
                        add(j, k - 2, base)
                add(j, RING - 2, base)
                add(j, RING - 1, base)

        @block.tensor
        def _(pe):
            pe.wait_ge(up, 1)
            with pe.Fori(0, EIT) as j:
                for k in range(RING):
                    i = j * RING + k
                    pe.wait_ge(msg_ready, i + (1 + RING))
                    pe.wait_ge(added, i + 1)
                    for f in range(FH):
                        mm = pe.matmul(s.bank[k % PSR][:, f * P:(f + 1) * P], msg[:, k % PSR, f * P:(f + 1) * P], sel[:, k % PSR, :], start=True, stop=True)
                    mm.then_inc(mm_done, 1)


def phase_project(nc, s, aggT, w, w_in):
    with ExitStack() as ctx:
        tile = ctx.enter_context(nc.sbuf_tensor("a_tile", [P, GT, FH, TP], F32))
        staged, mm, added = (s.sem("a_" + n) for n in ("staged", "mm", "added"))
        block = ctx.enter_context(nc.Block())

        @block.scalar
        def _(act):
            act.sem_inc(mm, 2 * GT)
            with act.Fori(0, NT // GT) as c:
                for k in range(GT):
                    act.wait_ge(mm, (c * GT + k) * 2 + 2)
                    act.copy(tile[:, k], aggT[:, :, bass.ds((c * GT + k) * TP, TP)]).then_inc(staged, 1)

        @block.tensor
        def _(pe):
            pe.wait_ge(w_in, 16 * TYPES)
            with pe.Fori(0, NT // GT) as c:
                for k in range(GT):
                    pe.wait_ge(staged, c * GT + k + 1)
                    for half in range(2):
                        n = k * 2 + half
                        pe.wait_ge(added, ((c * GT + k) * 2 + half) * 2 + 2)
                        for f in range(FH):
                            i = pe.matmul(s.bank[n % 5][0:TP, :], tile[:, k, f, :], w[:, f, 2 * half:2 * half + 2, :].rearrange("p t n -> p (t n)"), start=(f == 0), stop=(f == FH - 1))
                        i.then_inc(mm, 1)

        @block.vector
        def _(dve):
            dve.sem_inc(added, 10)
            with dve.Fori(0, NT // GT) as c:
                for k in range(GT):
                    to = s.x[:, bass.ds(c * GT + k, 1), :].rearrange("p t n -> p (t n)")
                    for y in range(TYPES):
                        n = k * 2 + y // 2
                        dve.wait_ge(mm, (c * GT + k) * 2 + y // 2 + 1 + 2 * GT)
                        dve.wait_ge(added, (c * GT + k) * 4 + y + 10)
                        dve.scalar_tensor_tensor(out=to, in0=s.bank[n % 5][0:TP, (y % 2) * D:(y % 2 + 1) * D], scalar=s.skip_type[:, bass.ds(c * GT + k, 1), y], in1=to,
                                                 op0=ALU.mult, op1=ALU.add).then_inc(added, 1)


def phase_attention(nc, s, a):
    q_dram = nc.dram_tensor("q_dram", [N, D], F32, kind="Internal").ap()
    k_dram = nc.dram_tensor("k_dram", [RELS * NR, D], F32, kind="Internal").ap()
    v_dram = nc.dram_tensor("v_dram", [RELS * NR, D], F32, kind="Internal").ap()
    phase_types(nc, s, a)
    with ExitStack() as ctx:
        alpha = ctx.enter_context(nc.sbuf_tensor("alpha", [P, HEADS, EC * P], F32))
        with ExitStack() as v_ctx:
            vT = v_ctx.enter_context(nc.sbuf_tensor("vT", [P, FH, NR], F32))
            rel_v = v_ctx.enter_context(nc.sbuf_tensor("rel_v", [P, FH, RELS, P], F32))
            phase_tables(nc, s, a, q_dram, k_dram, vT, rel_v)
            score = v_ctx.enter_context(nc.sbuf_tensor("score", [P, HEADS, EC * P], F32))
            phase_scores(nc, s, q_dram, k_dram, v_dram, vT, rel_v, score)
            phase_softmax(nc, s, score, alpha)
        aggT = ctx.enter_context(nc.sbuf_tensor("aggT1", [P, FH, NPAD], F32))
        wa = ctx.enter_context(nc.sbuf_tensor("wa", [P, FH, TYPES, D], F32))
        wa_in = s.sem("a_w_in")
        phase_messages(nc, s, a, v_dram, alpha, aggT, wa, wa_in)
        phase_project(nc, s, aggT, wa, wa_in)


MX, MF = 8, 1024
CAP = 489
BUF = 31 * P
FAR = 100000.0
assert CAP == -(-5 * N // (4 * MX)) and BUF >= MX * CAP


def phase_switch_route(nc, s, a, buf_dram, slot_in, slot_out, keep, load_experts):
    with ExitStack() as ctx:
        def sb(name, shape, dt=F32):
            return ctx.enter_context(nc.sbuf_tensor("z_" + name, shape, dt))
        xT = sb("xT", [P, FH, NPAD])
        wg, bg = sb("wg", [P, FH, MX]), sb("bg", [TP, MX])
        x_tile = sb("x_tile", [P, GT, FH, TP])
        probs, spread, hot, count, before = (sb(n, [TP, NT, MX]) for n in ("probs", "spread", "hot", "count", "before"))
        top, top_i = sb("top", [TP, NT, 8]), sb("top_i", [TP, NT, 8], U32)
        best, pos, kept, far, red = (sb(n, [TP, NT]) for n in ("best", "pos", "kept", "far", "red"))
        upto, ones = sb("upto", [TP, TP]), sb("ones", [TP, TP])
        zero_row, zero_seq = sb("zero_row", [P, D]), sb("zero_seq", [TP, NT])
        w_in = s.sem("z_w_in")

        def load(sp):
            sp.dma_start(wg[:, :, :], a["L1_ffn_gate_w"].rearrange("(f p) n -> p f n", p=P)).then_inc(w_in, 16)
            sp.dma_start(bg[:, :], a["L1_ffn_gate_b"].rearrange("(o e) -> o e", o=1).broadcast_to([TP, MX])).then_inc(w_in, 16)
            load_experts(sp)

        phase_norm_to_T(nc, s, xT, "n3", load)
        staged, lg, taken, v, e_done, made, p, zeroed, z_up = (s.sem("z_" + n) for n in ("staged", "lg", "taken", "v", "e_done", "made", "p", "zeroed", "z_up"))
        marks = {}
        block = ctx.enter_context(nc.Block())

        @block.gpsimd
        def _(pool):
            pool.memset(ones[:, :], 1.0).then_inc(made, 1)
            pool.memset(upto[:, :], 1.0).then_inc(made, 1)
            pool.wait_ge(made, 2)
            pool.affine_select(out=upto[:, :], in_=upto[:, :], compare_op=ALU.is_ge, fill=0.0, base=0, pattern=[[1, TP]], channel_multiplier=-1).then_inc(made, 1)
            pool.memset(zero_row[:, :], 0.0).then_inc(z_up, 1)

        @block.sync
        def _(sp):
            sp.wait_ge(z_up, 1)
            sp.dma_start(buf_dram.rearrange("(p r) f -> p r f", p=P), zero_row[:, :].rearrange("p (o f) -> p o f", o=1).broadcast_to([P, BUF // P, D])).then_inc(zeroed, 16)
            sp.wait_ge(zeroed, 16)

        @block.vector
        def _(dve):
            n = [0]

            def step(ins):
                n[0] += 1
                ins.then_inc(v, 1)
                dve.wait_ge(v, n[0])

            def wide(v2):
                return v2[:, :].rearrange("p (t o) -> p t o", o=1).broadcast_to([TP, NT, MX])

            dve.sem_inc(taken, GT)
            step(dve.memset(zero_seq[:, :], 0.0))
            dve.wait_ge(w_in, 32)
            with dve.Fori(0, NT // GT) as c:
                for k in range(GT):
                    dve.wait_ge(lg, c * GT + (k + 1 + GT))
                    dve.tensor_tensor(probs[:, bass.ds(c * GT + k, 1), :].rearrange("p t e -> p (t e)"), s.bank[k][0:TP, 0:MX], bg[:, :], ALU.add).then_inc(taken, 1)
            dve.wait_ge(taken, NT + GT)
            step(dve.tensor_reduce(red[:, :], probs[:, :, :], AX.X, ALU.max))
            step(dve.tensor_copy(spread[:, :, :], wide(red)))
            step(dve.tensor_tensor(probs[:, :, :], probs[:, :, :], spread[:, :, :], ALU.subtract))
            marks["shifted"] = n[0]
            dve.wait_ge(e_done, 1)
            step(dve.tensor_reduce(red[:, :], probs[:, :, :], AX.X, ALU.add))
            step(dve.reciprocal(best[:, :], red[:, :]))
            step(dve.tensor_copy(spread[:, :, :], wide(best)))
            step(dve.tensor_tensor(probs[:, :, :], probs[:, :, :], spread[:, :, :], ALU.mult))
            for t in range(NT):
                step(dve.max(top[:, t, :], probs[:, t, :]))
                step(dve.max_index(top_i[:, t, :], top[:, t, :], probs[:, t, :]))
            step(dve.tensor_copy(best[:, :], top_i[:, :, 0]))
            for t in range(NT):
                step(dve.tensor_scalar(hot[:, t, :], s.iota_row[0:TP, 0:MX], best[:, t:t + 1], None, ALU.is_equal))
            marks["hot"] = n[0]
            dve.wait_ge(p, 1)
            step(dve.tensor_copy(count[:, :, :], s.bank[6][0:TP, 0:NT * MX].rearrange("p (t e) -> p t e", e=MX)))
            for e in range(MX):
                step(dve.tensor_tensor_scan(before[:, :, e], zero_seq[:, :], count[:, :, e], 0.0, ALU.add, ALU.add))
            step(dve.tensor_tensor(before[:, :, :], before[:, :, :], count[:, :, :], ALU.subtract))
            step(dve.tensor_tensor(before[:, :, :], before[:, :, :], s.bank[5][0:TP, 0:NT * MX].rearrange("p (t e) -> p t e", e=MX), ALU.add))
            step(dve.tensor_tensor(before[:, :, :], before[:, :, :], hot[:, :, :], ALU.mult))
            step(dve.tensor_reduce(pos[:, :], before[:, :, :], AX.X, ALU.add))
            step(dve.tensor_scalar(kept[:, :], pos[:, :], float(CAP), None, ALU.is_le))
            step(dve.tensor_tensor(keep[:, :], kept[:, :], top[:, :, 0], ALU.mult))
            step(dve.tensor_scalar(far[:, :], kept[:, :], -FAR, FAR, ALU.mult, ALU.add))
            step(dve.tensor_scalar(red[:, :], pos[:, :], float(CAP), 1.0, ALU.min, ALU.subtract))
            step(dve.scalar_tensor_tensor(out=red[:, :], in0=best[:, :], scalar=float(CAP), in1=red[:, :], op0=ALU.mult, op1=ALU.add))
            step(dve.tensor_copy(slot_out[:, :], red[:, :]))
            step(dve.tensor_tensor(red[:, :], red[:, :], far[:, :], ALU.add))
            step(dve.tensor_copy(slot_in[:, :], red[:, :]))

        @block.scalar
        def _(act):
            act.sem_inc(lg, GT)
            with act.Fori(0, NT // GT) as c:
                for k in range(GT):
                    act.wait_ge(lg, c * GT + k + 1)
                    act.copy(x_tile[:, k], xT[:, :, bass.ds((c * GT + k) * TP, TP)]).then_inc(staged, 1)
            act.wait_ge(v, marks["shifted"])
            act.activation(probs[:, :, :], probs[:, :, :], ACT.Exp).then_inc(e_done, 1)

        @block.tensor
        def _(pe):
            pe.wait_ge(w_in, 32)
            with pe.Fori(0, NT // GT) as c:
                for k in range(GT):
                    pe.wait_ge(staged, c * GT + k + 1)
                    pe.wait_ge(taken, c * GT + k + 1)
                    for f in range(FH):
                        i = pe.matmul(s.bank[k][0:TP, 0:MX], x_tile[:, k, f, :], wg[:, f, :], start=(f == 0), stop=(f == FH - 1))
                    i.then_inc(lg, 1)
            pe.wait_ge(made, 3)
            pe.wait_ge(v, marks["hot"])
            everyone = hot[:, :, :].rearrange("p t e -> p (t e)")
            pe.matmul(s.bank[5][0:TP, 0:NT * MX], upto[:, :], everyone, start=True, stop=True)
            pe.matmul(s.bank[6][0:TP, 0:NT * MX], ones[:, :], everyone, start=True, stop=True).then_inc(p, 1)


def phase_dispatch(nc, s, buf_dram, slot_in):
    with ExitStack() as ctx:
        xn = ctx.enter_context(nc.sbuf_tensor("xn", [TP, NT, D], F32))
        normed, sent = s.sem("i_normed"), s.sem("i_sent")
        block = ctx.enter_context(nc.Block())

        @block.vector
        def _(dve):
            for t in range(NT):
                dve.tensor_scalar(xn[:, t, :], s.x[:, t, :], s.mv[:, t, 0:1], s.rstd[:, t:t + 1], ALU.subtract, ALU.mult).then_inc(normed, 1)

        @block.gpsimd
        def _(pool):
            for t in range(NT):
                pool.wait_ge(normed, t + 1)
                pool.indirect_dma_start(out=buf_dram, out_offset=bass.IndirectOffsetOnAxis(ap=slot_in[:, t:t + 1], axis=0), in_=xn[:, t, :],
                                        in_offset=None, bounds_check=MX * CAP - 1, oob_is_err=False).then_inc(sent, 16)
            pool.wait_ge(sent, 16 * NT)


def load_weights(sp, a, weights, e, k):
    w1, w2, _, _, e_in, _ = weights
    one = bass.ds(e, 1)
    sp.dma_start(w1[:, k], a["L1_ffn_w1"][one].rearrange("o (f p) n -> p (o f) n", p=P)).then_inc(e_in[k], 16)
    sp.dma_start(w2[:, k], a["L1_ffn_w2"][one].rearrange("o (j p) n -> p (o j) n", p=P)).then_inc(e_in[k], 16)


def phase_switch_experts(nc, s, a, buf_dram, y_dram, weights):
    HM, RT = MF // P, -(-CAP // P)
    WHOLE = CAP // P
    REST = CAP - WHOLE * P
    with ExitStack() as ctx:
        def sb(name, shape, dt=F32):
            return ctx.enter_context(nc.sbuf_tensor("x_" + name, shape, dt))
        w1, w2, b1, b2, e_in, b_in = weights
        rows, rowsT = sb("rows", [P, 2, RT, D]), sb("rowsT", [P, 2, FH, CAP])
        hid, y = sb("hid", [P, 2, HM, CAP]), sb("y", [P, 2, RT, D])
        turned, te, hm, he, ym, ye = (s.sem("x_" + n) for n in ("turned", "te", "hm", "he", "ym", "ye"))
        stored = [s.sem(f"x_stored{k}") for k in range(2)]
        block = ctx.enter_context(nc.Block())
        PAIRS = MX // 2

        def size(r):
            return P if r < WHOLE else REST

        @block.sync
        def _(sp):
            def load_rows(e, k):
                sp.dma_start(rows[:, k, 0:WHOLE, :], buf_dram[bass.ds(e * CAP, WHOLE * P), :].rearrange("(r p) f -> p r f", p=P)).then_inc(e_in[k], 16)
                sp.dma_start(rows[0:REST, k, WHOLE, :], buf_dram[bass.ds(e * CAP + WHOLE * P, REST), :]).then_inc(e_in[k], 16)

            def store(e, k):
                sp.wait_ge(ye, e * RT + (RT + 2))
                sp.dma_start(y_dram[bass.ds(e * CAP, WHOLE * P), :].rearrange("(r p) f -> p r f", p=P), y[:, k, 0:WHOLE, :]).then_inc(stored[k], 16)
                sp.dma_start(y_dram[bass.ds(e * CAP + WHOLE * P, REST), :], y[0:REST, k, WHOLE, :]).then_inc(stored[k], 16)

            load_rows(0, 0)
            load_rows(1, 1)
            with sp.Fori(0, PAIRS - 1) as j:
                for k in range(2):
                    sp.wait_ge(ym, (j * 2 + k) * RT + RT)
                    load_weights(sp, a, weights, j * 2 + (k + 2), k)
                    load_rows(j * 2 + (k + 2), k)
                    store(j * 2 + k, k)
            store(MX - 2, 0)
            store(MX - 1, 1)
            for k in range(2):
                sp.wait_ge(stored[k], 32 * PAIRS)

        @block.tensor
        def _(pe):
            def hidden(e, k, j):
                wait_own(pe, s, e_in[k], j * 64 + 64)
                for r in range(RT):
                    pe.wait_ge(te, e * RT + r + 1)
                    for f in range(FH):
                        i = pe.transpose(s.bank[6 + r % 2][:, f * P:f * P + size(r)], rows[0:size(r), k, r, f * P:(f + 1) * P], s.ident[0:size(r), 0:size(r)])
                    i.then_inc(turned, 1)
                wait_own(pe, s, te, e * RT + (RT + 2))
                for m in range(HM):
                    pe.wait_ge(he, e * HM + m + 1)
                    for f in range(FH):
                        i = pe.matmul(s.bank[m % 4][:, 0:CAP], w1[:, k, f, m * P:(m + 1) * P], rowsT[:, k, f, :], start=(f == 0), stop=(f == FH - 1))
                    i.then_inc(hm, 1)

            def output(e, k):
                wait_own(pe, s, he, e * HM + (HM + 4))
                for r in range(RT):
                    pe.wait_ge(ye, e * RT + r + 1)
                    for m in range(HM):
                        i = pe.matmul(s.bank[4 + r % 2][0:size(r), 0:D], hid[:, k, m, r * P:r * P + size(r)], w2[:, k, m, :], start=(m == 0), stop=(m == HM - 1))
                    i.then_inc(ym, 1)

            hidden(0, 0, 0)
            with pe.Fori(0, PAIRS - 1) as j:
                hidden(j * 2 + 1, 1, j)
                output(j * 2, 0)
                hidden(j * 2 + 2, 0, j + 1)
                output(j * 2 + 1, 1)
            hidden(MX - 1, 1, PAIRS - 1)
            output(MX - 2, 0)
            output(MX - 1, 1)

        @block.scalar
        def _(act):
            act.sem_inc(te, 2)
            act.sem_inc(he, 4)
            act.wait_ge(b_in, 32)
            with act.Fori(0, PAIRS) as j:
                for k in range(2):
                    e = j * 2 + k
                    for r in range(RT):
                        act.wait_ge(turned, e * RT + r + 1)
                        act.copy(rowsT[:, k, :, r * P:r * P + size(r)], s.bank[6 + r % 2][:, 0:FH * P].rearrange("p (f n) -> p f n", f=FH)[:, :, 0:size(r)]).then_inc(te, 1)
                    for m in range(HM):
                        act.wait_ge(hm, e * HM + m + 1)
                        act.activation(hid[:, k, m, :], s.bank[m % 4][:, 0:CAP], ACT.Relu, bias=b1[:, bass.ds(e * HM + m, 1)]).then_inc(he, 1)

        @block.vector
        def _(dve):
            dve.sem_inc(ye, 2)
            dve.wait_ge(b_in, 32)

            def add_bias(j, first):
                for k in range(2):
                    e = j * 2 + k
                    if not first:
                        wait_own(dve, s, stored[k], j * 32)
                    for r in range(RT):
                        dve.wait_ge(ym, e * RT + r + 1)
                        dve.tensor_tensor(y[0:size(r), k, r, :], s.bank[4 + r % 2][0:size(r), 0:D], b2[0:size(r), bass.ds(e, 1), :].rearrange("p o n -> p (o n)"), ALU.add).then_inc(ye, 1)

            add_bias(0, True)
            with dve.Fori(1, PAIRS) as j:
                add_bias(j, False)


def phase_combine(nc, s, y_dram, slot_out, keep, out):
    with ExitStack() as ctx:
        def sb(name, shape):
            return ctx.enter_context(nc.sbuf_tensor("o_" + name, shape, F32))
        rows = sb("rows", [TP, NT, D])
        number, mask_hi, mask_lo = (sb(n, [TP, GT, D]) for n in ("number", "mask_hi", "mask_lo"))
        hi, lo = sb("hi", [TP, GT, D]), sb("lo", [TP, GT, D])
        row_in = [s.sem(f"o_row_in{c}") for c in range(NT // GT)]
        v, added, stored = s.sem("o_v"), s.sem("o_added"), s.sem("o_stored")
        block = ctx.enter_context(nc.Block())
        out_rows = out.rearrange("(t p) f -> p t f", p=TP)
        FMAX = 3.4028234663852886e38

        @block.gpsimd
        def _(pool):
            for t in range(NT):
                pool.indirect_dma_start(out=rows[:, t, :], out_offset=None, in_=y_dram,
                                        in_offset=bass.IndirectOffsetOnAxis(ap=slot_out[:, t:t + 1], axis=0)).then_inc(row_in[t // GT], 16)

        @block.vector
        def _(dve):
            n = [0]

            def step(ins):
                n[0] += 1
                ins.then_inc(v, 1)
                dve.wait_ge(v, n[0])

            step(dve.memset(hi[:, :, :], 10000.0))
            step(dve.memset(lo[:, :, :], -10000.0))
            for c in range(NT // GT):
                group = slice(c * GT, (c + 1) * GT)
                y = rows[:, group, :]
                dve.wait_ge(row_in[c], 16 * GT)
                for k in range(GT):
                    step(dve.tensor_scalar(rows[:, c * GT + k, :], rows[:, c * GT + k, :], keep[:, c * GT + k:c * GT + k + 1], None, ALU.mult))
                step(dve.tensor_scalar(number[:, :, :], y, 0.0, None, ALU.max))
                step(dve.scalar_tensor_tensor(out=number[:, :, :], in0=y, scalar=0.0, in1=number[:, :, :], op0=ALU.min, op1=ALU.add))
                step(dve.tensor_scalar(mask_hi[:, :, :], number[:, :, :], FMAX, None, ALU.is_gt))
                step(dve.tensor_scalar(mask_lo[:, :, :], number[:, :, :], -FMAX, None, ALU.is_lt))
                step(dve.copy_predicated(number[:, :, :], mask_hi[:, :, :].bitcast(I32), hi[:, :, :]))
                step(dve.copy_predicated(number[:, :, :], mask_lo[:, :, :].bitcast(I32), lo[:, :, :]))
                dve.tensor_tensor(s.x[:, group, :], s.x[:, group, :], number[:, :, :], ALU.add).then_inc(added, 1)

        @block.sync
        def _(sp):
            for c in range(NT // GT):
                sp.wait_ge(added, c + 1)
                sp.dma_start(out_rows[:, c * GT:(c + 1) * GT, :], s.x[:, c * GT:(c + 1) * GT, :]).then_inc(stored, 16)
            sp.wait_ge(stored, 16 * (NT // GT))


def phase_switch(nc, s, a, out):
    buf_dram = nc.dram_tensor("buf_dram", [BUF, D], F32, kind="Internal").ap()
    y_dram = nc.dram_tensor("y_dram", [MX * CAP, D], F32, kind="Internal").ap()
    with ExitStack() as ctx:
        slot_in = ctx.enter_context(nc.sbuf_tensor("slot_in", [TP, NT], I32))
        slot_out = ctx.enter_context(nc.sbuf_tensor("slot_out", [TP, NT], I32))
        keep = ctx.enter_context(nc.sbuf_tensor("keep", [TP, NT], F32))
        with ExitStack() as w_ctx:
            def sb(name, shape):
                return w_ctx.enter_context(nc.sbuf_tensor("x_" + name, shape, F32))
            w1, w2 = sb("w1", [P, 2, FH, MF]), sb("w2", [P, 2, MF // P, D])
            b1, b2 = sb("b1", [P, MX * (MF // P)]), sb("b2", [P, MX, D])
            weights = w1, w2, b1, b2, [s.sem(f"x_in{k}") for k in range(2)], s.sem("x_b_in")

            def load(sp):
                for e in range(2):
                    load_weights(sp, a, weights, e, e)
                sp.dma_start(b1[:, :], a["moe_b1_cols"]).then_inc(weights[5], 16)
                sp.dma_start(b2[:, :, :], a["L1_ffn_b2"].rearrange("(o e) n -> o e n", o=1).broadcast_to([P, MX, D])).then_inc(weights[5], 16)

            phase_switch_route(nc, s, a, buf_dram, slot_in, slot_out, keep, load)
            phase_dispatch(nc, s, buf_dram, slot_in)
            phase_switch_experts(nc, s, a, buf_dram, y_dram, weights)
        phase_combine(nc, s, y_dram, slot_out, keep, out)


def build(nc, a, out, stop="0123"):
    m_dram = nc.dram_tensor("m_dram", [N, D], F32, kind="Internal").ap()
    with ExitStack() as ctx:
        s = open_shared(nc, ctx, a)
        phase_edges(nc, s, a)
        if "0" in stop:
            phase_gated_gnn(nc, s, a, m_dram)
            end_stage(nc, s)
        if "1" in stop:
            phase_ffn0(nc, s, a)
            end_stage(nc, s)
        if "2" in stop:
            phase_attention(nc, s, a)
            end_stage(nc, s)
        if "3" in stop:
            phase_switch(nc, s, a, out)
            return
        stored = s.sem("stored")
        with nc.Block() as block:
            @block.sync
            def _(sp):
                sp.dma_start(out.rearrange("(t p) f -> p t f", p=TP), s.x[:, :, :]).then_inc(stored, 16)
                sp.wait_ge(stored, 16)


_INS = ["x", "src", "dst", "edge_type_8", "edge_weight", "node_type_4", "L0_gnn_weight", "w_ihT", "w_hhT", "b_ih_cols", "b_hh_cols",
        "L0_ffn_router_w1", "router_b1_cols", "L0_ffn_router_w2", "L0_ffn_router_b2", "L0_ffn_expert_w1", "expert_b1_cols", "L0_ffn_expert_w2",
        "expert_b2_cols", "L0_ffn_expert_w3", "L0_ffn_expert_b3",
        "L1_gnn_k_linears", "L1_gnn_q_linears", "L1_gnn_v_linears", "L1_gnn_a_linears", "rel_attT", "L1_gnn_relation_msg", "priT", "L1_gnn_skip",
        "L1_ffn_gate_w", "L1_ffn_gate_b", "L1_ffn_w1", "moe_b1_cols", "L1_ffn_w2", "L1_ffn_b2"]
_OUTS = [((3125, 256), "float32")]


def kernel(**inputs):
    import numpy as _np
    import concourse.bacc as _bacc
    from concourse import mybir as _mybir
    from concourse.bass_utils import run_bass_kernel_spmd as _run

    inputs["w_ihT"] = _np.asarray(inputs["L0_gnn_w_ih"]).T
    inputs["w_hhT"] = _np.asarray(inputs["L0_gnn_w_hh"]).T
    for name in ("router_b1", "expert_b1", "expert_b2"):
        inputs[f"{name}_cols"] = _np.asarray(inputs[f"L0_ffn_{name}"]).reshape(-1, P).T
    inputs["rel_attT"] = _np.asarray(inputs["L1_gnn_relation_att"]).transpose(0, 1, 3, 2)
    inputs["priT"] = _np.asarray(inputs["L1_gnn_relation_pri"]).T
    inputs["moe_b1_cols"] = _np.asarray(inputs["L1_ffn_b1"]).reshape(-1, P).T
    for side in ("ih", "hh"):
        inputs[f"b_{side}_cols"] = _np.asarray(inputs[f"L0_gnn_b_{side}"]).reshape(-1, P).T
    nc = _bacc.Bacc("TRN2", target_bir_lowering=False, num_devices=1)
    arrays, args = {}, {}
    for name in _INS:
        v = _np.ascontiguousarray(inputs[name])
        arrays[f"in_{name}_dram"] = v
        args[name] = nc.dram_tensor(f"in_{name}_dram", v.shape, _mybir.dt.from_np(v.dtype), kind="ExternalInput").ap()
    out = nc.dram_tensor("out_0_dram", _OUTS[0][0], _mybir.dt.from_np(_np.dtype(_OUTS[0][1])), kind="ExternalOutput").ap()
    build(nc, args, out)
    r = _run(nc, [arrays], core_ids=[0])
    return r.results[0]["out_0_dram"]
```

```python
from contextlib import ExitStack

import concourse.bass as bass
from concourse import mybir

ALU = mybir.AluOpType
ACT = mybir.ActivationFunctionType
AX = mybir.AxisListType
F32 = mybir.dt.float32
I32 = mybir.dt.int32
U32 = mybir.dt.uint32

N, D, E = 3125, 256, 53125
TP, NT, GT = 125, 25, 5
P = 128
FH = D // P
ET = -(-E // P)
EC = -(-ET // P)
NPAD = 3200
RING = 16
EIT = ET // RING
BL = 8
DVE, SP = mybir.EngineType.DVE, mybir.EngineType.SP
HR = RING // 2
PSR = 4
PAD_DST = 4000
WIN_MAX = N - P
LAYERS = 5
RELS, TYPES, HEADS, DK = 8, 4, 4, 64
NG, GN = NT // GT, GT * TP
CUTS = (-(-GN // 2), GN // 2)
GATES = 6
GHC = -(-N // EIT)
NR = GHC * EIT
assert ET == EIT * RING and NR <= NPAD and NT == NG * GT
EPS = 1e-5
BIG = 1e38


def wait_own(eng, s, sem, value):
    eng.wait_ge(sem, value)
    eng.sem_inc(s.passed, 1)


def load_bases(nc, eng_type, s, at, count):
    _, values = nc.values_load_multi_w_load_instructions(s.base[0:1, bass.ds(at, count)], engines=(eng_type,), min_val=0, max_val=WIN_MAX,
                                                         skip_runtime_bounds_check_because="phase_edges clips the bases")
    return values


class Shared:
    pass


def open_shared(nc, ctx, a):
    s = Shared()
    s.sb = lambda name, shape, dt=F32: ctx.enter_context(nc.sbuf_tensor(name, shape, dt))
    s.open_sems = []

    def sem(name):
        s.open_sems.append(nc.alloc_semaphore(name=name))
        return s.open_sems[-1]

    s.sem = sem
    s.passed = nc.alloc_semaphore(name="passed")
    s.x = s.sb("x", [TP, NT, D])
    s.ident = s.sb("ident", [P, P])
    s.iota_row = s.sb("iota_row", [P, P])
    s.first_row = s.sb("first_row", [P, P])
    s.dst_by_tile = s.sb("dst_by_tile", [P, EC, P])
    s.src_idx = s.sb("src_idx", [P, EC * P], I32)
    s.rel_idx = s.sb("rel_idx", [P, EC * P], I32)
    s.dst_rel = s.sb("dst_rel", [P, EC * P])
    s.weight = s.sb("weight", [P, EC * P])
    s.base = s.sb("base", [P, EC * P], I32)
    s.stats = s.sb("stats", [TP, NT, 6])
    s.mv = s.sb("mv", [TP, NT, 2])
    s.rstd = s.sb("rstd", [TP, NT])
    s.is_type = s.sb("is_type", [TP, NT, TYPES])
    s.skip_type = s.sb("skip_type", [TP, NT, TYPES])
    s.eps = s.sb("eps", [P, 1])
    s.zero = s.sb("zero", [P, 1])
    s.bank = [ctx.enter_context(nc.psum_tensor(f"bank{i}", [P, 512], F32)) for i in range(8)]
    return s


def end_stage(nc, s):
    nc.all_engine_barrier()
    nc.clear_and_free_semaphores(s.open_sems)
    nc.all_engine_barrier()
    s.open_sems = []


def phase_edges(nc, s, a):
    with ExitStack() as ctx:
        def sb(name, shape, dt=F32):
            return ctx.enter_context(nc.sbuf_tensor(name, shape, dt))
        raw_i = sb("raw_i", [P, 3, EC, P], I32)
        raw_f = sb("raw_f", [P, 4, EC, P])
        dst_e = sb("dst_e", [P, EC * P])
        base_f = sb("base_f", [P, EC * P])
        type_i, type_f = sb("type_i", [NT, TP], I32), sb("type_f", [NT, TP])
        typ, skip = sb("typ", [TP, NT]), sb("skip", [TP, TYPES])
        types_in, types_v, types_p, skipped = s.sem("e_types_in"), s.sem("e_types_v"), s.sem("e_types_p"), s.sem("e_skipped")
        cleared, loaded, converted = s.sem("e_cleared"), s.sem("e_loaded"), s.sem("e_converted")
        made, turned, copied, x_in = s.sem("e_made"), s.sem("e_turned"), s.sem("e_copied"), s.sem("x_in")
        full = ET - 1 - (EC - 1) * P
        rest = E - (ET - 1) * P
        block = ctx.enter_context(nc.Block())

        @block.sync
        def _(sp):
            sp.dma_start(s.x[:, :, :], a["x"].rearrange("(t p) f -> p t f", p=TP)).then_inc(x_in, 16)
            sp.wait_ge(cleared, 4)
            n = 0
            for k, name in enumerate(("src", "dst", "edge_type_8", "edge_weight")):
                to = raw_f[:, 3] if k == 3 else raw_i[:, k]
                for c in range(EC):
                    rows = P if c < EC - 1 else full
                    at = c * P * P
                    sp.dma_start(to[0:rows, c, :], a[name][at:at + rows * P].rearrange("(i p) -> i p", p=P)).then_inc(loaded, 16)
                    n += 16
                sp.dma_start(to[full:full + 1, EC - 1, 0:rest], a[name][(ET - 1) * P:E].rearrange("(i p) -> i p", i=1)).then_inc(loaded, 16)
                n += 16
            sp.dma_start(type_i[:, :], a["node_type_4"].rearrange("(t p) -> t p", p=TP)).then_inc(types_in, 16)
            sp.dma_start(skip[:, :], a["L1_gnn_skip"].rearrange("(o t) -> o t", o=1).broadcast_to([TP, TYPES])).then_inc(types_in, 16)
            sp.wait_ge(loaded, n)
            sp.wait_ge(types_in, 32)
            sp.wait_ge(x_in, 16)

        @block.scalar
        def _(act):
            act.wait_ge(types_in, 32)
            act.activation(skip[:, :], skip[:, :], ACT.Sigmoid).then_inc(skipped, 1)

        @block.gpsimd
        def _(pool):
            pool.memset(s.ident[:, :], 0.0).then_inc(made, 1)
            pool.memset(s.first_row[:, :], 0.0).then_inc(made, 1)
            pool.iota(s.iota_row[:, :], pattern=[[1, P]], base=0, channel_multiplier=0,
                      allow_small_or_imprecise_dtypes=True).then_inc(made, 1)
            pool.wait_ge(made, 3)
            pool.affine_select(out=s.ident[:, :], in_=s.ident[:, :], compare_op=ALU.not_equal, fill=1.0, base=0,
                               pattern=[[-1, P]], channel_multiplier=1).then_inc(made, 1)
            pool.affine_select(out=s.first_row[:, :], in_=s.first_row[:, :], compare_op=ALU.not_equal, fill=1.0, base=0,
                               pattern=[[0, P]], channel_multiplier=1).then_inc(made, 1)

        @block.vector
        def _(dve):
            for k, fill in ((0, 0), (1, PAD_DST), (2, 0)):
                dve.memset(raw_i[:, k, EC - 1, :], fill).then_inc(cleared, 1)
            dve.memset(raw_f[:, 3, EC - 1, :], 0.0).then_inc(cleared, 1)
            dve.memset(s.eps[:, :], EPS).then_inc(cleared, 1)
            dve.memset(s.zero[:, :], 0.0).then_inc(cleared, 1)
            dve.wait_ge(loaded, 16 * 4 * (EC + 1))
            dve.tensor_copy(raw_f[:, 0], raw_i[:, 0]).then_inc(converted, 1)
            dve.tensor_copy(raw_f[:, 1], raw_i[:, 1]).then_inc(converted, 1)
            dve.tensor_copy(s.dst_by_tile[:, :, :], raw_i[:, 1]).then_inc(converted, 1)
            dve.wait_ge(converted, 1)
            dve.scalar_tensor_tensor(out=raw_f[:, 2], in0=raw_i[:, 2], scalar=float(NR), in1=raw_f[:, 0],
                                     op0=ALU.mult, op1=ALU.add).then_inc(converted, 1)
            for k, to in ((0, s.src_idx), (1, dst_e), (2, s.rel_idx), (3, s.weight)):
                dve.wait_ge(turned, k + 1)
                dve.tensor_copy(to[:, :], s.bank[k][:, :]).then_inc(copied, 1)
            dve.wait_ge(types_in, 32)
            dve.tensor_copy(type_f[:, :], type_i[:, :]).then_inc(types_v, 1)
            dve.wait_ge(turned, 5)
            dve.tensor_scalar(base_f[:, :], s.bank[4][:, :], float(WIN_MAX), None, ALU.min).then_inc(copied, 1)
            dve.wait_ge(copied, 5)
            dve.tensor_copy(s.base[:, :], base_f[:, :]).then_inc(copied, 1)
            dve.tensor_tensor(s.dst_rel[:, :], dst_e[:, :], base_f[:, :], ALU.subtract).then_inc(copied, 1)
            dve.wait_ge(types_p, 1)
            dve.tensor_copy(typ[:, :], s.bank[5][0:TP, 0:NT]).then_inc(types_v, 1)
            dve.wait_ge(types_v, 2)
            dve.wait_ge(skipped, 1)
            for t in range(TYPES):
                dve.tensor_scalar(s.is_type[:, :, t], typ[:, :], float(t), None, ALU.is_equal).then_inc(types_v, 1)
                dve.tensor_scalar(s.skip_type[:, :, t], typ[:, :], float(t), skip[:, t:t + 1], ALU.is_equal, ALU.mult).then_inc(types_v, 1)

        @block.tensor
        def _(pe):
            pe.wait_ge(made, 5)
            pe.wait_ge(converted, 4)
            for k in range(4):
                for c in range(EC):
                    mm = pe.transpose(s.bank[k][:, c * P:(c + 1) * P], raw_f[:, k, c, :], s.ident[:, :])
                mm.then_inc(turned, 1)
            pe.wait_ge(copied, 2)
            pe.matmul(s.bank[4][:, :], s.first_row[:, :], dst_e[:, :], start=True, stop=True).then_inc(turned, 1)
            pe.wait_ge(types_v, 1)
            pe.transpose(s.bank[5][0:TP, 0:NT], type_f[:, :], s.ident[0:NT, 0:NT]).then_inc(types_p, 1)


def phase_norm_to_T(nc, s, hT, tag, load=None, keep=None):
    with ExitStack() as ctx:
        slots = 2 * GT if keep else GT
        xn = ctx.enter_context(nc.sbuf_tensor(tag + "_xn", [TP, slots, D], F32))
        std = ctx.enter_context(nc.sbuf_tensor(tag + "_std", [TP, NT], F32))
        done, root, inverse = s.sem(tag + "_stats"), s.sem(tag + "_root"), s.sem(tag + "_inverse")
        clear, normed, turned, copied = s.sem(tag + "_clear"), s.sem(tag + "_normed"), s.sem(tag + "_turned"), s.sem(tag + "_copied")
        kept = [s.sem(f"{tag}_kept{n}") for n in range(2)] if keep else None
        block = ctx.enter_context(nc.Block())
        if load:
            @block.sync
            def _(sp):
                load(sp)
                if keep:
                    kept_rows, all_kept = keep
                    for c in range(NG):
                        at = c % 2 * GT
                        sp.wait_ge(normed, (c + 1) * GT)
                        sp.dma_start(kept_rows[c * GN:(c + 1) * GN, :].rearrange("(k p) n -> p k n", p=TP), xn[:, at:at + GT, :]).then_inc(kept[c % 2], 16)
                    sp.wait_ge(kept[0], 16 * ((NG + 1) // 2))
                    sp.wait_ge(kept[1], 16 * (NG // 2))
                    sp.sem_inc(all_kept, 1)

        @block.vector
        def _(dve):
            dve.memset(hT[:, :, N:], 0.0).then_inc(clear, 1)
            dve.sem_inc(turned, GT)

            def measure(c):
                for t in range(c * GT, (c + 1) * GT):
                    dve.bn_stats(s.stats[:, t, :], s.x[:, t, :]).then_inc(done, 1)
                for k, t in enumerate(range(c * GT, (c + 1) * GT)):
                    dve.wait_ge(done, c * 2 * GT + k + 1)
                    dve.bn_aggr(s.mv[:, t, :], s.stats[:, t, :]).then_inc(done, 1)

            measure(0)
            for c in range(NG):
                group = slice(c * GT, (c + 1) * GT)
                if c + 1 < NG:
                    measure(c + 1)
                dve.wait_ge(root, c + 1)
                dve.reciprocal(s.rstd[:, group], std[:, group]).then_inc(inverse, 1)
                dve.wait_ge(inverse, c + 1)
                if keep and c >= 2:
                    dve.wait_ge(kept[c % 2], c // 2 * 16)
                for k in range(GT):
                    t = c * GT + k
                    dve.wait_ge(turned, t + 1)
                    dve.tensor_scalar(xn[:, t % slots, :], s.x[:, t, :], s.mv[:, t, 0:1], s.rstd[:, t:t + 1], ALU.subtract, ALU.mult).then_inc(normed, 1)

        @block.tensor
        def _(pe):
            for t in range(NT):
                k = t % GT
                pe.wait_ge(normed, t + 1)
                pe.wait_ge(copied, t + 1)
                for f in range(FH):
                    mm = pe.transpose(s.bank[k][:, f * TP:(f + 1) * TP], xn[:, t % slots, f * P:(f + 1) * P], s.ident[0:TP, 0:TP])
                mm.then_inc(turned, 1)

        @block.scalar
        def _(act):
            act.sem_inc(copied, GT)

            def deviation(c):
                group = slice(c * GT, (c + 1) * GT)
                act.wait_ge(done, (c + 1) * 2 * GT)
                act.activation(std[:, group], s.mv[:, group, 1], ACT.Sqrt, bias=s.eps[0:TP, :]).then_inc(root, 1)

            deviation(0)
            for c in range(NG):
                if c + 1 < NG:
                    deviation(c + 1)
                for k in range(GT):
                    t = c * GT + k
                    act.wait_ge(turned, t + 1 + GT)
                    act.copy(hT[:, :, t * TP:(t + 1) * TP], s.bank[k][:, 0:FH * TP].rearrange("p (f n) -> p f n", f=FH)).then_inc(copied, 1)


def phase_gated_gnn(nc, s, a, h_dram):
    with ExitStack() as ctx:
        def sb(name, shape, dt=F32):
            return ctx.enter_context(nc.sbuf_tensor(name, shape, dt))
        hT = sb("hT", [P, FH, NPAD])
        w_msgT = sb("w_msgT", [P, FH, D])
        w_in_side = sb("w_in_side", [P, FH, 3 * D])
        w_ih = sb("w_ih", [P, FH, 3 * D])
        w_hh = sb("w_hh", [P, FH, 3 * D])
        b_ih = sb("b_ih", [P, GATES])
        b_hh = sb("b_hh", [P, GATES])
        b_sum = sb("b_sum", [P, GATES])
        w_in, w_msg_in = s.sem("g_w_in"), s.sem("g_w_msg_in")

        def load(sp):
            sp.dma_start(w_msgT[:, :, :], a["w_msgT"][0].rearrange("(f p) n -> p f n", p=P)).then_inc(w_msg_in, 16)
            sp.dma_start(w_ih[:, :, :], a["w_ihT"].rearrange("(f p) g -> p f g", p=P)).then_inc(w_in, 16)
            sp.dma_start(w_hh[:, :, :], a["w_hhT"].rearrange("(f p) g -> p f g", p=P)).then_inc(w_in, 16)
            sp.dma_start(b_ih[:, :], a["b_ih_cols"]).then_inc(w_in, 16)
            sp.dma_start(b_hh[:, :], a["b_hh_cols"]).then_inc(w_in, 16)

        h_ready = s.sem("g_h_ready")
        phase_norm_to_T(nc, s, hT, "n0", load, (h_dram, h_ready))

        aggT = sb("aggT", [P, FH, NPAD])
        gh = sb("gh", [P, GATES, GHC * EIT])
        h_group = sb("h_group", [P, FH, GN])
        rows = sb("rows", [P, RING, D])
        h_out = rows[0:TP, 0:GT, :]
        idx = sb("idx", [P, RING], I32)
        sel = sb("sel", [P, PSR, P])

        b_ready = s.sem("g_b_ready")
        side_mm, side_left = s.sem("g_side_mm"), s.sem("g_side_left")
        staged, tile_done, tile_left = s.sem("g_staged"), s.sem("g_tile_done"), s.sem("g_tile_left")
        h_stored, h_out_free = s.sem("g_h_stored"), s.sem("g_h_out_free")
        row_in = [s.sem(f"g_row_in{k}") for k in range(RING)]
        idx_ready = s.sem("g_idx_ready")
        sel_ready, mm_done, added = s.sem("g_sel_ready"), s.sem("g_mm_done"), s.sem("g_added")
        gh_mm, gh_copied = s.sem("g_gh_mm"), s.sem("g_gh_copied")
        gi_done, gate_act, gate_dve, cleared = s.sem("g_gi_done"), s.sem("g_gate_act"), s.sem("g_gate_dve"), s.sem("g_cleared")
        SIDE = 3 * D // 2
        OPS = 14
        t_banks = s.bank[6:8]
        PAIRS = ((0, 2), (2, 2), (4, 1))
        TB = len(PAIRS)
        block = ctx.enter_context(nc.Block())

        def cut_columns(c, cut):
            return bass.ds(c * GN + cut * CUTS[0], CUTS[cut])

        @block.sync
        def _(sp):
            def store_group(group, c):
                sp.wait_ge(tile_left, group * TB + (TB + 1))
                sp.dma_start(h_dram[bass.ds(c * GN, GN), :].rearrange("(k p) n -> p k n", p=TP), h_out[:, :, :]).then_inc(h_stored, 16)
                sp.wait_ge(h_stored, group * 16 + 16)
                sp.sem_inc(h_out_free, 1)

            with sp.Fori(0, LAYERS - 1) as l:
                wait_own(sp, s, side_mm, l * 4 + 4)
                sp.dma_start(w_msgT[:, :, :], a["w_msgT"][bass.ds(l + 1, 1)].rearrange("l (f p) n -> p (l f) n", p=P)).then_inc(w_msg_in, 16)
                with sp.Fori(0, NG) as c:
                    store_group(l * NG + c, c)
                sp.sem_inc(h_ready, 1)

        @block.gpsimd
        def _(pool):
            with pool.Fori(0, LAYERS) as l:
                wait_own(pool, s, h_ready, l + 1)
                with pool.Fori(0, EIT) as j:
                    for k in range(RING):
                        if k % HR == 0:
                            wait_own(pool, s, idx_ready, (l * EIT + j) * 2 + (k // HR + 1))
                        pool.indirect_dma_start(out=rows[:, k, :], out_offset=None, in_=h_dram,
                                                in_offset=bass.IndirectOffsetOnAxis(ap=idx[:, k:k + 1], axis=0)).then_inc(row_in[k], 16)

        @block.scalar
        def _(act):
            def stage_group(group, c):
                act.wait_ge(tile_done, group * TB + TB)
                act.copy(h_group[:, :, :], hT[:, :, bass.ds(c * GN, GN)]).then_inc(staged, 1)

            def copy_out(group):
                wait_own(act, s, h_out_free, group + 1)
                for b, (k, n) in enumerate(PAIRS):
                    act.wait_ge(tile_done, group * TB + (b + 1 + TB))
                    act.copy(h_out[:, k:k + n, :].rearrange("p t n -> p (t n)"), t_banks[b % 2][0:TP, 0:n * D]).then_inc(tile_left, 1)

            def gather(l):
                with act.Fori(0, EIT) as j:
                    for half in range(2):
                        wait_own(act, s, mm_done, l * ET + j * RING + (half + 1) * HR)
                        act.copy(idx[:, half * HR:(half + 1) * HR], s.src_idx[:, bass.ds(j * RING + half * HR, HR)]).then_inc(idx_ready, 1)
                    for half in range(2):
                        wait_own(act, s, gh_mm, (l * EIT + j) * 2 + (half + 1))
                        act.copy(gh[:, 3 * half:3 * half + 3, bass.ds(j * GHC, GHC)],
                                 s.bank[4 + half][:, 0:3 * GHC].rearrange("p (q n) -> p q n", q=3)).then_inc(gh_copied, 1)

            def gates(l, c, cut, between=None):
                q = l * (2 * NG) + c * 2 + cut
                for part in range(GATES):
                    if part == 4 and between:
                        between()
                    wait_own(act, s, gate_dve, q * OPS + (OPS + (part + 1 if part < 4 else part + 3)))
                    at = gh[:, part, cut_columns(c, cut)]
                    act.activation(at, at, ACT.Sigmoid if part < 4 else ACT.Tanh,
                                   bias=(b_sum if part < 4 else b_ih)[:, part:part + 1]).then_inc(gate_act, 1)

            def clear(c, cut):
                act.copy(aggT[:, :, cut_columns(c, cut)], s.zero[:, 0:1].unsqueeze(1).to_broadcast([P, FH, CUTS[cut]])).then_inc(cleared, 1)

            def lagging(l, c, last):
                gates(l, c + 1, 0, between=lambda: stage_group(l * NG + c, c))
                if not last:
                    copy_out(l * NG + c)
                clear(c + 1, 0)
                gates(l, c + 1, 1)
                clear(c + 1, 1)

            def layer(l, last):
                gather(l)
                for cut in range(2):
                    gates(l, 0, cut)
                    clear(0, cut)
                with act.Fori(0, NG - 1) as c:
                    lagging(l, c, last)
                act.wait_ge(gate_dve, (l + 1) * (2 * NG * OPS) + OPS)
                stage_group(l * NG + (NG - 1), NG - 1)
                if not last:
                    copy_out(l * NG + (NG - 1))

            act.sem_inc(tile_done, TB)
            act.sem_inc(h_out_free, 1)
            act.wait_ge(w_in, 16 * 4)
            act.wait_ge(b_ready, 1)
            with act.Fori(0, LAYERS - 1) as l:
                layer(l, False)
            layer(LAYERS - 1, True)

        @block.vector
        def _(dve):
            def select(i, k):
                dve.tensor_scalar(sel[:, k % PSR, :], s.iota_row[:, :], s.dst_rel[:, bass.ds(i + k, 1)],
                                  s.weight[:, bass.ds(i + k, 1)], ALU.is_equal, ALU.mult).then_inc(sel_ready, 1)

            def add(l, i, k, base):
                win = aggT[:, :, bass.ds(base[k], P)]
                dve.wait_ge(mm_done, l * ET + i + (k + 1 + RING))
                dve.wait_ge(added, l * ET + i + (k + PSR))
                dve.tensor_tensor(win, win, s.bank[k % PSR][:, 0:D].rearrange("p (f n) -> p f n", f=FH), ALU.add).then_inc(added, 1)

            def gather(l):
                for i in range(4):
                    dve.wait_ge(side_mm, l * 4 + (i + 1))
                    dve.tensor_copy(w_in_side[:, i // 2, i % 2 * SIDE:(i % 2 + 1) * SIDE], t_banks[i % 2][:, 0:SIDE]).then_inc(side_left, 1)
                wait_own(dve, s, cleared, l * (2 * NG) + 1)
                with dve.Fori(0, EIT) as j:
                    i = j * RING
                    base = []
                    for k in range(RING):
                        if k % BL == 0:
                            base += load_bases(nc, DVE, s, i + k, BL)
                        if k == 0:
                            dve.wait_ge(mm_done, l * ET + i + (k + 1 + RING - PSR))
                        select(i, k)
                        if k >= 2:
                            add(l, i, k - 2, base)
                    add(l, i, RING - 2, base)
                    add(l, i, RING - 1, base)

            def gru(l, c, cut):
                q = l * (2 * NG) + c * 2 + cut
                w = CUTS[cut]
                part = [gh[:, p, cut_columns(c, cut)] for p in range(GATES)]
                old = [hT[:, g, cut_columns(c, cut)] for g in range(FH)]
                for p in range(4):
                    dve.wait_ge(gi_done, q * GATES + (p + 1))
                    dve.tensor_tensor(part[p], part[p], s.bank[p][:, 0:w], ALU.add).then_inc(gate_dve, 1)
                for g in range(FH):
                    dve.wait_ge(gate_act, q * GATES + (g + 1))
                    dve.scalar_tensor_tensor(out=part[4 + g], in0=part[4 + g], scalar=b_hh[:, 4 + g:5 + g], in1=part[g],
                                             op0=ALU.add, op1=ALU.mult).then_inc(gate_dve, 1)
                for g in range(FH):
                    dve.wait_ge(gi_done, q * GATES + (g + 5))
                    dve.wait_ge(gate_dve, q * OPS + (OPS + 5 + g))
                    dve.tensor_tensor(part[4 + g], part[4 + g], s.bank[4 + g][:, 0:w], ALU.add).then_inc(gate_dve, 1)
                for g in range(FH):
                    dve.wait_ge(gate_act, q * GATES + (g + 5))
                    dve.tensor_tensor(part[g], old[g], part[4 + g], ALU.subtract).then_inc(gate_dve, 1)
                for g in range(FH):
                    dve.wait_ge(gate_dve, q * OPS + (OPS + 9 + g))
                    dve.tensor_tensor(part[g], part[g], part[2 + g], ALU.mult).then_inc(gate_dve, 1)
                for g in range(FH):
                    dve.wait_ge(gate_dve, q * OPS + (OPS + 11 + g))
                    dve.tensor_tensor(old[g], part[g], part[4 + g], ALU.add).then_inc(gate_dve, 1)

            def add_out(c):
                group = (LAYERS - 1) * NG + c
                for b, (k, n) in enumerate(PAIRS):
                    dve.wait_ge(tile_done, group * TB + (b + 1 + TB))
                    to = s.x[:, bass.ds(c * GT + k, n), :].rearrange("p t n -> p (t n)")
                    dve.tensor_tensor(to, to, t_banks[b % 2][0:TP, 0:n * D], ALU.add).then_inc(tile_left, 1)

            def layer(l, last):
                gather(l)
                wait_own(dve, s, gh_copied, (l + 1) * (2 * EIT) + 2)
                gru(l, 0, 0)
                gru(l, 0, 1)
                with dve.Fori(0, NG - 1) as c:
                    gru(l, c + 1, 0)
                    if last:
                        add_out(c)
                    gru(l, c + 1, 1)
                if last:
                    add_out(NG - 1)

            dve.sem_inc(mm_done, RING)
            dve.sem_inc(added, PSR)
            dve.sem_inc(gh_copied, 2)
            dve.sem_inc(side_left, 2)
            dve.sem_inc(gate_dve, OPS)
            dve.sem_inc(tile_left, 1)
            dve.memset(aggT[:, :, :], 0.0).then_inc(cleared, 1)
            dve.wait_ge(w_in, 16 * 4)
            dve.tensor_tensor(b_sum[:, :], b_ih[:, :], b_hh[:, :], ALU.add).then_inc(b_ready, 1)
            with dve.Fori(0, LAYERS - 1) as l:
                layer(l, False)
            layer(LAYERS - 1, True)

        @block.tensor
        def _(pe):
            def group_tiles(group):
                pe.wait_ge(staged, group + 1)
                for b, (first, n) in enumerate(PAIRS):
                    pe.wait_ge(tile_left, group * TB + max(1, b))
                    for k in range(first, first + n):
                        for f in range(FH):
                            at = (k - first) * D + f * P
                            mm = pe.transpose(t_banks[b % 2][0:TP, at:at + P], h_group[:, f, k * TP:(k + 1) * TP], s.ident[:, :])
                    mm.then_inc(tile_done, 1)

            def hidden_gates(l, j, part):
                half, at = part // 3, part % 3 * GHC
                if part % 3 == 0:
                    pe.wait_ge(gh_copied, (l * EIT + j) * 2 + (half + 1))
                for f in range(FH):
                    mm = pe.matmul(s.bank[4 + half][:, at:at + GHC], w_hh[:, f, part * P:(part + 1) * P],
                                   hT[:, f, bass.ds(j * GHC, GHC)], start=(f == 0), stop=(f == FH - 1))
                if part % 3 == 2:
                    mm.then_inc(gh_mm, 1)

            def gather(l):
                wait_own(pe, s, gate_dve, l * (2 * NG * OPS) + OPS)
                wait_own(pe, s, w_msg_in, l * 16 + 16)
                wait_own(pe, s, tile_left, l * (NG * TB) + 1)
                for i in range(4):
                    pe.wait_ge(side_left, l * 4 + (i + 1))
                    for f in range(FH):
                        mm = pe.matmul(t_banks[i % 2][:, 0:SIDE], w_msgT[:, f, i // 2 * P:(i // 2 + 1) * P],
                                       w_ih[:, f, i % 2 * SIDE:(i % 2 + 1) * SIDE], start=(f == 0), stop=(f == FH - 1))
                    mm.then_inc(side_mm, 1)
                with pe.Fori(0, EIT) as j:
                    for k in range(RING):
                        i = j * RING + k
                        pe.wait_ge(row_in[k], (l * EIT + j + 1) * 16)
                        pe.wait_ge(sel_ready, l * ET + i + 1)
                        pe.wait_ge(added, l * ET + i + 1)
                        for f in range(FH):
                            mm = pe.matmul(s.bank[k % PSR][:, f * P:(f + 1) * P], rows[:, k, f * P:(f + 1) * P], sel[:, k % PSR, :],
                                           start=True, stop=True)
                        mm.then_inc(mm_done, 1)
                        if k < GATES:
                            hidden_gates(l, j, k)

            def inputs(l, c, cut):
                q = l * (2 * NG) + c * 2 + cut
                for part in range(GATES):
                    if part in (0, 4):
                        pe.wait_ge(gate_dve, q * OPS + (4 if part == 0 else 8))
                    for f in range(FH):
                        mm = pe.matmul(s.bank[part][:, 0:CUTS[cut]], w_in_side[:, f, part * P:(part + 1) * P], aggT[:, f, cut_columns(c, cut)],
                                       start=(f == 0), stop=(f == FH - 1))
                    mm.then_inc(gi_done, 1)

            def layer(l):
                gather(l)
                wait_own(pe, s, added, l * ET + ET + PSR)
                wait_own(pe, s, gh_copied, (l + 1) * (2 * EIT) + 2)
                wait_own(pe, s, side_left, l * 4 + 6)
                inputs(l, 0, 0)
                inputs(l, 0, 1)
                with pe.Fori(0, NG - 1) as c:
                    inputs(l, c + 1, 0)
                    group_tiles(l * NG + c)
                    inputs(l, c + 1, 1)
                group_tiles(l * NG + (NG - 1))

            pe.wait_ge(w_in, 16 * 4)
            pe.wait_ge(added, PSR)
            with pe.Fori(0, LAYERS) as l:
                layer(l)


def phase_router(nc, s, xT, gate, weights):
    EX, EP = 6, 8
    with ExitStack() as ctx:
        def sb(name, shape, dt=F32):
            return ctx.enter_context(nc.sbuf_tensor(name, shape, dt))
        w1, b1, w2, b2, w_in = weights
        rh = sb("rh", [P, GT * TP])
        logits, probs, top, top_i, top_f = sb("logits", [TP, NT, EP]), sb("probs", [TP, NT, EP]), sb("top", [TP, NT, EP]), sb("top_i", [TP, NT, EP], U32), sb("top_f", [TP, NT, EP])
        one = [sb(f"r_one{n}", [TP, NT]) for n in range(4)]
        pick = sb("r_pick", [TP, NT, EP])
        hid, relu, lg, taken, v, e_done = (s.sem("r_" + n) for n in ("hid", "relu", "lg", "taken", "v", "exp"))
        block = ctx.enter_context(nc.Block())
        CH = GT * TP
        cuts = ((0, 313), (313, CH - 313))

        @block.tensor
        def _(pe):
            pe.wait_ge(w_in, 64)
            with pe.Fori(0, NT // GT) as c:
                for h, (at, n) in enumerate(cuts):
                    for f in range(FH):
                        mm = pe.matmul(s.bank[h][:, 0:n], w1[:, f, :], xT[:, f, bass.ds(c * CH + at, n)], start=(f == 0), stop=(f == FH - 1))
                    mm.then_inc(hid, 1)
                for k in range(GT):
                    if k == 0:
                        pe.wait_ge(taken, c * GT + 1)
                        pe.wait_ge(relu, c * 2 + 2)
                    pe.matmul(s.bank[2 + k][0:TP, 0:EX], rh[:, k * TP:(k + 1) * TP], w2[:, :], start=True, stop=True).then_inc(lg, 1)

        @block.scalar
        def _(act):
            act.wait_ge(w_in, 64)
            with act.Fori(0, NT // GT) as c:
                act.wait_ge(taken, c * GT + 1)
                for h, (at, n) in enumerate(cuts):
                    act.wait_ge(hid, c * 2 + h + 1)
                    act.activation(rh[:, at:at + n], s.bank[h][:, 0:n], ACT.Relu, bias=b1[:, :]).then_inc(relu, 1)
            act.wait_ge(v, 5)
            act.activation(logits[:, :, 0:EX], logits[:, :, 0:EX], ACT.Exp).then_inc(e_done, 1)
            act.wait_ge(v, 9 + 2 * NT + 1)
            act.activation(one[1][:, :], one[1][:, :], ACT.Exp).then_inc(e_done, 1)

        @block.vector
        def _(dve):
            n = [0]

            def step(ins, alone=True):
                n[0] += 1
                ins.then_inc(v, 1)
                if alone:
                    dve.wait_ge(v, n[0])

            def side(ins):
                step(ins, alone=False)

            def joined():
                dve.wait_ge(v, n[0])
            step(dve.memset(logits[:, :, :], 0.0))
            step(dve.memset(probs[:, :, :], -1.0))
            dve.sem_inc(taken, 1)
            dve.wait_ge(taken, 1)
            dve.wait_ge(w_in, 64)
            with dve.Fori(0, NT // GT) as c:
                for k in range(GT):
                    dve.wait_ge(lg, c * GT + k + 1)
                    dve.tensor_tensor(logits[:, bass.ds(c * GT + k, 1), 0:EX].rearrange("p t e -> p (t e)"), s.bank[2 + k][0:TP, 0:EX], b2[:, :], ALU.add).then_inc(taken, 1)
            dve.wait_ge(taken, NT + 1)
            L = logits[:, :, 0:EX]

            def wide(v2):
                return v2[:, :].rearrange("p (t o) -> p t o", o=1).broadcast_to([TP, NT, EX])
            step(dve.tensor_reduce(one[0][:, :], L, AX.X, ALU.max))
            step(dve.tensor_copy(pick[:, :, 0:EX], wide(one[0])))
            step(dve.tensor_tensor(L, L, pick[:, :, 0:EX], ALU.subtract))
            dve.wait_ge(e_done, 1)
            step(dve.tensor_reduce(one[0][:, :], L, AX.X, ALU.add))
            step(dve.reciprocal(one[2][:, :], one[0][:, :]))
            step(dve.tensor_copy(pick[:, :, 0:EX], wide(one[2])))
            step(dve.tensor_tensor(probs[:, :, 0:EX], L, pick[:, :, 0:EX], ALU.mult))
            for t in range(NT):
                side(dve.max(top[:, t, :], probs[:, t, :]))
            joined()
            for t in range(NT):
                side(dve.max_index(top_i[:, t, :], top[:, t, :], probs[:, t, :]))
            joined()
            step(dve.tensor_tensor(one[1][:, :], top[:, :, 1], top[:, :, 0], ALU.subtract))
            step(dve.tensor_copy(top_f[:, :, :], top_i[:, :, :]))
            dve.wait_ge(e_done, 2)
            step(dve.tensor_scalar(one[0][:, :], one[1][:, :], 1.0, None, ALU.add))
            step(dve.reciprocal(one[2][:, :], one[0][:, :]))
            step(dve.tensor_tensor(one[3][:, :], one[1][:, :], one[2][:, :], ALU.mult))
            for t in range(NT):
                side(dve.tensor_scalar(gate[:, t, :], s.iota_row[0:TP, 0:EP], top_f[:, t, 0:1], one[2][:, t:t + 1], ALU.is_equal, ALU.mult))
                side(dve.tensor_scalar(pick[:, t, :], s.iota_row[0:TP, 0:EP], top_f[:, t, 1:2], one[3][:, t:t + 1], ALU.is_equal, ALU.mult))
            joined()
            step(dve.tensor_tensor(gate[:, :, :], gate[:, :, :], pick[:, :, :], ALU.add))


def phase_experts(nc, s, xT, gate, weights):
    EX = 6
    CH = GT * TP
    cuts = ((0, 313), (313, CH - 313))
    with ExitStack() as ctx:
        def sb(name, shape, dt=F32):
            return ctx.enter_context(nc.sbuf_tensor(name, shape, dt))
        w, b, b3, w_in = weights
        h1, h2 = sb("eh1", [P, 2, FH, CH]), sb("eh2", [P, 2, FH, CH])
        gate_now = sb("gate_now", [TP, GT, 8])
        mm, ev, om, oa, biased, gc = (s.sem("f_" + n) for n in ("mm", "ev", "om", "oa", "biased", "gc"))
        block = ctx.enter_context(nc.Block())
        order = []
        for e in range(EX + 2):
            if e < EX:
                order += [("h", 0, e, m, q) for m in range(FH) for q in range(2)]
            if 1 <= e <= EX:
                order += [("h", 1, e - 1, m, q) for m in range(FH) for q in range(2)]
            if e >= 2:
                order += [("o", e - 2, k) for k in range(GT)]
        hidden = [g for g in order if g[0] == "h"]
        outs = [g for g in order if g[0] == "o"]
        NH, NO = len(hidden), len(outs)
        HB, OB = 4, 4

        @block.tensor
        def _(pe):
            pe.wait_ge(w_in, 16 * (3 * EX + 3))
            with pe.Fori(0, NT // GT) as c:
                nh = no = 0
                for g in order:
                    if g[0] == "h":
                        _, layer, e, m, q = g
                        at, n = cuts[q]
                        pe.wait_ge(ev, c * NH + nh + 1)
                        if layer == 1:
                            pe.wait_ge(ev, c * NH + hidden.index(("h", 0, e, FH - 1, 1)) + 1 + HB)
                        for f in range(FH):
                            rhs = xT[:, f, bass.ds(c * CH + at, n)] if layer == 0 else h1[:, e % 2, f, at:at + n]
                            i = pe.matmul(s.bank[nh % HB][:, 0:n], w[layer][:, e, f, m * P:(m + 1) * P], rhs, start=(f == 0), stop=(f == FH - 1))
                        i.then_inc(mm, 1)
                        nh += 1
                        continue
                    bank = s.bank[HB + no % OB][0:TP, 0:D]
                    pe.wait_ge(oa, c * NO + max(no + 1, OB))
                    _, e, k = g
                    if k == 0:
                        pe.wait_ge(ev, c * NH + hidden.index(("h", 1, e, FH - 1, 1)) + 1 + HB)
                    for f in range(FH):
                        i = pe.matmul(bank, h2[:, e % 2, f, k * TP:(k + 1) * TP], w[2][:, e, f, :], start=(f == 0), stop=(f == FH - 1))
                    i.then_inc(om, 1)
                    no += 1

        @block.scalar
        def _(act):
            act.wait_ge(w_in, 16 * (3 * EX + 3))
            act.sem_inc(ev, HB)
            with act.Fori(0, NT // GT) as c:
                for n, (_, layer, e, m, q) in enumerate(hidden):
                    at, size = cuts[q]
                    act.wait_ge(mm, c * NH + n + 1)
                    to = (h1 if layer == 0 else h2)[:, e % 2, m, at:at + size]
                    act.activation(to, s.bank[n % HB][:, 0:size], ACT.Relu, bias=b[layer][:, e * FH + m:e * FH + m + 1]).then_inc(ev, 1)

        @block.vector
        def _(dve):
            dve.sem_inc(oa, OB)
            dve.wait_ge(w_in, 16 * (3 * EX + 3))
            with dve.Fori(0, NT // GT) as c:
                wait_own(dve, s, oa, c * NO + OB)
                dve.tensor_copy(gate_now[:, :, :], gate[:, bass.ds(c * GT, GT), :]).then_inc(gc, 1)
                wait_own(dve, s, gc, c + 1)
                for no, (_, e, k) in enumerate(outs):
                    to = s.x[:, bass.ds(c * GT + k, 1), :].rearrange("p t n -> p (t n)")
                    if no >= GT:
                        dve.wait_ge(oa, c * NO + (no - GT + 1 + OB))
                    dve.scalar_tensor_tensor(out=to, in0=b3[:, e, :], scalar=gate_now[:, k, e:e + 1], in1=to, op0=ALU.mult, op1=ALU.add).then_inc(biased, 1)
                    dve.wait_ge(om, c * NO + no + 1)
                    dve.wait_ge(biased, c * NO + no + 1)
                    dve.scalar_tensor_tensor(out=to, in0=s.bank[HB + no % OB][0:TP, 0:D], scalar=gate_now[:, k, e:e + 1], in1=to,
                                             op0=ALU.mult, op1=ALU.add).then_inc(oa, 1)


def phase_ffn0(nc, s, a):
    with ExitStack() as ctx:
        xT = ctx.enter_context(nc.sbuf_tensor("xT0", [P, FH, NPAD], F32))
        gate = ctx.enter_context(nc.sbuf_tensor("gate", [TP, NT, 8], F32))

        def sb(name, shape):
            return ctx.enter_context(nc.sbuf_tensor(name, shape, F32))
        EX = 6
        rw1, rb1, rw2, rb2 = sb("rw1", [P, FH, P]), sb("rb1", [P, 1]), sb("rw2", [P, EX]), sb("rb2", [TP, EX])
        w = [sb(f"ew{n}", [P, EX, FH, D]) for n in (1, 2, 3)]
        b = [sb(f"eb{n}", [P, EX * FH]) for n in (1, 2)]
        b3 = sb("eb3", [TP, EX, D])
        r_in, w_in = s.sem("r_w_in"), s.sem("f_w_in")

        def load(sp):
            sp.dma_start(rw1[:, :, :], a["L0_ffn_router_w1"].rearrange("(f p) n -> p f n", p=P)).then_inc(r_in, 16)
            sp.dma_start(rb1[:, :], a["router_b1_cols"]).then_inc(r_in, 16)
            sp.dma_start(rw2[:, :], a["L0_ffn_router_w2"]).then_inc(r_in, 16)
            sp.dma_start(rb2[:, :], a["L0_ffn_router_b2"].rearrange("(o e) -> o e", o=1).broadcast_to([TP, EX])).then_inc(r_in, 16)
            for n in (1, 2, 3):
                for e in range(EX):
                    sp.dma_start(w[n - 1][:, e], a[f"L0_ffn_expert_w{n}"][e].rearrange("(f p) n -> p f n", p=P)).then_inc(w_in, 16)
            for n in (1, 2):
                sp.dma_start(b[n - 1][:, :], a[f"expert_b{n}_cols"]).then_inc(w_in, 16)
            sp.dma_start(b3[:, :, :], a["L0_ffn_expert_b3"].rearrange("(o e) n -> o e n", o=1).broadcast_to([TP, EX, D])).then_inc(w_in, 16)

        phase_norm_to_T(nc, s, xT, "n1", load)
        phase_router(nc, s, xT, gate, (rw1, rb1, rw2, rb2, r_in))
        phase_experts(nc, s, xT, gate, (w, b, b3, w_in))


def phase_tables(nc, s, a, q_dram, k_dram, vT, rel_v):
    W3 = 3 * D
    with ExitStack() as ctx:
        def sb(name, shape, dt=F32):
            return ctx.enter_context(nc.sbuf_tensor(name, shape, dt))
        xT = sb("xT1", [P, FH, N + TP])
        w = sb("wqkv", [P, FH, TYPES, W3])
        rel_k = sb("rel_k", [P, FH, RELS, P])
        pri = sb("pri", [P, FH * RELS])
        x_tile = sb("x_tile", [P, 2, FH, TP])
        qkv = sb("qkv", [TP, 2, W3])
        kT = sb("kT", [P, 2, FH, TP])
        tab = sb("tab", [TP, 2, RELS, D])
        names = ("w_in", "z", "scaled", "staged", "mm", "summed", "turned", "kv", "tm", "te")
        w_in, z, scaled, staged, mm, summed, turned, kv, tm, te = (s.sem("t_" + n) for n in names)
        q_stored = [s.sem(f"t_q_stored{n}") for n in range(2)]
        t_stored = [s.sem(f"t_t_stored{n}") for n in range(2)]
        NW = 3 * TYPES + 3 * HEADS + 1
        PAIRS = NT // 2
        k_rows = k_dram.rearrange("(r n) f -> n r f", r=RELS)

        with nc.Block() as block:

            @block.vector
            def _(dve):
                dve.memset(rel_k[:, :, :, :], 0.0).then_inc(z, 1)
                dve.memset(rel_v[:, :, :, :], 0.0).then_inc(z, 1)
                dve.memset(vT[:, :, N:], 0.0).then_inc(z, 1)
                dve.memset(tab[0:NR - N, 0], 0.0).then_inc(z, 1)

            @block.sync
            def _(sp):
                for n, name in enumerate(("q", "k", "v")):
                    for t in range(TYPES):
                        sp.dma_start(w[:, :, t, n * D:(n + 1) * D], a[f"L1_gnn_{name}_linears"][t].rearrange("(f p) n -> p f n", p=P)).then_inc(w_in, 16)
                sp.wait_ge(z, 4)
                sp.dma_start(k_rows[N:NR], tab[0:NR - N, 0]).then_inc(w_in, 16)
                for h in range(HEADS):
                    at = DK * (h % 2)
                    sp.dma_start(rel_k[at:at + DK, h // 2, :, at:at + DK], a["rel_attT"][:, h].rearrange("r e d -> e r d")).then_inc(w_in, 16)
                    sp.dma_start(rel_v[at:at + DK, h // 2, :, at:at + DK], a["L1_gnn_relation_msg"][:, h].rearrange("r d e -> d r e")).then_inc(w_in, 16)
                    sp.dma_start(pri[at:at + DK, (h // 2) * RELS:(h // 2 + 1) * RELS], a["priT"][h:h + 1, :].broadcast_to([DK, RELS])).then_inc(w_in, 16)

        phase_norm_to_T(nc, s, xT, "n2")
        block = ctx.enter_context(nc.Block())

        @block.sync
        def _(sp):
            def store(t, k):
                rows = bass.ds(t * TP, TP)
                sp.wait_ge(summed, t * 8 + 12)
                sp.dma_start(q_dram[rows, :], qkv[:, k, 0:D]).then_inc(q_stored[k], 16)
                sp.wait_ge(te, t * 4 + 5)
                sp.dma_start(k_rows[rows], tab[:, k]).then_inc(t_stored[k], 16)

            with sp.Fori(0, PAIRS) as j:
                store(j * 2, 0)
                store(j * 2 + 1, 1)
            store(NT - 1, 0)
            sp.wait_ge(q_stored[0], 16 * (PAIRS + 1))
            sp.wait_ge(q_stored[1], 16 * PAIRS)
            sp.wait_ge(t_stored[0], 16 * (PAIRS + 1))
            sp.wait_ge(t_stored[1], 16 * PAIRS)

        @block.scalar
        def _(act):
            def evacuate(t, k, j):
                act.wait_ge(turned, t + 1)
                act.copy(kT[:, k], s.bank[4][:, 0:FH * TP].rearrange("p (f n) -> p f n", f=FH)).then_inc(kv, 1)
                act.copy(vT[:, :, bass.ds(t * TP, TP)], s.bank[4][:, FH * TP:2 * FH * TP].rearrange("p (f n) -> p f n", f=FH)).then_inc(kv, 1)
                if j is not None:
                    wait_own(act, s, t_stored[k], j * 16)
                for n in range(4):
                    f, quad = n // 2, n % 2
                    act.wait_ge(tm, t * 4 + n + 1)
                    act.copy(tab[:, k, 4 * quad:4 * quad + 4, f * P:(f + 1) * P],
                             s.bank[5 + n % 3][0:TP, :].rearrange("p (r d) -> p r d", r=4)).then_inc(te, 1)

            act.wait_ge(scaled, 2)
            act.sem_inc(te, 1)
            for k in range(2):
                act.copy(x_tile[:, k], xT[:, :, k * TP:(k + 1) * TP]).then_inc(staged, 1)
            def round_of(j, first):
                for k in range(2):
                    evacuate(j * 2 + k, k, None if first else j)
                    act.wait_ge(mm, j * 8 + (4 * k + 4))
                    act.copy(x_tile[:, k], xT[:, :, bass.ds(j * (2 * TP) + (2 + k) * TP, TP)]).then_inc(staged, 1)

            round_of(0, True)
            with act.Fori(1, PAIRS) as j:
                round_of(j, False)
            evacuate(NT - 1, 0, PAIRS)

        @block.vector
        def _(dve):
            dve.sem_inc(summed, 4)
            dve.wait_ge(w_in, 16 * NW)
            att = rel_k[:, :, :, :].rearrange("p f r d -> p (f r) d")
            dve.scalar_tensor_tensor(out=att, in0=att, scalar=1.0 / DK ** 0.5,
                                     in1=pri[:, :].rearrange("p (r o) -> p r o", o=1).broadcast_to([P, FH * RELS, P]),
                                     op0=ALU.mult, op1=ALU.mult).then_inc(scaled, 2)

            def accumulate(t, k, j):
                if j is not None:
                    wait_own(dve, s, q_stored[k], j * 16)
                for y in range(TYPES):
                    dve.wait_ge(mm, t * 4 + y + 1)
                    one = s.is_type[:, bass.ds(t, 1), y]
                    for part, (lo, hi) in enumerate(((0, 512), (512, W3))):
                        bank, to = s.bank[2 * (y % 2) + part][0:TP, 0:hi - lo], qkv[:, k, lo:hi]
                        if y == 0:
                            dve.tensor_scalar(to, bank, one, None, ALU.mult).then_inc(summed, 1)
                        else:
                            dve.wait_ge(summed, t * 8 + 2 * y + part - 1 + 4)
                            dve.scalar_tensor_tensor(out=to, in0=bank, scalar=one, in1=to, op0=ALU.mult, op1=ALU.add).then_inc(summed, 1)

            accumulate(0, 0, None)
            accumulate(1, 1, None)
            with dve.Fori(1, PAIRS) as j:
                accumulate(j * 2, 0, j)
                accumulate(j * 2 + 1, 1, j)
            accumulate(NT - 1, 0, PAIRS)

        @block.tensor
        def _(pe):
            def typed(t, k):
                pe.wait_ge(staged, t + 1)
                for y in range(TYPES):
                    pe.wait_ge(summed, t * 8 + 2 * y + 2)
                    for part, (lo, hi) in enumerate(((0, 512), (512, W3))):
                        for f in range(FH):
                            i = pe.matmul(s.bank[2 * (y % 2) + part][0:TP, 0:hi - lo], x_tile[:, k, f, :], w[:, f, y, lo:hi], start=(f == 0), stop=(f == FH - 1))
                    i.then_inc(mm, 1)

            def turn(t, k):
                pe.wait_ge(summed, t * 8 + 12)
                pe.wait_ge(kv, t * 2 + 2)
                for n in range(4):
                    i = pe.transpose(s.bank[4][:, n * TP:(n + 1) * TP], qkv[:, k, D + n * P:D + (n + 1) * P], s.ident[0:TP, 0:TP])
                i.then_inc(turned, 1)

            def tables(t, k):
                pe.wait_ge(kv, t * 2 + 4)
                for n in range(4):
                    f, quad = n // 2, n % 2
                    pe.wait_ge(te, t * 4 + (1 if n < 3 else n - 3 + 2))
                    pe.matmul(s.bank[5 + n % 3][0:TP, :], kT[:, k, f, :], rel_k[:, f, 4 * quad:4 * quad + 4, :].rearrange("p r d -> p (r d)"),
                              start=True, stop=True).then_inc(tm, 1)

            pe.wait_ge(w_in, 16 * NW)
            pe.wait_ge(scaled, 2)
            typed(0, 0)
            turn(0, 0)
            with pe.Fori(0, PAIRS) as j:
                typed(j * 2 + 1, 1)
                tables(j * 2, 0)
                turn(j * 2 + 1, 1)
                typed(j * 2 + 2, 0)
                tables(j * 2 + 1, 1)
                turn(j * 2 + 2, 0)
            tables(NT - 1, 0)

        @block.gpsimd
        def _(pool):
            pool.sem_inc(kv, 2)


def phase_scores(nc, s, q_dram, k_dram, v_dram, vT, rel_v, score):
    QR = 8
    V_MM, V_OUT = (1, 3, 5, 7), (2, 4, 6, 8)
    with ExitStack() as ctx:
        def sb(name, shape, dt=F32):
            return ctx.enter_context(nc.sbuf_tensor(name, shape, dt))
        rows = sb("c_rows", [P, RING, D])
        idx = sb("c_idx", [P, RING], I32)
        q_win = sb("q_win", [P, QR, D])
        sel, selT = sb("c_sel", [P, PSR, P]), sb("c_selT", [P, PSR, P])
        prod = sb("c_prod", [P, 2, D])
        v_tile = sb("v_tile", [P, FH, GHC])
        tab = sb("v_tab", [GHC, RELS, D])
        v_rows = v_dram.rearrange("(r n) f -> n r f", r=RELS)
        v_staged, v_mm, v_left, v_stored = (s.sem("c_" + n) for n in ("v_staged", "v_mm", "v_left", "v_stored"))
        names = ("idx_ready", "sel_ready", "turned", "selT_ready", "q_done", "prod_done", "red_done", "up")
        idx_ready, sel_ready, turned, selT_ready, q_done, prod_done, red_done, up = (s.sem("c_" + n) for n in names)
        row_in = [s.sem(f"c_row_in{k}") for k in range(RING)]
        q_in = [s.sem(f"c_q_in{k}") for k in range(QR)]
        block = ctx.enter_context(nc.Block())

        @block.gpsimd
        def _(pool):
            pool.wait_ge(up, 4)
            with pool.Fori(0, EIT) as j:
                for k in range(RING):
                    if k % HR == 0:
                        wait_own(pool, s, idx_ready, j * 2 + (k // HR + 1))
                    pool.indirect_dma_start(out=rows[:, k, :], out_offset=None, in_=k_dram,
                                            in_offset=bass.IndirectOffsetOnAxis(ap=idx[:, k:k + 1], axis=0)).then_inc(row_in[k], 16)

        @block.sync
        def _(sp):
            sp.wait_ge(up, 4)
            with sp.Fori(0, EIT) as j:
                for k in range(RING):
                    if k % BL == 0:
                        base = load_bases(nc, SP, s, j * RING + k, BL)
                    sp.wait_ge(q_done, j * RING + (k + 1))
                    sp.dma_start(q_win[:, k % QR, :], q_dram[bass.ds(base[k % BL], P), :]).then_inc(q_in[k % QR], 16)

        @block.scalar
        def _(act):
            def stage(j, half):
                wait_own(act, s, prod_done, j * RING + (half + 1) * HR)
                act.copy(idx[:, half * HR:(half + 1) * HR], s.rel_idx[:, bass.ds(j * RING + half * HR, HR)]).then_inc(idx_ready, 1)

            def evacuate(i, k):
                act.wait_ge(q_done, i + (QR - PSR + 1) + 0)
                act.wait_ge(turned, i + 1)
                act.copy(selT[:, k % PSR, :], s.bank[k % 2][:, 0:P]).then_inc(selT_ready, 1)

            def stage_v(j):
                wait_own(act, s, v_mm, j * 4 + 4)
                act.copy(v_tile[:, :, :], vT[:, :, bass.ds(j * GHC, GHC)]).then_inc(v_staged, 1)

            def evacuate_v(j, n):
                f, quad = n // 2, n % 2
                act.wait_ge(v_mm, j * 4 + (n + 5))
                act.copy(tab[:, 4 * quad:4 * quad + 4, f * P:(f + 1) * P],
                         s.bank[6 + n % 2][0:GHC, :].rearrange("p (r d) -> p r d", r=4)).then_inc(v_left, 1)

            act.wait_ge(up, 4)
            act.sem_inc(v_mm, 4)
            act.sem_inc(v_left, 2)
            act.copy(idx[:, 0:HR], s.rel_idx[:, 0:HR]).then_inc(idx_ready, 1)
            act.wait_ge(turned, 1)
            act.copy(selT[:, 0, :], s.bank[0][:, 0:P]).then_inc(selT_ready, 1)
            with act.Fori(0, EIT) as j:
                for k in range(RING):
                    if k == 2:
                        stage(j, 1)
                    if k == HR + 2:
                        stage(j + 1, 0)
                    evacuate(j * RING + (k + 1), k + 1)
                    if k == 0:
                        stage_v(j)
                    if k in V_OUT:
                        evacuate_v(j, V_OUT.index(k))
                    if k == V_OUT[-1]:
                        act.wait_ge(v_left, j * 4 + 6)
                        act.dma_start(v_rows[bass.ds(j * GHC, GHC)], tab[:, :, :]).then_inc(v_stored, 16)
                    if k == RING - 1:
                        wait_own(act, s, v_stored, j * 16 + 16)

        @block.vector
        def _(dve):
            def select(i, k):
                dve.tensor_scalar(sel[:, k % PSR, :], s.iota_row[:, :], s.dst_rel[:, bass.ds(i, 1)], None, ALU.is_equal).then_inc(sel_ready, 1)

            dve.sem_inc(prod_done, RING)
            dve.sem_inc(q_done, QR)
            dve.sem_inc(up, 4)
            dve.memset(score[:, :, :], 0.0).then_inc(up, 1)
            dve.wait_ge(up, 5)
            select(0, 0)
            select(1, 1)
            select(2, 2)
            with dve.Fori(0, EIT) as j:
                for k in range(RING):
                    i = j * RING + k
                    dve.wait_ge(row_in[k], (j + 1) * 16)
                    dve.wait_ge(q_done, i + (1 + QR))
                    dve.tensor_tensor(prod[:, k % 2, :], rows[:, k, :], s.bank[2 + k % PSR][:, 0:D], ALU.mult).then_inc(prod_done, 1)
                    select(i + 3, k + 3)
                    dve.wait_ge(prod_done, i + (1 + RING))
                    dve.tensor_reduce(score[:, :, bass.ds(i, 1)].rearrange("p h o -> p (h o)"), prod[:, k % 2, :].rearrange("p (h d) -> p h d", h=HEADS), AX.X, ALU.add).then_inc(red_done, 1)

        @block.tensor
        def _(pe):
            def turn(i, k):
                pe.wait_ge(sel_ready, i + 1)
                pe.transpose(s.bank[k % 2][:, 0:P], sel[:, k % PSR, :], s.ident[:, :]).then_inc(turned, 1)

            pe.wait_ge(up, 4)
            turn(0, 0)
            with pe.Fori(0, EIT) as j:
                for k in range(RING):
                    i = j * RING + k
                    pe.wait_ge(selT_ready, i + 1)
                    turn(i + 1, k + 1)
                    pe.wait_ge(q_in[k % QR], (j * 2 + (k // QR + 1)) * 16)
                    pe.wait_ge(prod_done, i + (1 + RING - PSR))
                    pe.matmul(s.bank[2 + k % PSR][:, 0:D], selT[:, k % PSR, :], q_win[:, k % QR, :], start=True, stop=True).then_inc(q_done, 1)
                    if k in V_MM:
                        n = V_MM.index(k)
                        if n == 0:
                            pe.wait_ge(v_staged, j + 1)
                        pe.wait_ge(v_left, j * 4 + (n + 1))
                        pe.matmul(s.bank[6 + n % 2][0:GHC, :], v_tile[:, n // 2, :], rel_v[:, n // 2, n % 2 * 4:n % 2 * 4 + 4, :].rearrange("p r d -> p (r d)"),
                                  start=True, stop=True).then_inc(v_mm, 1)


def phase_softmax(nc, s, score, alpha):
    TILE = [P, EC, HEADS, P]
    with ExitStack() as ctx:
        def sb(name, shape, dt=F32):
            return ctx.enter_context(nc.sbuf_tensor("m_" + name, shape, dt))
        sc, same_f, same_b, pen_f, pen_b, fwd, bwd, seg, ex = (sb(n, TILE) for n in ("sc", "same_f", "same_b", "pen_f", "pen_b", "fwd", "bwd", "seg", "ex"))
        same, out_first, out_last = (sb(n, [P, EC, P]) for n in ("same", "out_first", "out_last"))
        ends = sb("ends", [P, EC, 4, HEADS])
        whole = sb("whole", [P, EC, HEADS])
        tot = sb("tot", [P, EC, 2, HEADS])
        SEQ = 2 * EC * P
        val, key, t_f, t_b, t_same_f, t_same_b, t_pen_f, t_pen_b = (sb(n, [HEADS, SEQ]) for n in ("val", "key", "t_f", "t_b", "t_same_f", "t_same_b", "t_pen_f", "t_pen_b"))
        v, p, sc_in, e_done = s.sem("m_v"), s.sem("m_p"), s.sem("m_sc_in"), s.sem("m_e")
        block = ctx.enter_context(nc.Block())
        marks = {}

        def flat(t):
            return t[:, :, :, :].rearrange("p c h e -> p (c h e)")

        def seq(t, c):
            return t[:, c * 2 * P:(c + 1) * 2 * P].rearrange("h (i w) -> h w i", w=2)

        @block.vector
        def _(dve):
            n = [0]

            def step(ins, alone=True):
                n[0] += 1
                ins.then_inc(v, 1)
                if alone:
                    dve.wait_ge(v, n[0])

            def side(ins):
                step(ins, alone=False)

            def joined():
                dve.wait_ge(v, n[0])

            keys = s.dst_by_tile
            side(dve.memset(same[:, :, 0:1], 0.0))
            step(dve.tensor_tensor(same[:, :, 1:P], keys[:, :, 1:P], keys[:, :, 0:P - 1], ALU.is_equal))
            step(dve.memset(flat(same_b), 0.0))
            for h in range(HEADS):
                side(dve.tensor_copy(same_f[:, :, h, :], same[:, :, :]))
                side(dve.tensor_copy(same_b[:, :, h, 0:P - 1], same[:, :, 1:P]))
            joined()
            side(dve.tensor_scalar(flat(pen_f), flat(same_f), 1.0, BIG, ALU.subtract, ALU.mult))
            side(dve.tensor_scalar(flat(pen_b), flat(same_b), 1.0, BIG, ALU.subtract, ALU.mult))
            for c in range(EC):
                side(dve.tensor_scalar(out_first[:, c, :], keys[:, c, :], keys[:, c, 0:1], 1.0, ALU.is_equal, ALU.subtract))
                side(dve.tensor_scalar(out_last[:, c, :], keys[:, c, :], keys[:, c, P - 1:P], 1.0, ALU.is_equal, ALU.subtract))
                side(dve.tensor_copy(ends[:, c, 2, :], keys[:, c, 0:1].broadcast_to([P, HEADS])))
                side(dve.tensor_copy(ends[:, c, 3, :], keys[:, c, P - 1:P].broadcast_to([P, HEADS])))
            joined()
            side(dve.tensor_scalar(out_first[:, :, :], out_first[:, :, :], BIG, None, ALU.mult))
            side(dve.tensor_scalar(out_last[:, :, :], out_last[:, :, :], BIG, None, ALU.mult))
            step(dve.tensor_tensor(whole[:, :, :], ends[:, :, 2, :], ends[:, :, 3, :], ALU.not_equal))

            def across(last, scan):
                side(dve.tensor_copy(ends[:, :, 0, :], seg[:, :, :, 0]))
                step(dve.tensor_copy(ends[:, :, 1, :], seg[:, :, :, P - 1]))
                if scan == "add":
                    step(dve.tensor_tensor(ends[:, :, 1, :], ends[:, :, 1, :], whole[:, :, :], ALU.mult))
                marks["ends", scan] = n[0]
                dve.wait_ge(p, last + 1)
                for c in range(EC):
                    b = s.bank[c][0:HEADS, :].rearrange("h (w i) -> h w i", w=4)
                    side(dve.tensor_copy(seq(val, c), b[:, 0:2, :]))
                    if scan == "max":
                        side(dve.tensor_copy(seq(key, c), b[:, 2:4, :]))
                joined()
                if scan == "max":
                    side(dve.memset(t_same_f[:, 0:1], 0.0))
                    side(dve.memset(t_same_b[:, SEQ - 1:SEQ], 0.0))
                    step(dve.tensor_tensor(t_same_f[:, 1:SEQ], key[:, 1:SEQ], key[:, 0:SEQ - 1], ALU.is_equal))
                    step(dve.tensor_copy(t_same_b[:, 0:SEQ - 1], t_same_f[:, 1:SEQ]))
                    side(dve.tensor_scalar(t_pen_f[:, :], t_same_f[:, :], 1.0, BIG, ALU.subtract, ALU.mult))
                    step(dve.tensor_scalar(t_pen_b[:, :], t_same_b[:, :], 1.0, BIG, ALU.subtract, ALU.mult))
                    both(t_f[:, :], t_b[:, :], val[:, :], t_pen_f[:, :], t_pen_b[:, :], "max")
                    step(dve.tensor_tensor(val[:, :], t_f[:, :], t_b[:, :], ALU.max))
                else:
                    both(t_f[:, :], t_b[:, :], val[:, :], t_same_f[:, :], t_same_b[:, :], "add")
                    step(dve.tensor_tensor(t_f[:, :], t_f[:, :], t_b[:, :], ALU.add))
                    step(dve.tensor_tensor(val[:, :], t_f[:, :], val[:, :], ALU.subtract))
                marks["tot", scan] = n[0]
                dve.wait_ge(p, last + 2)
                step(dve.tensor_copy(tot[:, :, :, :].rearrange("p c w h -> p (c w h)"), s.bank[4][:, 0:EC * 2 * HEADS]))
                for w, outside in enumerate((out_first, out_last)):
                    for c in range(EC):
                        for h in range(HEADS):
                            side(dve.scalar_tensor_tensor(out=seg[:, c, h, :], in0=outside[:, c, :], scalar=tot[:, c, w, h:h + 1], in1=seg[:, c, h, :],
                                                          op0=ALU.add, op1=ALU.max))
                    joined()

            def both(f, b, x, m_f, m_b, scan):
                op0, op1 = (ALU.add, ALU.max) if scan == "max" else (ALU.mult, ALU.add)
                init = -BIG if scan == "max" else 0.0
                side(dve.tensor_tensor_scan(f, m_f, x, init, op0, op1))
                step(dve.tensor_tensor_scan(b[:, ::-1], m_b[:, ::-1], x[:, ::-1], init, op0, op1))

            dve.wait_ge(sc_in, HEADS)
            both(flat(fwd), flat(bwd), flat(sc), flat(pen_f), flat(pen_b), "max")
            step(dve.tensor_tensor(flat(seg), flat(fwd), flat(bwd), ALU.max))
            across(1, "max")
            step(dve.tensor_tensor(flat(sc), flat(sc), flat(seg), ALU.subtract))
            marks["shifted"] = n[0]
            dve.wait_ge(e_done, 1)
            both(flat(fwd), flat(bwd), flat(ex), flat(same_f), flat(same_b), "add")
            step(dve.tensor_tensor(flat(seg), flat(fwd), flat(bwd), ALU.add))
            step(dve.tensor_tensor(flat(seg), flat(seg), flat(ex), ALU.subtract))
            across(3, "add")
            step(dve.reciprocal(flat(fwd), flat(seg)))
            step(dve.tensor_tensor(flat(ex), flat(ex), flat(fwd), ALU.mult))
            marks["alpha"] = n[0]
            dve.wait_ge(p, 6)
            for h in range(1, HEADS, 2):
                side(dve.tensor_copy(alpha[:, h, :], s.bank[h][:, :]))

        @block.scalar
        def _(act):
            act.wait_ge(p, 1)
            for h in range(HEADS):
                act.copy(sc[:, :, h, :], s.bank[h][:, :].rearrange("p (c e) -> p c e", c=EC)).then_inc(sc_in, 1)
            act.wait_ge(v, marks["shifted"])
            act.activation(flat(ex), flat(sc), ACT.Exp).then_inc(e_done, 1)
            act.wait_ge(p, 6)
            for h in range(0, HEADS, 2):
                act.copy(alpha[:, h, :], s.bank[h][:, :]).then_inc(e_done, 1)

        @block.tensor
        def _(pe):
            for h in range(HEADS):
                for c in range(EC):
                    i = pe.transpose(s.bank[h][:, c * P:(c + 1) * P], score[:, h, c * P:(c + 1) * P], s.ident[:, :])
            i.then_inc(p, 1)
            for scan in ("max", "add"):
                pe.wait_ge(v, marks["ends", scan])
                for c in range(EC):
                    for w in range(4):
                        i = pe.transpose(s.bank[c][0:HEADS, w * P:(w + 1) * P], ends[:, c, w, :], s.ident[:, :])
                i.then_inc(p, 1)
                pe.wait_ge(v, marks["tot", scan])
                for c in range(EC):
                    for w in range(2):
                        at = (c * 2 + w) * HEADS
                        i = pe.transpose(s.bank[4][:, at:at + HEADS], seq(val, c)[:, w, :], s.ident[0:HEADS, 0:HEADS])
                i.then_inc(p, 1)
            pe.wait_ge(v, marks["alpha"])
            for h in range(HEADS):
                for c in range(EC):
                    i = pe.transpose(s.bank[h][:, c * P:(c + 1) * P], ex[:, c, h, :], s.ident[:, :])
            i.then_inc(p, 1)


def phase_messages(nc, s, a, v_dram, alpha, aggT, wa, wa_in):
    with ExitStack() as ctx:
        def sb(name, shape, dt=F32):
            return ctx.enter_context(nc.sbuf_tensor(name, shape, dt))
        rows = sb("d_rows", [P, RING, D])
        idx = sb("d_idx", [P, RING], I32)
        sel = sb("d_sel", [P, PSR, P])
        msg = sb("d_msg", [P, PSR, D])
        idx_ready, msg_ready, mm_done, added, up = (s.sem("d_" + n) for n in ("idx_ready", "msg_ready", "mm_done", "added", "up"))
        row_in = [s.sem(f"d_row_in{k}") for k in range(RING)]
        block = ctx.enter_context(nc.Block())

        @block.sync
        def _(sp):
            for t in range(TYPES):
                sp.dma_start(wa[:, :, t, :], a["L1_gnn_a_linears"][t].rearrange("(f p) n -> p f n", p=P)).then_inc(wa_in, 16)

        @block.gpsimd
        def _(pool):
            pool.wait_ge(up, 1)
            with pool.Fori(0, EIT) as j:
                for k in range(RING):
                    if k % HR == 0:
                        wait_own(pool, s, idx_ready, j * 2 + (k // HR + 1))
                    pool.indirect_dma_start(out=rows[:, k, :], out_offset=None, in_=v_dram,
                                            in_offset=bass.IndirectOffsetOnAxis(ap=idx[:, k:k + 1], axis=0)).then_inc(row_in[k], 16)

        @block.scalar
        def _(act):
            act.wait_ge(up, 1)
            with act.Fori(0, EIT) as j:
                for half in range(2):
                    wait_own(act, s, msg_ready, j * RING + (half + 1) * HR)
                    act.copy(idx[:, half * HR:(half + 1) * HR], s.rel_idx[:, bass.ds(j * RING + half * HR, HR)]).then_inc(idx_ready, 1)

        @block.vector
        def _(dve):
            def weigh(j, k):
                i = j * RING + k
                dve.tensor_scalar(sel[:, k % PSR, :], s.iota_row[:, :], s.dst_rel[:, bass.ds(i, 1)], None, ALU.is_equal).then_inc(up, 1)
                dve.wait_ge(row_in[k], (j + 1) * 16)
                dve.tensor_tensor(msg[:, k % PSR, :].rearrange("p (h d) -> p h d", h=HEADS), rows[:, k, :].rearrange("p (h d) -> p h d", h=HEADS),
                                  alpha[:, :, bass.ds(i, 1)].broadcast_to([P, HEADS, DK]), ALU.mult).then_inc(msg_ready, 1)

            def add(j, k, base):
                i = j * RING + k
                win = aggT[:, :, bass.ds(base[k], P)]
                dve.wait_ge(mm_done, i + 1)
                dve.wait_ge(added, i + PSR)
                dve.tensor_tensor(win, win, s.bank[k % PSR][:, 0:D].rearrange("p (f n) -> p f n", f=FH), ALU.add).then_inc(added, 1)

            dve.sem_inc(msg_ready, RING)
            dve.sem_inc(up, 1)
            dve.memset(aggT[:, :, :], 0.0).then_inc(added, PSR)
            dve.wait_ge(added, PSR)
            with dve.Fori(0, EIT) as j:
                base = []
                for k in range(RING):
                    if k % BL == 0:
                        base += load_bases(nc, DVE, s, j * RING + k, BL)
                    weigh(j, k)
                    if k >= 2:
                        add(j, k - 2, base)
                add(j, RING - 2, base)
                add(j, RING - 1, base)

        @block.tensor
        def _(pe):
            pe.wait_ge(up, 1)
            with pe.Fori(0, EIT) as j:
                for k in range(RING):
                    i = j * RING + k
                    pe.wait_ge(msg_ready, i + (1 + RING))
                    pe.wait_ge(added, i + 1)
                    for f in range(FH):
                        mm = pe.matmul(s.bank[k % PSR][:, f * P:(f + 1) * P], msg[:, k % PSR, f * P:(f + 1) * P], sel[:, k % PSR, :], start=True, stop=True)
                    mm.then_inc(mm_done, 1)


def phase_project(nc, s, aggT, w, w_in):
    with ExitStack() as ctx:
        tile = ctx.enter_context(nc.sbuf_tensor("a_tile", [P, GT, FH, TP], F32))
        staged, mm, added = (s.sem("a_" + n) for n in ("staged", "mm", "added"))
        block = ctx.enter_context(nc.Block())

        @block.scalar
        def _(act):
            act.sem_inc(mm, 2 * GT)
            with act.Fori(0, NT // GT) as c:
                for k in range(GT):
                    act.wait_ge(mm, (c * GT + k) * 2 + 2)
                    act.copy(tile[:, k], aggT[:, :, bass.ds((c * GT + k) * TP, TP)]).then_inc(staged, 1)

        @block.tensor
        def _(pe):
            pe.wait_ge(w_in, 16 * TYPES)
            with pe.Fori(0, NT // GT) as c:
                for k in range(GT):
                    pe.wait_ge(staged, c * GT + k + 1)
                    for half in range(2):
                        n = k * 2 + half
                        pe.wait_ge(added, ((c * GT + k) * 2 + half) * 2 + 2)
                        for f in range(FH):
                            i = pe.matmul(s.bank[n % 5][0:TP, :], tile[:, k, f, :], w[:, f, 2 * half:2 * half + 2, :].rearrange("p t n -> p (t n)"), start=(f == 0), stop=(f == FH - 1))
                        i.then_inc(mm, 1)

        @block.vector
        def _(dve):
            dve.sem_inc(added, 10)
            with dve.Fori(0, NT // GT) as c:
                for k in range(GT):
                    to = s.x[:, bass.ds(c * GT + k, 1), :].rearrange("p t n -> p (t n)")
                    for y in range(TYPES):
                        n = k * 2 + y // 2
                        dve.wait_ge(mm, (c * GT + k) * 2 + y // 2 + 1 + 2 * GT)
                        dve.wait_ge(added, (c * GT + k) * 4 + y + 10)
                        dve.scalar_tensor_tensor(out=to, in0=s.bank[n % 5][0:TP, (y % 2) * D:(y % 2 + 1) * D], scalar=s.skip_type[:, bass.ds(c * GT + k, 1), y], in1=to,
                                                 op0=ALU.mult, op1=ALU.add).then_inc(added, 1)


def phase_attention(nc, s, a):
    q_dram = nc.dram_tensor("q_dram", [N, D], F32, kind="Internal").ap()
    k_dram = nc.dram_tensor("k_dram", [RELS * NR, D], F32, kind="Internal").ap()
    v_dram = nc.dram_tensor("v_dram", [RELS * NR, D], F32, kind="Internal").ap()
    with ExitStack() as ctx:
        alpha = ctx.enter_context(nc.sbuf_tensor("alpha", [P, HEADS, EC * P], F32))
        with ExitStack() as v_ctx:
            vT = v_ctx.enter_context(nc.sbuf_tensor("vT", [P, FH, NR], F32))
            rel_v = v_ctx.enter_context(nc.sbuf_tensor("rel_v", [P, FH, RELS, P], F32))
            phase_tables(nc, s, a, q_dram, k_dram, vT, rel_v)
            score = v_ctx.enter_context(nc.sbuf_tensor("score", [P, HEADS, EC * P], F32))
            phase_scores(nc, s, q_dram, k_dram, v_dram, vT, rel_v, score)
            phase_softmax(nc, s, score, alpha)
        aggT = ctx.enter_context(nc.sbuf_tensor("aggT1", [P, FH, NPAD], F32))
        wa = ctx.enter_context(nc.sbuf_tensor("wa", [P, FH, TYPES, D], F32))
        wa_in = s.sem("a_w_in")
        phase_messages(nc, s, a, v_dram, alpha, aggT, wa, wa_in)
        phase_project(nc, s, aggT, wa, wa_in)


MX, MF = 8, 1024
CAP = 489
BUF = 31 * P
FAR = 100000.0
assert CAP == -(-5 * N // (4 * MX)) and BUF >= MX * CAP


def phase_switch_route(nc, s, a, buf_dram, slot_in, slot_out, keep, load_experts):
    with ExitStack() as ctx:
        def sb(name, shape, dt=F32):
            return ctx.enter_context(nc.sbuf_tensor("z_" + name, shape, dt))
        xT = sb("xT", [P, FH, NPAD])
        wg, bg = sb("wg", [P, FH, MX]), sb("bg", [TP, MX])
        x_tile = sb("x_tile", [P, GT, FH, TP])
        probs, spread, hot, count, before = (sb(n, [TP, NT, MX]) for n in ("probs", "spread", "hot", "count", "before"))
        top, top_i = sb("top", [TP, NT, 8]), sb("top_i", [TP, NT, 8], U32)
        best, pos, kept, far, red = (sb(n, [TP, NT]) for n in ("best", "pos", "kept", "far", "red"))
        upto, ones = sb("upto", [TP, TP]), sb("ones", [TP, TP])
        zero_row, zero_seq = sb("zero_row", [P, D]), sb("zero_seq", [TP, NT])
        w_in = s.sem("z_w_in")

        def load(sp):
            sp.dma_start(wg[:, :, :], a["L1_ffn_gate_w"].rearrange("(f p) n -> p f n", p=P)).then_inc(w_in, 16)
            sp.dma_start(bg[:, :], a["L1_ffn_gate_b"].rearrange("(o e) -> o e", o=1).broadcast_to([TP, MX])).then_inc(w_in, 16)
            load_experts(sp)

        phase_norm_to_T(nc, s, xT, "n3", load)
        staged, lg, taken, v, e_done, made, p, zeroed, z_up = (s.sem("z_" + n) for n in ("staged", "lg", "taken", "v", "e_done", "made", "p", "zeroed", "z_up"))
        marks = {}
        block = ctx.enter_context(nc.Block())

        @block.gpsimd
        def _(pool):
            pool.memset(ones[:, :], 1.0).then_inc(made, 1)
            pool.memset(upto[:, :], 1.0).then_inc(made, 1)
            pool.wait_ge(made, 2)
            pool.affine_select(out=upto[:, :], in_=upto[:, :], compare_op=ALU.is_ge, fill=0.0, base=0, pattern=[[1, TP]], channel_multiplier=-1).then_inc(made, 1)
            pool.memset(zero_row[:, :], 0.0).then_inc(z_up, 1)

        @block.sync
        def _(sp):
            sp.wait_ge(z_up, 1)
            sp.dma_start(buf_dram.rearrange("(p r) f -> p r f", p=P), zero_row[:, :].rearrange("p (o f) -> p o f", o=1).broadcast_to([P, BUF // P, D])).then_inc(zeroed, 16)
            sp.wait_ge(zeroed, 16)

        @block.vector
        def _(dve):
            n = [0]

            def step(ins, alone=True):
                n[0] += 1
                ins.then_inc(v, 1)
                if alone:
                    dve.wait_ge(v, n[0])

            def side(ins):
                step(ins, alone=False)

            def joined():
                dve.wait_ge(v, n[0])

            def wide(v2):
                return v2[:, :].rearrange("p (t o) -> p t o", o=1).broadcast_to([TP, NT, MX])

            dve.sem_inc(taken, GT)
            step(dve.memset(zero_seq[:, :], 0.0))
            dve.wait_ge(w_in, 32)
            with dve.Fori(0, NT // GT) as c:
                for k in range(GT):
                    dve.wait_ge(lg, c * GT + (k + 1 + GT))
                    dve.tensor_tensor(probs[:, bass.ds(c * GT + k, 1), :].rearrange("p t e -> p (t e)"), s.bank[k][0:TP, 0:MX], bg[:, :], ALU.add).then_inc(taken, 1)
            dve.wait_ge(taken, NT + GT)
            step(dve.tensor_reduce(red[:, :], probs[:, :, :], AX.X, ALU.max))
            step(dve.tensor_copy(spread[:, :, :], wide(red)))
            step(dve.tensor_tensor(probs[:, :, :], probs[:, :, :], spread[:, :, :], ALU.subtract))
            marks["shifted"] = n[0]
            dve.wait_ge(e_done, 1)
            step(dve.tensor_reduce(red[:, :], probs[:, :, :], AX.X, ALU.add))
            step(dve.reciprocal(best[:, :], red[:, :]))
            step(dve.tensor_copy(spread[:, :, :], wide(best)))
            step(dve.tensor_tensor(probs[:, :, :], probs[:, :, :], spread[:, :, :], ALU.mult))
            for t in range(NT):
                side(dve.max(top[:, t, :], probs[:, t, :]))
            joined()
            for t in range(NT):
                side(dve.max_index(top_i[:, t, :], top[:, t, :], probs[:, t, :]))
            joined()
            step(dve.tensor_copy(best[:, :], top_i[:, :, 0]))
            for t in range(NT):
                side(dve.tensor_scalar(hot[:, t, :], s.iota_row[0:TP, 0:MX], best[:, t:t + 1], None, ALU.is_equal))
            joined()
            marks["hot"] = n[0]
            dve.wait_ge(p, 1)
            step(dve.tensor_copy(count[:, :, :], s.bank[6][0:TP, 0:NT * MX].rearrange("p (t e) -> p t e", e=MX)))
            for e in range(MX):
                side(dve.tensor_tensor_scan(before[:, :, e], zero_seq[:, :], count[:, :, e], 0.0, ALU.add, ALU.add))
            joined()
            step(dve.tensor_tensor(before[:, :, :], before[:, :, :], count[:, :, :], ALU.subtract))
            step(dve.tensor_tensor(before[:, :, :], before[:, :, :], s.bank[5][0:TP, 0:NT * MX].rearrange("p (t e) -> p t e", e=MX), ALU.add))
            step(dve.tensor_tensor(before[:, :, :], before[:, :, :], hot[:, :, :], ALU.mult))
            step(dve.tensor_reduce(pos[:, :], before[:, :, :], AX.X, ALU.add))
            step(dve.tensor_scalar(kept[:, :], pos[:, :], float(CAP), None, ALU.is_le))
            step(dve.tensor_tensor(keep[:, :], kept[:, :], top[:, :, 0], ALU.mult))
            step(dve.tensor_scalar(far[:, :], kept[:, :], -FAR, FAR, ALU.mult, ALU.add))
            step(dve.tensor_scalar(red[:, :], pos[:, :], float(CAP), 1.0, ALU.min, ALU.subtract))
            step(dve.scalar_tensor_tensor(out=red[:, :], in0=best[:, :], scalar=float(CAP), in1=red[:, :], op0=ALU.mult, op1=ALU.add))
            step(dve.tensor_copy(slot_out[:, :], red[:, :]))
            step(dve.tensor_tensor(red[:, :], red[:, :], far[:, :], ALU.add))
            step(dve.tensor_copy(slot_in[:, :], red[:, :]))

        @block.scalar
        def _(act):
            act.sem_inc(lg, GT)
            with act.Fori(0, NT // GT) as c:
                for k in range(GT):
                    act.wait_ge(lg, c * GT + k + 1)
                    act.copy(x_tile[:, k], xT[:, :, bass.ds((c * GT + k) * TP, TP)]).then_inc(staged, 1)
            act.wait_ge(v, marks["shifted"])
            act.activation(probs[:, :, :], probs[:, :, :], ACT.Exp).then_inc(e_done, 1)

        @block.tensor
        def _(pe):
            pe.wait_ge(w_in, 32)
            with pe.Fori(0, NT // GT) as c:
                for k in range(GT):
                    pe.wait_ge(staged, c * GT + k + 1)
                    pe.wait_ge(taken, c * GT + k + 1)
                    for f in range(FH):
                        i = pe.matmul(s.bank[k][0:TP, 0:MX], x_tile[:, k, f, :], wg[:, f, :], start=(f == 0), stop=(f == FH - 1))
                    i.then_inc(lg, 1)
            pe.wait_ge(made, 3)
            pe.wait_ge(v, marks["hot"])
            everyone = hot[:, :, :].rearrange("p t e -> p (t e)")
            pe.matmul(s.bank[5][0:TP, 0:NT * MX], upto[:, :], everyone, start=True, stop=True)
            pe.matmul(s.bank[6][0:TP, 0:NT * MX], ones[:, :], everyone, start=True, stop=True).then_inc(p, 1)


def phase_dispatch(nc, s, buf_dram, slot_in):
    with ExitStack() as ctx:
        xn = ctx.enter_context(nc.sbuf_tensor("xn", [TP, NT, D], F32))
        normed, sent = s.sem("i_normed"), s.sem("i_sent")
        block = ctx.enter_context(nc.Block())

        @block.vector
        def _(dve):
            for t in range(NT):
                dve.tensor_scalar(xn[:, t, :], s.x[:, t, :], s.mv[:, t, 0:1], s.rstd[:, t:t + 1], ALU.subtract, ALU.mult).then_inc(normed, 1)

        @block.gpsimd
        def _(pool):
            for t in range(NT):
                pool.wait_ge(normed, t + 1)
                pool.indirect_dma_start(out=buf_dram, out_offset=bass.IndirectOffsetOnAxis(ap=slot_in[:, t:t + 1], axis=0), in_=xn[:, t, :],
                                        in_offset=None, bounds_check=MX * CAP - 1, oob_is_err=False).then_inc(sent, 16)
            pool.wait_ge(sent, 16 * NT)


def load_w1(sp, a, weights, e, k):
    w1, in1 = weights[0], weights[4]
    sp.dma_start(w1[:, k], a["L1_ffn_w1"][bass.ds(e, 1)].rearrange("o (f p) n -> p (o f) n", p=P)).then_inc(in1[k], 16)


def load_w2(sp, a, weights, e, k):
    w2, in2 = weights[1], weights[5]
    sp.dma_start(w2[:, k], a["L1_ffn_w2"][bass.ds(e, 1)].rearrange("o (j p) n -> p (o j) n", p=P)).then_inc(in2[k], 16)


def phase_switch_experts(nc, s, a, buf_dram, y_dram, weights):
    HM, RT = MF // P, -(-CAP // P)
    WHOLE = CAP // P
    REST = CAP - WHOLE * P
    with ExitStack() as ctx:
        def sb(name, shape, dt=F32):
            return ctx.enter_context(nc.sbuf_tensor("x_" + name, shape, dt))
        w1, w2, b1, b2, in1, in2, b_in = weights
        rows, rowsT = sb("rows", [P, 2, RT, D]), sb("rowsT", [P, 2, FH, CAP])
        hid, y = sb("hid", [P, 2, HM, CAP]), sb("y", [P, 2, RT, D])
        turned, te, hm, he, ym, ye = (s.sem("x_" + n) for n in ("turned", "te", "hm", "he", "ym", "ye"))
        stored = [s.sem(f"x_stored{k}") for k in range(2)]
        block = ctx.enter_context(nc.Block())
        PAIRS = MX // 2

        def size(r):
            return P if r < WHOLE else REST

        @block.sync
        def _(sp):
            def load_rows(e, k):
                sp.dma_start(rows[:, k, 0:WHOLE, :], buf_dram[bass.ds(e * CAP, WHOLE * P), :].rearrange("(r p) f -> p r f", p=P)).then_inc(in1[k], 16)
                sp.dma_start(rows[0:REST, k, WHOLE, :], buf_dram[bass.ds(e * CAP + WHOLE * P, REST), :]).then_inc(in1[k], 16)

            def store(e, k):
                sp.wait_ge(ye, e * RT + (RT + 2))
                sp.dma_start(y_dram[bass.ds(e * CAP, WHOLE * P), :].rearrange("(r p) f -> p r f", p=P), y[:, k, 0:WHOLE, :]).then_inc(stored[k], 16)
                sp.dma_start(y_dram[bass.ds(e * CAP + WHOLE * P, REST), :], y[0:REST, k, WHOLE, :]).then_inc(stored[k], 16)

            load_rows(0, 0)
            load_rows(1, 1)
            with sp.Fori(0, PAIRS - 1) as j:
                for k in range(2):
                    sp.wait_ge(hm, (j * 2 + k) * HM + HM)
                    load_w1(sp, a, weights, j * 2 + (k + 2), k)
                    load_rows(j * 2 + (k + 2), k)
                    sp.wait_ge(ym, (j * 2 + k) * RT + RT)
                    load_w2(sp, a, weights, j * 2 + (k + 2), k)
                    store(j * 2 + k, k)
            store(MX - 2, 0)
            store(MX - 1, 1)
            for k in range(2):
                sp.wait_ge(stored[k], 32 * PAIRS)

        @block.tensor
        def _(pe):
            def hidden(e, k, j):
                wait_own(pe, s, in1[k], j * 48 + 48)
                for r in range(RT):
                    pe.wait_ge(te, e * RT + r + 1)
                    for f in range(FH):
                        i = pe.transpose(s.bank[6 + r % 2][:, f * P:f * P + size(r)], rows[0:size(r), k, r, f * P:(f + 1) * P], s.ident[0:size(r), 0:size(r)])
                    i.then_inc(turned, 1)
                wait_own(pe, s, te, e * RT + (RT + 2))
                for m in range(HM):
                    pe.wait_ge(he, e * HM + m + 1)
                    for f in range(FH):
                        i = pe.matmul(s.bank[m % 4][:, 0:CAP], w1[:, k, f, m * P:(m + 1) * P], rowsT[:, k, f, :], start=(f == 0), stop=(f == FH - 1))
                    i.then_inc(hm, 1)

            def output(e, k, j):
                wait_own(pe, s, in2[k], j * 16 + 16)
                wait_own(pe, s, he, e * HM + (HM + 4))
                for r in range(RT):
                    pe.wait_ge(ye, e * RT + r + 1)
                    for m in range(HM):
                        i = pe.matmul(s.bank[4 + r % 2][0:size(r), 0:D], hid[:, k, m, r * P:r * P + size(r)], w2[:, k, m, :], start=(m == 0), stop=(m == HM - 1))
                    i.then_inc(ym, 1)

            hidden(0, 0, 0)
            with pe.Fori(0, PAIRS - 1) as j:
                hidden(j * 2 + 1, 1, j)
                output(j * 2, 0, j)
                hidden(j * 2 + 2, 0, j + 1)
                output(j * 2 + 1, 1, j)
            hidden(MX - 1, 1, PAIRS - 1)
            output(MX - 2, 0, PAIRS - 1)
            output(MX - 1, 1, PAIRS - 1)

        @block.scalar
        def _(act):
            act.sem_inc(te, 2)
            act.sem_inc(he, 4)
            act.wait_ge(b_in, 32)
            with act.Fori(0, PAIRS) as j:
                for k in range(2):
                    e = j * 2 + k
                    for r in range(RT):
                        act.wait_ge(turned, e * RT + r + 1)
                        act.copy(rowsT[:, k, :, r * P:r * P + size(r)], s.bank[6 + r % 2][:, 0:FH * P].rearrange("p (f n) -> p f n", f=FH)[:, :, 0:size(r)]).then_inc(te, 1)
                    for m in range(HM):
                        act.wait_ge(hm, e * HM + m + 1)
                        act.activation(hid[:, k, m, :], s.bank[m % 4][:, 0:CAP], ACT.Relu, bias=b1[:, bass.ds(e * HM + m, 1)]).then_inc(he, 1)

        @block.vector
        def _(dve):
            dve.sem_inc(ye, 2)
            dve.wait_ge(b_in, 32)

            def add_bias(j, first):
                for k in range(2):
                    e = j * 2 + k
                    if not first:
                        wait_own(dve, s, stored[k], j * 32)
                    for r in range(RT):
                        dve.wait_ge(ym, e * RT + r + 1)
                        dve.tensor_tensor(y[0:size(r), k, r, :], s.bank[4 + r % 2][0:size(r), 0:D], b2[0:size(r), bass.ds(e, 1), :].rearrange("p o n -> p (o n)"), ALU.add).then_inc(ye, 1)

            add_bias(0, True)
            with dve.Fori(1, PAIRS) as j:
                add_bias(j, False)


def phase_combine(nc, s, y_dram, slot_out, keep, out):
    with ExitStack() as ctx:
        def sb(name, shape):
            return ctx.enter_context(nc.sbuf_tensor("o_" + name, shape, F32))
        rows = sb("rows", [TP, NT, D])
        number, clipped, infinite = (sb(n, [TP, GT, D]) for n in ("number", "clipped", "infinite"))
        row_in = [s.sem(f"o_row_in{c}") for c in range(NT // GT)]
        v, kept, added, stored = s.sem("o_v"), s.sem("o_kept"), s.sem("o_added"), s.sem("o_stored")
        block = ctx.enter_context(nc.Block())
        out_rows = out.rearrange("(t p) f -> p t f", p=TP)
        FMAX = 3.4028234663852886e38

        @block.gpsimd
        def _(pool):
            for t in range(NT):
                pool.indirect_dma_start(out=rows[:, t, :], out_offset=None, in_=y_dram,
                                        in_offset=bass.IndirectOffsetOnAxis(ap=slot_out[:, t:t + 1], axis=0)).then_inc(row_in[t // GT], 16)

        @block.vector
        def _(dve):
            n = [0]

            def step(ins, alone=True):
                n[0] += 1
                ins.then_inc(v, 1)
                if alone:
                    dve.wait_ge(v, n[0])

            def side(ins):
                step(ins, alone=False)

            def joined():
                dve.wait_ge(v, n[0])

            for c in range(NT // GT):
                group = slice(c * GT, (c + 1) * GT)
                y = rows[:, group, :]
                dve.wait_ge(kept, (c + 1) * GT)
                if c:
                    dve.wait_ge(added, c)
                side(dve.tensor_scalar(number[:, :, :], y, 0.0, None, ALU.max))
                side(dve.tensor_scalar(clipped[:, :, :], y, -10000.0, 10000.0, ALU.max, ALU.min))
                joined()
                step(dve.scalar_tensor_tensor(out=number[:, :, :], in0=y, scalar=0.0, in1=number[:, :, :], op0=ALU.min, op1=ALU.add))
                step(dve.tensor_scalar(infinite[:, :, :], number[:, :, :], -FMAX, None, ALU.is_lt))
                step(dve.scalar_tensor_tensor(out=infinite[:, :, :], in0=number[:, :, :], scalar=FMAX, in1=infinite[:, :, :], op0=ALU.is_gt, op1=ALU.max))
                step(dve.copy_predicated(number[:, :, :], infinite[:, :, :].bitcast(I32), clipped[:, :, :]))
                dve.tensor_tensor(s.x[:, group, :], s.x[:, group, :], number[:, :, :], ALU.add).then_inc(added, 1)

        @block.scalar
        def _(act):
            for t in range(NT):
                act.wait_ge(row_in[t // GT], 16 * GT)
                act.activation(rows[:, t, :], rows[:, t, :], ACT.Copy, scale=keep[:, t:t + 1]).then_inc(kept, 1)

        @block.sync
        def _(sp):
            for c in range(NT // GT):
                sp.wait_ge(added, c + 1)
                sp.dma_start(out_rows[:, c * GT:(c + 1) * GT, :], s.x[:, c * GT:(c + 1) * GT, :]).then_inc(stored, 16)
            sp.wait_ge(stored, 16 * (NT // GT))


def phase_switch(nc, s, a, out):
    buf_dram = nc.dram_tensor("buf_dram", [BUF, D], F32, kind="Internal").ap()
    y_dram = nc.dram_tensor("y_dram", [MX * CAP, D], F32, kind="Internal").ap()
    with ExitStack() as ctx:
        slot_in = ctx.enter_context(nc.sbuf_tensor("slot_in", [TP, NT], I32))
        slot_out = ctx.enter_context(nc.sbuf_tensor("slot_out", [TP, NT], I32))
        keep = ctx.enter_context(nc.sbuf_tensor("keep", [TP, NT], F32))
        with ExitStack() as w_ctx:
            def sb(name, shape):
                return w_ctx.enter_context(nc.sbuf_tensor("x_" + name, shape, F32))
            w1, w2 = sb("w1", [P, 2, FH, MF]), sb("w2", [P, 2, MF // P, D])
            b1, b2 = sb("b1", [P, MX * (MF // P)]), sb("b2", [P, MX, D])
            in1, in2 = ([s.sem(f"x_in{n}_{k}") for k in range(2)] for n in (1, 2))
            b_in = s.sem("x_b_in")
            weights = w1, w2, b1, b2, in1, in2, b_in

            def load(sp):
                for e in range(2):
                    load_w1(sp, a, weights, e, e)
                    load_w2(sp, a, weights, e, e)
                sp.dma_start(b1[:, :], a["moe_b1_cols"]).then_inc(b_in, 16)
                sp.dma_start(b2[:, :, :], a["L1_ffn_b2"].rearrange("(o e) n -> o e n", o=1).broadcast_to([P, MX, D])).then_inc(b_in, 16)

            phase_switch_route(nc, s, a, buf_dram, slot_in, slot_out, keep, load)
            phase_dispatch(nc, s, buf_dram, slot_in)
            phase_switch_experts(nc, s, a, buf_dram, y_dram, weights)
        phase_combine(nc, s, y_dram, slot_out, keep, out)


def build(nc, a, out, stop="0123"):
    h_dram = nc.dram_tensor("h_dram", [N, D], F32, kind="Internal").ap()
    with ExitStack() as ctx:
        s = open_shared(nc, ctx, a)
        phase_edges(nc, s, a)
        if "0" in stop:
            phase_gated_gnn(nc, s, a, h_dram)
            end_stage(nc, s)
        if "1" in stop:
            phase_ffn0(nc, s, a)
            end_stage(nc, s)
        if "2" in stop:
            phase_attention(nc, s, a)
            end_stage(nc, s)
        if "3" in stop:
            phase_switch(nc, s, a, out)
            return
        stored = s.sem("stored")
        with nc.Block() as block:
            @block.sync
            def _(sp):
                sp.dma_start(out.rearrange("(t p) f -> p t f", p=TP), s.x[:, :, :]).then_inc(stored, 16)
                sp.wait_ge(stored, 16)


_INS = ["x", "src", "dst", "edge_type_8", "edge_weight", "node_type_4", "w_msgT", "w_ihT", "w_hhT", "b_ih_cols", "b_hh_cols",
        "L0_ffn_router_w1", "router_b1_cols", "L0_ffn_router_w2", "L0_ffn_router_b2", "L0_ffn_expert_w1", "expert_b1_cols", "L0_ffn_expert_w2",
        "expert_b2_cols", "L0_ffn_expert_w3", "L0_ffn_expert_b3",
        "L1_gnn_k_linears", "L1_gnn_q_linears", "L1_gnn_v_linears", "L1_gnn_a_linears", "rel_attT", "L1_gnn_relation_msg", "priT", "L1_gnn_skip",
        "L1_ffn_gate_w", "L1_ffn_gate_b", "L1_ffn_w1", "moe_b1_cols", "L1_ffn_w2", "L1_ffn_b2"]
_OUTS = [((3125, 256), "float32")]


def kernel(**inputs):
    import numpy as _np
    import concourse.bacc as _bacc
    from concourse import mybir as _mybir
    from concourse.bass_utils import run_bass_kernel_spmd as _run

    inputs["w_msgT"] = _np.asarray(inputs["L0_gnn_weight"]).transpose(0, 2, 1)
    inputs["w_ihT"] = _np.asarray(inputs["L0_gnn_w_ih"]).T
    inputs["w_hhT"] = _np.asarray(inputs["L0_gnn_w_hh"]).T
    for name in ("router_b1", "expert_b1", "expert_b2"):
        inputs[f"{name}_cols"] = _np.asarray(inputs[f"L0_ffn_{name}"]).reshape(-1, P).T
    inputs["rel_attT"] = _np.asarray(inputs["L1_gnn_relation_att"]).transpose(0, 1, 3, 2)
    inputs["priT"] = _np.asarray(inputs["L1_gnn_relation_pri"]).T
    inputs["moe_b1_cols"] = _np.asarray(inputs["L1_ffn_b1"]).reshape(-1, P).T
    for side in ("ih", "hh"):
        inputs[f"b_{side}_cols"] = _np.asarray(inputs[f"L0_gnn_b_{side}"]).reshape(-1, P).T
    nc = _bacc.Bacc("TRN2", target_bir_lowering=False, num_devices=1)
    arrays, args = {}, {}
    for name in _INS:
        v = _np.ascontiguousarray(inputs[name])
        arrays[f"in_{name}_dram"] = v
        args[name] = nc.dram_tensor(f"in_{name}_dram", v.shape, _mybir.dt.from_np(v.dtype), kind="ExternalInput").ap()
    out = nc.dram_tensor("out_0_dram", _OUTS[0][0], _mybir.dt.from_np(_np.dtype(_OUTS[0][1])), kind="ExternalOutput").ap()
    build(nc, args, out)
    r = _run(nc, [arrays], core_ids=[0])
    return r.results[0]["out_0_dram"]
```
